# Optimizing a Trainium2 kernel written in Bass

```python
import numpy as np
import jax
import jax.numpy as jnp

def _softmax(x, axis=-1):
    return jax.nn.softmax(x, axis=axis)

def _gelu(x):
    return jax.nn.gelu(x, approximate=True)

def _silu(x):
    return jax.nn.silu(x)

def _sigmoid(x):
    return jax.nn.sigmoid(x)

def _layernorm(x, axis=-1, eps=1e-05):
    m = jnp.mean(x, axis=axis, keepdims=True)
    v = jnp.var(x, axis=axis, keepdims=True)
    return (x - m) / jnp.sqrt(v + eps)

def _scatter_add(tgt, idx, src, axis=0):
    return tgt.at[idx].add(src)

def _segment_sum(src, seg, n):
    return jax.ops.segment_sum(src, seg, n)
kernel_name = 'mk_gnn_ffn_d4_gnn_r8_38f386'

def setup_inputs(seed: int=0):
    np.random.seed(seed)
    _w = jnp.asarray

    def _rec_inputs():
        import jax
        import jax.numpy as jnp
        _gk = jax.random.key(seed)
        x = -0.0003929 + 0.9999 * jax.random.normal(jax.random.fold_in(_gk, 1), (6250, 256), jnp.float32)
        src = jax.random.randint(jax.random.fold_in(_gk, 2), (100000,), 0, 6250, jnp.int32)
        dst = jax.random.randint(jax.random.fold_in(_gk, 3), (100000,), 0, 6250, jnp.int32)
        _o = jnp.argsort(dst, stable=True)
        src = src[_o]
        dst = dst[_o]
        edge_weight = 0.00540447 + 1.00226 * jax.random.normal(jax.random.fold_in(_gk, 13), (100000,), jnp.float32)
        return (x, src, dst, edge_weight)
    x, src, dst, edge_weight = _rec_inputs()

    def _L0_gnn_setup():
        import jax, jax.numpy as jnp
        import numpy as np
        from itertools import combinations
        NDIM = 256
        BATCH = 8192

        def _build_mat(rots, idx_i, idx_j, ndim):

            def step(mat, t):
                i, j, theta = t
                c = jnp.cos(theta)
                s = jnp.sin(theta)
                ri = mat[i]
                rj = mat[j]
                mat = mat.at[i].set(c * ri - s * rj)
                mat = mat.at[j].set(s * ri + c * rj)
                return (mat, None)
            mat0 = jnp.eye(ndim, dtype=rots.dtype)
            mat, _ = jax.lax.scan(step, mat0, (idx_i, idx_j, rots))
            return mat.T
        key = jax.random.key(seed)
        k1, k2 = jax.random.split(key)
        pairs = np.array(list(combinations(range(NDIM), 2)), dtype=np.int32)
        return {'x': jax.random.normal(k1, (BATCH, NDIM), dtype=jnp.float32), 'rots': jax.random.normal(k2, (pairs.shape[0],), dtype=jnp.float32), 'idx_i': jnp.asarray(pairs[:, 0]), 'idx_j': jnp.asarray(pairs[:, 1])}
    _L0_gnn_all = _L0_gnn_setup()
    _L0_gnn_in = {k: v for k, v in _L0_gnn_all.items() if k in ()}
    del _L0_gnn_all

    def _L0_ffn_setup():
        import math
        import jax, jax.numpy as jnp
        import numpy as np
        CAPACITY_FACTOR = 1.25
        key = jax.random.key(seed)
        ks = jax.random.split(key, 5)
        B, L, D, F, E = (8, 1024, 256, 1024, 8)
        h = jax.random.normal(ks[0], (B, L, D), dtype=jnp.float32)
        gate_w = jax.random.normal(ks[1], (D, E), dtype=jnp.float32) * 0.02
        gate_b = jnp.zeros((E,), dtype=jnp.float32)
        w1 = jax.random.normal(ks[2], (E, D, F), dtype=jnp.float32) * (1.0 / math.sqrt(D))
        b1 = jnp.zeros((E, F), dtype=jnp.float32)
        w2 = jax.random.normal(ks[3], (E, F, D), dtype=jnp.float32) * (1.0 / math.sqrt(F))
        b2 = jnp.zeros((E, D), dtype=jnp.float32)
        return {'h': h, 'gate_w': gate_w, 'gate_b': gate_b, 'w1': w1, 'b1': b1, 'w2': w2, 'b2': b2}
    _L0_ffn_all = _L0_ffn_setup()
    _L0_ffn_in = {k: v for k, v in _L0_ffn_all.items() if k in ('gate_w', 'gate_b', 'w1', 'b1', 'w2', 'b2')}
    del _L0_ffn_all

    def _L1_gnn_setup():
        import jax, jax.numpy as jnp
        import numpy as np
        from jax.ops import segment_max, segment_sum
        N_NODES = 6250
        N_EDGES = 100000
        IN_CH = 256
        HEADS = 8
        OUT_CH = 32
        NEG_SLOPE = 0.2
        EPS = 1e-16
        key = jax.random.key(seed)
        k1, k2, k3, k4, k5 = jax.random.split(key, 5)
        x = jax.random.normal(k1, (N_NODES, IN_CH), dtype=jnp.float32)
        edge_index = jax.random.randint(k2, (2, N_EDGES), 0, N_NODES, dtype=jnp.int64)
        W = jax.random.normal(k3, (HEADS * OUT_CH, IN_CH), dtype=jnp.float32) * (1.0 / np.sqrt(IN_CH))
        a_left = jax.random.normal(k4, (HEADS, OUT_CH), dtype=jnp.float32) * (1.0 / np.sqrt(OUT_CH))
        a_right = jax.random.normal(k5, (HEADS, OUT_CH), dtype=jnp.float32) * (1.0 / np.sqrt(OUT_CH))
        return {'x': x, 'edge_index': edge_index, 'W': W, 'a_left': a_left, 'a_right': a_right}
    _L1_gnn_all = _L1_gnn_setup()
    _L1_gnn_in = {k: v for k, v in _L1_gnn_all.items() if k in ('W', 'a_left', 'a_right')}
    del _L1_gnn_all

    def _L1_ffn_setup():
        import jax, jax.numpy as jnp
        import numpy as np
        IN_CH = 256
        OUT_CH = 256
        key = jax.random.key(seed)
        kx, kw, kb = jax.random.split(key, 3)
        x = jax.random.normal(kx, (8, 512, IN_CH), dtype=jnp.float32)
        bound = 1.0 / np.sqrt(IN_CH)
        weight = jax.random.uniform(kw, (OUT_CH, IN_CH), dtype=jnp.float32, minval=-bound, maxval=bound)
        bias = jax.random.uniform(kb, (OUT_CH,), dtype=jnp.float32, minval=-bound, maxval=bound)
        return {'x': x, 'weight': weight, 'bias': bias}
    _L1_ffn_all = _L1_ffn_setup()
    _L1_ffn_in = {k: v for k, v in _L1_ffn_all.items() if k in ('weight', 'bias')}
    del _L1_ffn_all

    def _L2_gnn_setup():
        import jax, jax.numpy as jnp
        import numpy as np
        BN_EPS = 1e-05
        key = jax.random.key(seed)
        k1, k2, k3 = jax.random.split(key, 3)
        N, F, H, E = (6250, 256, 256, 200000)
        x = jax.random.normal(k1, (N, F), dtype=jnp.float32)
        edge_index = jax.random.randint(k2, (2, E), 0, N, dtype=jnp.int64)
        lim = 1.0 / np.sqrt(F)
        W = jax.random.uniform(k3, (H, F), dtype=jnp.float32, minval=-lim, maxval=lim)
        b = jnp.zeros((H,), dtype=jnp.float32)
        bn_w = jnp.ones((H,), dtype=jnp.float32)
        bn_b = jnp.zeros((H,), dtype=jnp.float32)
        return {'x': x, 'edge_index': edge_index, 'W': W, 'b': b, 'bn_w': bn_w, 'bn_b': bn_b}
    _L2_gnn_all = _L2_gnn_setup()
    _L2_gnn_in = {k: v for k, v in _L2_gnn_all.items() if k in ('W', 'b', 'bn_w', 'bn_b')}
    del _L2_gnn_all

    def _L2_ffn_setup():
        import jax, jax.numpy as jnp
        import numpy as np
        B, T, D, H, E = (16, 512, 256, 512, 8)
        key = jax.random.key(seed)
        ks = jax.random.split(key, 5)
        x = jax.random.normal(ks[0], (B, T, D), dtype=jnp.float32)
        gate_w = jax.random.normal(ks[1], (D, E), dtype=jnp.float32) * 0.02
        gate_b = jnp.zeros((E,), dtype=jnp.float32)
        W1 = jax.random.normal(ks[2], (E, D, H), dtype=jnp.float32) * 0.02
        b1 = jnp.zeros((E, H), dtype=jnp.float32)
        W2 = jax.random.normal(ks[3], (E, H, D), dtype=jnp.float32) * 0.02
        b2 = jnp.zeros((E, D), dtype=jnp.float32)
        return {'x': x, 'gate_w': gate_w, 'gate_b': gate_b, 'W1': W1, 'b1': b1, 'W2': W2, 'b2': b2}
    _L2_ffn_all = _L2_ffn_setup()
    _L2_ffn_in = {k: v for k, v in _L2_ffn_all.items() if k in ('gate_w', 'gate_b', 'W1', 'b1', 'W2', 'b2')}
    del _L2_ffn_all

    def _L3_gnn_setup():
        import jax, jax.numpy as jnp
        import numpy as np
        N = 12500
        E = 100000
        F_IN = 256
        HID = 64
        H = 4
        NEG_SLOPE = 0.2
        BN_EPS = 1e-05

        def _add_self_loops(edge_index, n):
            loop = jnp.arange(n, dtype=edge_index.dtype)
            src = jnp.concatenate([edge_index[0], loop])
            dst = jnp.concatenate([edge_index[1], loop])
            return (src, dst)

        def _batch_norm(x, g, b):
            m = x.mean(0)
            v = x.var(0)
            return g * (x - m) * jax.lax.rsqrt(v + BN_EPS) + b

        def _gcn_conv(x, src, dst, W, b, n):
            deg = jax.ops.segment_sum(jnp.ones_like(dst, jnp.float32), dst, n)
            dinv = jax.lax.rsqrt(jnp.maximum(deg, 1.0))
            norm = dinv[src] * dinv[dst]
            h = x @ W
            out = jax.ops.segment_sum(h[src] * norm[:, None], dst, n)
            return out + b

        def _gat_conv(x, src, dst, W, a_src, a_dst, b, n):
            h = (x @ W).reshape(n, H, HID)
            alpha_s = jnp.einsum('nhc,hc->nh', h, a_src)
            alpha_d = jnp.einsum('nhc,hc->nh', h, a_dst)
            e = alpha_s[src] + alpha_d[dst]
            e = jnp.where(e > 0, e, NEG_SLOPE * e)
            emax = jax.ops.segment_max(e, dst, n)
            w = jnp.exp(e - emax[dst])
            wsum = jax.ops.segment_sum(w, dst, n)
            att = w / wsum[dst]
            out = jax.ops.segment_sum(att[:, :, None] * h[src], dst, n)
            return out.reshape(n, H * HID) + b
        key = jax.random.key(seed)
        ks = jax.random.split(key, 20)
        s = 0.05
        return {'x': jax.random.normal(ks[0], (N, F_IN), jnp.float32), 'edge_index': jax.random.randint(ks[1], (2, E), 0, N, jnp.int64), 'W_gcn': jax.random.normal(ks[2], (F_IN, HID), jnp.float32) * s, 'b_gcn': jnp.zeros((HID,), jnp.float32), 'g0': jnp.ones((HID,), jnp.float32), 'beta0': jnp.zeros((HID,), jnp.float32), 'W1': jax.random.normal(ks[3], (HID, H * HID), jnp.float32) * s, 'a_src1': jax.random.normal(ks[4], (H, HID), jnp.float32) * s, 'a_dst1': jax.random.normal(ks[5], (H, HID), jnp.float32) * s, 'b1': jnp.zeros((H * HID,), jnp.float32), 'g1': jnp.ones((H * HID,), jnp.float32), 'beta1': jnp.zeros((H * HID,), jnp.float32), 'W2': jax.random.normal(ks[6], (H * HID, H * HID), jnp.float32) * s, 'a_src2': jax.random.normal(ks[7], (H, HID), jnp.float32) * s, 'a_dst2': jax.random.normal(ks[8], (H, HID), jnp.float32) * s, 'b2': jnp.zeros((H * HID,), jnp.float32), 'g2': jnp.ones((H * HID,), jnp.float32), 'beta2': jnp.zeros((H * HID,), jnp.float32)}
    _L3_gnn_all = _L3_gnn_setup()
    _L3_gnn_in = {k: v for k, v in _L3_gnn_all.items() if k in ('W_gcn', 'b_gcn', 'g0', 'beta0', 'W1', 'a_src1', 'a_dst1', 'b1', 'g1', 'beta1', 'W2', 'a_src2', 'a_dst2', 'b2', 'g2', 'beta2')}
    del _L3_gnn_all

    def _L3_ffn_setup():
        import jax, jax.numpy as jnp
        import numpy as np
        B, S, D, E, H, K = (4, 512, 256, 8, 512, 2)
        key = jax.random.key(seed)
        ks = jax.random.split(key, 6)
        x = jax.random.normal(ks[0], (B, S, D), jnp.float32)
        Wg = jax.random.normal(ks[1], (D, E), jnp.float32) * 0.02
        bg = jnp.zeros((E,), jnp.float32)
        W1 = jax.random.normal(ks[2], (E, D, H), jnp.float32) * 0.02
        b1 = jnp.zeros((E, H), jnp.float32)
        W2 = jax.random.normal(ks[3], (E, H, D), jnp.float32) * 0.02
        b2 = jnp.zeros((E, D), jnp.float32)
        return {'x': x, 'Wg': Wg, 'bg': bg, 'W1': W1, 'b1': b1, 'W2': W2, 'b2': b2}
    _L3_ffn_all = _L3_ffn_setup()
    _L3_ffn_in = {k: v for k, v in _L3_ffn_all.items() if k in ('Wg', 'bg', 'W1', 'b1', 'W2', 'b2')}
    del _L3_ffn_all
    return {'x': x, 'src': src, 'dst': dst, 'edge_weight': edge_weight, 'L0_ffn_gate_w': _L0_ffn_in['gate_w'], 'L0_ffn_gate_b': _L0_ffn_in['gate_b'], 'L0_ffn_w1': _L0_ffn_in['w1'], 'L0_ffn_b1': _L0_ffn_in['b1'], 'L0_ffn_w2': _L0_ffn_in['w2'], 'L0_ffn_b2': _L0_ffn_in['b2'], 'L1_gnn_W': _L1_gnn_in['W'], 'L1_gnn_a_left': _L1_gnn_in['a_left'], 'L1_gnn_a_right': _L1_gnn_in['a_right'], 'L1_ffn_weight': _L1_ffn_in['weight'], 'L1_ffn_bias': _L1_ffn_in['bias'], 'L2_gnn_W': _L2_gnn_in['W'], 'L2_gnn_b': _L2_gnn_in['b'], 'L2_gnn_bn_w': _L2_gnn_in['bn_w'], 'L2_gnn_bn_b': _L2_gnn_in['bn_b'], 'L2_ffn_gate_w': _L2_ffn_in['gate_w'], 'L2_ffn_gate_b': _L2_ffn_in['gate_b'], 'L2_ffn_W1': _L2_ffn_in['W1'], 'L2_ffn_b1': _L2_ffn_in['b1'], 'L2_ffn_W2': _L2_ffn_in['W2'], 'L2_ffn_b2': _L2_ffn_in['b2'], 'L3_gnn_W_gcn': _L3_gnn_in['W_gcn'], 'L3_gnn_b_gcn': _L3_gnn_in['b_gcn'], 'L3_gnn_g0': _L3_gnn_in['g0'], 'L3_gnn_beta0': _L3_gnn_in['beta0'], 'L3_gnn_W1': _L3_gnn_in['W1'], 'L3_gnn_a_src1': _L3_gnn_in['a_src1'], 'L3_gnn_a_dst1': _L3_gnn_in['a_dst1'], 'L3_gnn_b1': _L3_gnn_in['b1'], 'L3_gnn_g1': _L3_gnn_in['g1'], 'L3_gnn_beta1': _L3_gnn_in['beta1'], 'L3_gnn_W2': _L3_gnn_in['W2'], 'L3_gnn_a_src2': _L3_gnn_in['a_src2'], 'L3_gnn_a_dst2': _L3_gnn_in['a_dst2'], 'L3_gnn_b2': _L3_gnn_in['b2'], 'L3_gnn_g2': _L3_gnn_in['g2'], 'L3_gnn_beta2': _L3_gnn_in['beta2'], 'L3_ffn_Wg': _L3_ffn_in['Wg'], 'L3_ffn_bg': _L3_ffn_in['bg'], 'L3_ffn_W1': _L3_ffn_in['W1'], 'L3_ffn_b1': _L3_ffn_in['b1'], 'L3_ffn_W2': _L3_ffn_in['W2'], 'L3_ffn_b2': _L3_ffn_in['b2']}

def reference(x, src, dst, edge_weight, L0_ffn_gate_w, L0_ffn_gate_b, L0_ffn_w1, L0_ffn_b1, L0_ffn_w2, L0_ffn_b2, L1_gnn_W, L1_gnn_a_left, L1_gnn_a_right, L1_ffn_weight, L1_ffn_bias, L2_gnn_W, L2_gnn_b, L2_gnn_bn_w, L2_gnn_bn_b, L2_ffn_gate_w, L2_ffn_gate_b, L2_ffn_W1, L2_ffn_b1, L2_ffn_W2, L2_ffn_b2, L3_gnn_W_gcn, L3_gnn_b_gcn, L3_gnn_g0, L3_gnn_beta0, L3_gnn_W1, L3_gnn_a_src1, L3_gnn_a_dst1, L3_gnn_b1, L3_gnn_g1, L3_gnn_beta1, L3_gnn_W2, L3_gnn_a_src2, L3_gnn_a_dst2, L3_gnn_b2, L3_gnn_g2, L3_gnn_beta2, L3_ffn_Wg, L3_ffn_bg, L3_ffn_W1, L3_ffn_b1, L3_ffn_W2, L3_ffn_b2):
    import jax
    import jax.numpy as jnp

    def _L0_gnn_ref(x, rots, idx_i, idx_j):
        import jax, jax.numpy as jnp
        import numpy as np
        from itertools import combinations
        NDIM = 256
        BATCH = 8192

        def _build_mat(rots, idx_i, idx_j, ndim):

            def step(mat, t):
                i, j, theta = t
                c = jnp.cos(theta)
                s = jnp.sin(theta)
                ri = mat[i]
                rj = mat[j]
                mat = mat.at[i].set(c * ri - s * rj)
                mat = mat.at[j].set(s * ri + c * rj)
                return (mat, None)
            mat0 = jnp.eye(ndim, dtype=rots.dtype)
            mat, _ = jax.lax.scan(step, mat0, (idx_i, idx_j, rots))
            return mat.T
        m = _build_mat(rots, idx_i, idx_j, x.shape[-1])
        return x @ m

    def _L0_ffn_ref(h, gate_w, gate_b, w1, b1, w2, b2):
        import math
        import jax, jax.numpy as jnp
        import numpy as np
        CAPACITY_FACTOR = 1.25
        B, L, D = h.shape
        E = gate_w.shape[1]
        T = B * L
        C = max(1, math.ceil(CAPACITY_FACTOR * T / E))
        x = h.reshape(T, D)
        logits = x @ gate_w + gate_b
        probs = jax.nn.softmax(logits, axis=-1)
        idx = jnp.argmax(probs, axis=-1)
        prb = jnp.take_along_axis(probs, idx[:, None], axis=1)[:, 0]
        one_hot = jax.nn.one_hot(idx, E, dtype=jnp.float32)
        pos = (jnp.cumsum(one_hot, axis=0) * one_hot).sum(-1).astype(jnp.int32) - 1
        kept = pos < C
        pos_safe = jnp.where(kept, pos, C)
        buf = jnp.zeros((E, C, D), dtype=h.dtype).at[idx, pos_safe].set(x, mode='drop')
        hmid = jax.nn.relu(jnp.einsum('ecd,edf->ecf', buf, w1) + b1[:, None, :])
        ybuf = jnp.einsum('ecf,efd->ecd', hmid, w2) + b2[:, None, :]
        pos_g = jnp.minimum(pos, C - 1)
        y_tok = ybuf[idx, pos_g] * (prb * kept)[:, None]
        y = y_tok.reshape(B, L, D)
        y = jnp.nan_to_num(y, nan=0.0, posinf=10000.0, neginf=-10000.0)
        return y

    def _L1_gnn_ref(x, edge_index, W, a_left, a_right):
        import jax, jax.numpy as jnp
        import numpy as np
        from jax.ops import segment_max, segment_sum
        N_NODES = 6250
        N_EDGES = 100000
        IN_CH = 256
        HEADS = 8
        OUT_CH = 32
        NEG_SLOPE = 0.2
        EPS = 1e-16
        N = x.shape[0]
        H, C = (HEADS, OUT_CH)
        loops = jnp.arange(N, dtype=edge_index.dtype)
        src = jnp.concatenate([edge_index[0], loops])
        dst = jnp.concatenate([edge_index[1], loops])
        Wh = (x @ W.T).reshape(N, H, C)
        e_left = jnp.einsum('nhc,hc->nh', Wh, a_left)
        e_right = jnp.einsum('nhc,hc->nh', Wh, a_right)
        e = e_left[src] + e_right[dst]
        e = jnp.where(e >= 0, e, NEG_SLOPE * e)
        e_max = segment_max(e, dst, num_segments=N)
        e_max = jnp.where(jnp.isfinite(e_max), e_max, 0.0)
        e_exp = jnp.exp(e - e_max[dst])
        denom = segment_sum(e_exp, dst, num_segments=N)
        alpha = e_exp / (denom[dst] + EPS)
        out = segment_sum(Wh[src] * alpha[:, :, None], dst, num_segments=N)
        return out.reshape(N, H * C)

    def _L1_ffn_ref(x, weight, bias):
        import jax, jax.numpy as jnp
        import numpy as np
        IN_CH = 256
        OUT_CH = 256
        return jnp.einsum('bsi,oi->bso', x, weight) + bias

    def _L2_gnn_ref(x, edge_index, W, b, bn_w, bn_b):
        import jax, jax.numpy as jnp
        import numpy as np
        BN_EPS = 1e-05
        N = x.shape[0]
        src, dst = (edge_index[0], edge_index[1])
        agg = jax.ops.segment_sum(x[src], dst, num_segments=N)
        h = x + agg
        h = jnp.einsum('nf,hf->nh', h, W) + b
        mean = jnp.mean(h, axis=0)
        var = jnp.mean(jnp.square(h - mean), axis=0)
        out = (h - mean) * jax.lax.rsqrt(var + BN_EPS) * bn_w + bn_b
        return out

    def _L2_ffn_ref(x, gate_w, gate_b, W1, b1, W2, b2):
        import jax, jax.numpy as jnp
        import numpy as np
        B, T, D, H, E = (16, 512, 256, 512, 8)
        Bb, Tt, Dd = x.shape
        Ee = gate_w.shape[1]
        xf = x.reshape(-1, Dd)
        N = xf.shape[0]
        logits = xf @ gate_w + gate_b
        probs = jax.nn.softmax(logits, axis=-1)
        top2_vals, top2_idx = jax.lax.top_k(probs, 2)
        cw = jnp.zeros((N, Ee), dtype=xf.dtype).at[jnp.arange(N)[:, None], top2_idx].add(top2_vals)

        def step(acc, params):
            w1, bb1, w2, bb2, we = params
            h = jax.nn.gelu(xf @ w1 + bb1, approximate=False)
            y = h @ w2 + bb2
            return (acc + we[:, None] * y, None)
        out, _ = jax.lax.scan(step, jnp.zeros_like(xf), (W1, b1, W2, b2, cw.T))
        return out.reshape(Bb, Tt, Dd)

    def _L3_gnn_ref(x, edge_index, W_gcn, b_gcn, g0, beta0, W1, a_src1, a_dst1, b1, g1, beta1, W2, a_src2, a_dst2, b2, g2, beta2):
        import jax, jax.numpy as jnp
        import numpy as np
        N = 12500
        E = 100000
        F_IN = 256
        HID = 64
        H = 4
        NEG_SLOPE = 0.2
        BN_EPS = 1e-05

        def _add_self_loops(edge_index, n):
            loop = jnp.arange(n, dtype=edge_index.dtype)
            src = jnp.concatenate([edge_index[0], loop])
            dst = jnp.concatenate([edge_index[1], loop])
            return (src, dst)

        def _batch_norm(x, g, b):
            m = x.mean(0)
            v = x.var(0)
            return g * (x - m) * jax.lax.rsqrt(v + BN_EPS) + b

        def _gcn_conv(x, src, dst, W, b, n):
            deg = jax.ops.segment_sum(jnp.ones_like(dst, jnp.float32), dst, n)
            dinv = jax.lax.rsqrt(jnp.maximum(deg, 1.0))
            norm = dinv[src] * dinv[dst]
            h = x @ W
            out = jax.ops.segment_sum(h[src] * norm[:, None], dst, n)
            return out + b

        def _gat_conv(x, src, dst, W, a_src, a_dst, b, n):
            h = (x @ W).reshape(n, H, HID)
            alpha_s = jnp.einsum('nhc,hc->nh', h, a_src)
            alpha_d = jnp.einsum('nhc,hc->nh', h, a_dst)
            e = alpha_s[src] + alpha_d[dst]
            e = jnp.where(e > 0, e, NEG_SLOPE * e)
            emax = jax.ops.segment_max(e, dst, n)
            w = jnp.exp(e - emax[dst])
            wsum = jax.ops.segment_sum(w, dst, n)
            att = w / wsum[dst]
            out = jax.ops.segment_sum(att[:, :, None] * h[src], dst, n)
            return out.reshape(n, H * HID) + b
        n = x.shape[0]
        src, dst = _add_self_loops(edge_index, n)
        h = jax.nn.relu(_gcn_conv(x, src, dst, W_gcn, b_gcn, n))
        h = _batch_norm(h, g0, beta0)
        h = _gat_conv(h, src, dst, W1, a_src1, a_dst1, b1, n)
        h = jax.nn.elu(_batch_norm(h, g1, beta1))
        h = _gat_conv(h, src, dst, W2, a_src2, a_dst2, b2, n)
        h = jax.nn.elu(_batch_norm(h, g2, beta2))
        return h

    def _L3_ffn_ref(x, Wg, bg, W1, b1, W2, b2):
        import jax, jax.numpy as jnp
        import numpy as np
        B, S, D, E, H, K = (4, 512, 256, 8, 512, 2)
        Bv, Sv, Dv = x.shape
        gate_scores = x @ Wg + bg
        _, idx = jax.lax.top_k(gate_scores, K)
        mask = jax.nn.one_hot(idx, E, dtype=x.dtype).sum(axis=-2)
        xf = x.reshape(-1, Dv)
        mf = mask.reshape(-1, E)
        h = jax.nn.gelu(jnp.einsum('td,edh->teh', xf, W1) + b1[None], approximate=False)
        y = jnp.einsum('teh,ehd->ted', h, W2) + b2[None]
        out = jnp.einsum('ted,te->td', y, mf)
        return out.reshape(Bv, Sv, Dv)
    edge_index = jnp.stack([src, dst])
    x = x + _L0_gnn_ref(_layernorm(x, axis=-1), edge_weight, src, dst)
    x = x + _L0_ffn_ref(_layernorm(x, axis=-1)[None], L0_ffn_gate_w, L0_ffn_gate_b, L0_ffn_w1, L0_ffn_b1, L0_ffn_w2, L0_ffn_b2)[0]
    x = x + _L1_gnn_ref(_layernorm(x, axis=-1), edge_index, L1_gnn_W, L1_gnn_a_left, L1_gnn_a_right)
    x = x + _L1_ffn_ref(_layernorm(x, axis=-1)[None], L1_ffn_weight, L1_ffn_bias)[0]
    x = x + _L2_gnn_ref(_layernorm(x, axis=-1), edge_index, L2_gnn_W, L2_gnn_b, L2_gnn_bn_w, L2_gnn_bn_b)
    x = x + _L2_ffn_ref(_layernorm(x, axis=-1)[None], L2_ffn_gate_w, L2_ffn_gate_b, L2_ffn_W1, L2_ffn_b1, L2_ffn_W2, L2_ffn_b2)[0]
    x = x + _L3_gnn_ref(_layernorm(x, axis=-1), edge_index, L3_gnn_W_gcn, L3_gnn_b_gcn, L3_gnn_g0, L3_gnn_beta0, L3_gnn_W1, L3_gnn_a_src1, L3_gnn_a_dst1, L3_gnn_b1, L3_gnn_g1, L3_gnn_beta1, L3_gnn_W2, L3_gnn_a_src2, L3_gnn_a_dst2, L3_gnn_b2, L3_gnn_g2, L3_gnn_beta2)
    x = x + _L3_ffn_ref(_layernorm(x, axis=-1)[None], L3_ffn_Wg, L3_ffn_bg, L3_ffn_W1, L3_ffn_b1, L3_ffn_W2, L3_ffn_b2)[0]
    return x

_drawn_inputs = setup_inputs


def setup_inputs(seed=0):
    import zlib

    import numpy as np

    out = dict(_drawn_inputs(seed))
    spreads = {'L0_ffn_gate_b': (0.0, 0.1),
     'L0_ffn_b1': (0.0, 0.397),
     'L0_ffn_b2': (0.0, 0.307),
     'L2_gnn_b': (0.0, 2.0),
     'L2_gnn_bn_w': (1.0, 0.2),
     'L2_gnn_bn_b': (0.0, 0.1),
     'L2_ffn_gate_b': (0.0, 0.427),
     'L2_ffn_b1': (0.0, 0.8),
     'L2_ffn_b2': (0.0, 0.347),
     'L3_gnn_b_gcn': (0.0, 0.1),
     'L3_gnn_g0': (1.0, 0.2),
     'L3_gnn_beta0': (0.0, 2.0),
     'L3_gnn_b1': (0.0, 2.0),
     'L3_gnn_g1': (1.0, 0.2),
     'L3_gnn_beta1': (0.0, 0.365),
     'L3_gnn_b2': (0.0, 2.0),
     'L3_gnn_g2': (1.0, 0.2),
     'L3_gnn_beta2': (0.0, 0.1),
     'L3_ffn_bg': (0.0, 0.1),
     'L3_ffn_b1': (0.0, 0.422),
     'L3_ffn_b2': (0.0, 0.1)}
    factors = {'L2_ffn_gate_w': 2.679, 'L2_ffn_W1': 3.575, 'L2_ffn_W2': 3.395}
    for name, (base, spread) in spreads.items():
        noise = np.random.default_rng([zlib.crc32(name.encode()), seed]).standard_normal(out[name].shape)
        drawn = base * np.exp(spread * noise) if base else spread * noise
        out[name] = jnp.asarray(drawn.astype(out[name].dtype))
    for name, factor in factors.items():
        out[name] = (out[name] * factor).astype(out[name].dtype)
    return out
```

```python
import numpy as np
import concourse.bass as bass
from concourse import mybir
from contextlib import ExitStack

F32 = mybir.dt.float32
BF16 = mybir.dt.bfloat16
I32 = mybir.dt.int32
ALU = mybir.AluOpType
ACT = mybir.ActivationFunctionType
AX = mybir.AxisListType
DVE_ONLY = (mybir.EngineType.DVE,)

P = 128
N_NODES, D, N_EDGES = 6250, 256, 100000
NT = -(-N_NODES // P)
NP = NT * P
LAST = N_NODES - (NT - 1) * P
J = 16
CH = P * J
NC = -(-N_EDGES // CH)
EP = NC * CH
LC = N_EDGES - (NC - 1) * CH
BIG = 1e30
LN_EPS = 1e-5
assert LC % J == 0 and NC == NT


class Phase:

    def __init__(self, nc, name):
        self.nc, self.name, self.stack, self.sems = nc, f"{name}_{nc.next_id()}", ExitStack(), []

    def __enter__(self):
        return self

    def __exit__(self, *failed):
        self.stack.close()
        if failed[0] is None:
            self.nc.clear_and_free_semaphores(self.sems)
            self.nc.all_engine_barrier()

    def sb(self, name, shape, dt=F32):
        return self.stack.enter_context(self.nc.sbuf_tensor(f"{self.name}_{name}", shape, dt))

    def ps(self, name, shape, dt=F32):
        return self.stack.enter_context(self.nc.psum_tensor(f"{self.name}_{name}", shape, dt))

    def sem(self, name):
        self.sems.append(self.nc.alloc_semaphore(f"{self.name}_{name}"))
        return self.sems[-1]


class Chain:

    def __init__(self, eng, sem, base=0):
        self.eng, self.sem, self.base, self.n = eng, sem, base, 0

    def do(self, ins, wait=True):
        ins.then_inc(self.sem, 1)
        self.n += 1
        if wait:
            self.eng.wait_ge(self.sem, self.base + self.n)


def by_two(eng, n, body):
    with eng.Fori(0, n // 2) as i:
        body(2 * i, 0)
        body(2 * i + 1, 1)
    if n % 2:
        body(n - 1, 0)


def dram_view(ap, offset, dims):
    return bass.AP(tensor=ap.tensor, offset=offset, ap=[list(d) for d in dims])


class Store:
    pass


def constants(nc, g):
    with Phase(nc, "const") as ph:
        zeroed, placed, seq = ph.sem("zeroed"), ph.sem("placed"), ph.sem("seq")
        x_in, pad, low_ready, filled = ph.sem("x_in"), ph.sem("pad"), ph.sem("low_ready"), ph.sem("filled")
        low = ph.sb("low", [P, EP * 4 // P])
        with nc.Block() as block:
            @block.gpsimd
            def _(gp):
                nc.gpsimd.memset(g.ident[:, :], 0.0).then_inc(zeroed, 1)
                nc.gpsimd.memset(g.ones[:, :], 1.0).then_inc(placed, 1)
                gp.wait_ge(zeroed, 1)
                nc.gpsimd.affine_select(out=g.ident[:, :], in_=g.ident[:, :], compare_op=ALU.not_equal, fill=1.0,
                                        base=0, pattern=[[-1, P]], channel_multiplier=1).then_inc(placed, 1)
                nc.gpsimd.iota(g.iota_i[:, :], [[1, P]], base=0, channel_multiplier=0).then_inc(seq, 1)

            @block.vector
            def _(dv):
                nc.vector.memset(g.x[:, NT - 1, :], 0.0).then_inc(pad, 1)
                nc.vector.memset(low[:, :], -BIG).then_inc(low_ready, 1)
                dv.wait_ge(seq, 1)
                nc.vector.tensor_copy(g.iota[:, :], g.iota_i[:, :]).then_inc(placed, 1)

            @block.scalar
            def _(ac):
                ac.wait_ge(low_ready, 1)
                n = EP * 16 // P // 4
                for q in range(4):
                    ac.dma_start(g.inject8.rearrange("(p r) q -> p (r q)", p=P)[:, q * n:(q + 1) * n], low[:, :]).then_inc(filled, 16)
                for q in range(2):
                    ac.dma_start(g.inject4.rearrange("(p r) q -> p (r q)", p=P)[:, q * n:(q + 1) * n], low[:, :]).then_inc(filled, 16)
                ac.wait_ge(filled, 6 * 16)

            @block.sync
            def _(sp):
                sp.dma_start(g.x[:, 0:NT - 1, :], g.x_dram[0:(NT - 1) * P, :].rearrange("(t p) d -> p t d", p=P)).then_inc(x_in, 16)
                sp.wait_ge(pad, 1)
                sp.dma_start(g.x[0:LAST, NT - 1, :], g.x_dram[(NT - 1) * P:N_NODES, :]).then_inc(x_in, 16)
                sp.wait_ge(x_in, 32)


def edge_tables(nc, g):
    with Phase(nc, "edge") as ph:
        around = ph.sb("around", [P, NC, J + 2], I32)
        dst_i = ph.sb("dst_i", [P, NC * J], I32)
        hi_i = ph.sb("hi_i", [P, NC * J], I32)
        lo_i = ph.sb("lo_i", [P, NC * J], I32)
        hi = ph.sb("hi", [P, NC, J], BF16)
        lo = ph.sb("lo", [P, NC, J], BF16)
        iota_b = ph.sb("iota_b", [P, P], BF16)
        start = ph.sb("start", [P, NC, J])
        start_next = ph.sb("start_next", [P, NC, J])
        not_first = ph.sb("not_first", [P, NC, J])
        not_last = ph.sb("not_last", [P, NC, J])
        seen = ph.sb("seen", [P, NC, J])
        seen_b = ph.sb("seen_b", [P, NC, J])
        tmp = ph.sb("tmp", [P, NC, J])
        resets = ph.sb("resets", [P, 2, NC])
        reset_rows = ph.sb("reset_rows", [NC, 2, P])
        first_lo = ph.sb("first_lo", [1, 2, NC], I32)
        first_lof = ph.sb("first_lof", [1, NC])
        first_hot = g.agg[0:1, :, :].rearrange("o t w -> o (t w)")[:, 0:NC * 2 * P].rearrange("o (c a p) -> o c a p", c=NC, a=2)
        hot_lo = ph.sb("hot_lo", [P, 2, J, P], BF16)
        hot_hi = ph.sb("hot_hi", [P, 2, J, NT], BF16)
        zero_b = ph.sb("zero_b", [P, P], BF16)
        tri = ph.sb("tri", [NT, NT])
        deg = ph.sb("deg", [NT, P])
        first = ph.sb("first", [NT, P])
        none = ph.sb("none", [NT, P])
        offs = ph.sb("offs", [NT, 1])
        p_rs = ph.ps("p_rs", [NC, 2, P])
        p_deg = ph.ps("p_deg", [NT, P])
        p_off = ph.ps("p_off", [NT, 1])
        p_t = ph.ps("p_t", [P, 2, NT])
        blank, d_in, s_in, no_src, rs_done = (ph.sem(n) for n in ("blank", "d_in", "s_in", "no_src", "rs_done"))
        ops, rs_t, rs_ready = ph.sem("ops"), ph.sem("rs_t"), ph.sem("rs_ready")
        hot, hot_free, deg_done, deg_ready, off_done, t_done = (ph.sem(n) for n in ("hot", "hot_free", "deg_done", "deg_ready", "off_done", "t_done"))
        stored, tri_ready, hot_row = ph.sem("stored"), ph.sem("tri_ready"), ph.sem("hot_row")
        dst, src = g.dst_dram, g.src_dram
        full = NC - 1
        lp = LC // J
        flat = lambda t: t[:, :, :].rearrange("p c j -> p (c j)")
        with nc.Block() as block:
            @block.sync
            def _(sp):
                sp.wait_ge(blank, 2)
                sp.wait_ge(no_src, 1)
                e0 = full * CH
                sp.dma_start(around[:, 1:full, :], dram_view(dst, CH - 1, [[J, P], [CH, full - 1], [1, J + 2]])).then_inc(d_in, 16)
                sp.dma_start(around[1:P, 0, :], dram_view(dst, J - 1, [[J, P - 1], [1, J + 2]])).then_inc(d_in, 16)
                sp.dma_start(around[0:1, 0, 1:J + 2], dram_view(dst, 0, [[J, 1], [1, J + 1]])).then_inc(d_in, 16)
                sp.dma_start(around[0:lp - 1, full, :], dram_view(dst, e0 - 1, [[J, lp - 1], [1, J + 2]])).then_inc(d_in, 16)
                sp.dma_start(around[lp - 1:lp, full, 0:J + 1], dram_view(dst, e0 + (lp - 1) * J - 1, [[J, 1], [1, J + 1]])).then_inc(d_in, 16)
                sp.dma_start(around[lp:lp + 1, full, 0:1], dram_view(dst, N_EDGES - 1, [[1, 1], [1, 1]])).then_inc(d_in, 16)
                sp.dma_start(g.src_idx[:, 0:full * J].rearrange("p (c j) -> p c j", j=J),
                             dram_view(src, 0, [[J, P], [CH, full], [1, J]])).then_inc(s_in, 16)
                sp.dma_start(g.src_idx[0:lp, full * J:NC * J], dram_view(src, e0, [[J, lp], [1, J]])).then_inc(s_in, 16)
                sp.wait_ge(rs_ready, 1)
                sp.dma_start(g.resets_dram, reset_rows[:, :, :]).then_inc(stored, 16)
                sp.wait_ge(hot_row, 1)
                sp.dma_start(g.first_hot_dram, first_hot.rearrange("o c a p -> o (c a p)")).then_inc(stored, 16)
                sp.wait_ge(s_in, 32)
                sp.wait_ge(stored, 32)

            @block.gpsimd
            def _(gp):
                nc.gpsimd.memset(g.src_idx[:, :], 0).then_inc(no_src, 1)
                nc.gpsimd.memset(tri[:, :], 0.0).then_inc(tri_ready, 1)
                gp.wait_ge(tri_ready, 1)
                nc.gpsimd.affine_select(out=tri[:, :], in_=tri[:, :], compare_op=ALU.is_ge, fill=1.0,
                                        base=0, pattern=[[-1, NT]], channel_multiplier=1).then_inc(tri_ready, 1)

            @block.vector
            def _(dv):
                nc.vector.memset(around[:, :, :], NP - 1).then_inc(blank, 1)
                dv.wait_ge(blank, 1)
                ch = Chain(dv, ops)
                ch.do(nc.vector.memset(zero_b[:, :], 0.0))
                nc.vector.memset(around[0:1, 0, 0:1], -1).then_inc(blank, 1)
                ch.do(nc.vector.memset(not_first[:, :, :], 1.0), wait=False)
                ch.do(nc.vector.memset(not_last[:, :, :], 1.0))
                ch.do(nc.vector.memset(not_first[:, :, 0:1], 0.0), wait=False)
                ch.do(nc.vector.memset(not_last[:, :, J - 1:J], 0.0), wait=False)
                ch.do(nc.vector.tensor_copy(iota_b[:, :], g.iota[:, :]), wait=False)
                dv.wait_ge(d_in, 6 * 16)
                ch.do(nc.vector.tensor_tensor(start[:, :, :], around[:, :, 1:J + 1], around[:, :, 0:J], ALU.not_equal), wait=False)
                ch.do(nc.vector.tensor_tensor(start_next[:, :, :], around[:, :, 2:J + 2], around[:, :, 1:J + 1], ALU.not_equal), wait=False)
                ch.do(nc.vector.tensor_copy(dst_i[:, :].rearrange("p (c j) -> p c j", j=J), around[:, :, 1:J + 1]))
                ch.do(nc.vector.tensor_copy(g.dstf[:, :], dst_i[:, :]), wait=False)
                ch.do(nc.vector.tensor_scalar(hi_i[:, :], dst_i[:, :], 7, None, ALU.arith_shift_right), wait=False)
                ch.do(nc.vector.tensor_scalar(lo_i[:, :], dst_i[:, :], P - 1, None, ALU.bitwise_and))
                ch.do(nc.vector.tensor_copy(flat(hi), hi_i[:, :]), wait=False)
                ch.do(nc.vector.tensor_copy(flat(lo), lo_i[:, :]), wait=False)
                ch.do(nc.vector.tensor_scalar(tmp[:, :, :], not_first[:, :, :], -1.0, 1.0, ALU.mult, ALU.add))
                ch.do(nc.vector.tensor_tensor(seen[:, :, :], tmp[:, :, :], start[:, :, :], ALU.max))
                ch.do(nc.vector.tensor_scalar(tmp[:, :, :], not_last[:, :, :], -1.0, 1.0, ALU.mult, ALU.add))
                ch.do(nc.vector.tensor_scalar(g.fwd_reset[:, :], flat(seen), -BIG, None, ALU.mult))
                ch.do(nc.vector.tensor_tensor(seen_b[:, :, :], tmp[:, :, :], start_next[:, :, :], ALU.max))
                ch.do(nc.vector.tensor_scalar(g.bwd_reset[:, :], flat(seen_b), -BIG, None, ALU.mult))
                ch.do(nc.vector.tensor_tensor_scan(flat(seen), flat(not_first), flat(start), 0.0, ALU.mult, ALU.max), wait=False)
                ch.do(nc.vector.tensor_tensor_scan(flat(seen_b)[:, ::-1], flat(not_last)[:, ::-1], flat(start_next)[:, ::-1], 0.0, ALU.mult, ALU.max))
                ch.do(nc.vector.tensor_scalar(g.fwd_block[:, :], flat(seen), -BIG, None, ALU.mult), wait=False)
                ch.do(nc.vector.tensor_scalar(g.bwd_block[:, :], flat(seen_b), -BIG, None, ALU.mult), wait=False)
                ch.do(nc.vector.tensor_copy(resets[:, 0, :], seen[:, :, J - 1]), wait=False)
                ch.do(nc.vector.tensor_tensor(resets[:, 1, :], seen[:, :, J - 1], start_next[:, :, J - 1], ALU.max))
                nc.vector.sem_inc(rs_t, 1)
                ch.do(nc.vector.tensor_copy(g.chunk_tile[0:1, 0:NC], hi_i[0:1, :].rearrange("p (c j) -> p c j", j=J)[:, :, 0]), wait=False)
                ch.do(nc.vector.memset(g.chunk_tile[0:1, NC:NC + 1], NT - 1), wait=False)
                ch.do(nc.vector.tensor_copy(first_lof[0:1, :], lo_i[0:1, :].rearrange("p (c j) -> p c j", j=J)[:, :, 0]))
                ch.do(nc.vector.tensor_tensor(first_hot[0:1, :, 0, :], g.iota[0:1, :].unsqueeze(1).to_broadcast([1, NC, P]),
                                              first_lof[0:1, :].unsqueeze(2).to_broadcast([1, NC, P]), ALU.is_equal))
                nc.vector.tensor_scalar(first_hot[0:1, :, 1, :], first_hot[0:1, :, 0, :], -1.0, 1.0, ALU.mult, ALU.add).then_inc(hot_row, 1)
                dv.wait_ge(rs_done, 2)
                nc.vector.tensor_scalar(reset_rows[:, :, :], p_rs[:, :, :], -BIG, None, ALU.mult).then_inc(rs_ready, 1)
                nc.vector.sem_inc(hot_free, 2)

                def hots(c, s):
                    dv.wait_ge(hot_free, c + 1)
                    nc.vector.tensor_tensor(hot_lo[:, s, :, :], iota_b[:, :].unsqueeze(1).to_broadcast([P, J, P]),
                                            lo[:, bass.ds(c, 1), :].rearrange("p a j -> p (a j)").unsqueeze(2).to_broadcast([P, J, P]), ALU.is_equal).then_inc(hot, 1)
                    nc.vector.tensor_tensor(hot_hi[:, s, :, :], iota_b[:, 0:NT].unsqueeze(1).to_broadcast([P, J, NT]),
                                            hi[:, bass.ds(c, 1), :].rearrange("p a j -> p (a j)").unsqueeze(2).to_broadcast([P, J, NT]), ALU.is_equal).then_inc(hot, 1)
                by_two(dv, NC, hots)
                dv.wait_ge(deg_done, 1)
                ch.do(nc.vector.tensor_copy(deg[:, :], p_deg[:, :]))
                ch.do(nc.vector.tensor_tensor_scan(first[:, :], deg[:, :], deg[:, :], 0.0, ALU.add, ALU.bypass))
                nc.vector.sem_inc(deg_ready, 1)
                dv.wait_ge(off_done, 1)
                ch.do(nc.vector.tensor_copy(offs[:, :], p_off[:, :]))
                ch.do(nc.vector.tensor_tensor(first[:, :], first[:, :], deg[:, :], ALU.subtract), wait=False)
                ch.do(nc.vector.tensor_scalar(none[:, :], deg[:, :], 0.0, 2.0 * EP, ALU.is_equal, ALU.mult))
                ch.do(nc.vector.scalar_tensor_tensor(out=first[:, :], in0=first[:, :], scalar=offs[:, 0:1], in1=none[:, :], op0=ALU.add, op1=ALU.add))
                nc.vector.sem_inc(deg_ready, 1)
                dv.wait_ge(t_done, 2)
                ch.do(nc.vector.tensor_copy(g.deg[:, :], p_t[:, 0, :]), wait=False)
                ch.do(nc.vector.tensor_copy(g.first_edge[:, :], p_t[:, 1, :]))
                ch.do(nc.vector.tensor_scalar(g.no_edges[:, :], g.deg[:, :], 0.0, None, ALU.is_equal))

            @block.tensor
            def _(pe):
                pe.wait_ge(rs_t, 1)
                for a in range(2):
                    nc.tensor.transpose(p_rs[:, a, :], resets[:, a, :], g.ident[:, :]).then_inc(rs_done, 1)
                pe.wait_ge(ops, 1)
                nc.tensor.matmul(p_deg[:, :], zero_b[:, 0:NT], zero_b[:, :], start=True, stop=False, skip_group_check=True)

                def count(c, s):
                    pe.wait_ge(hot, 2 * (c + 1))
                    for j in range(J):
                        last = nc.tensor.matmul(p_deg[:, :], hot_hi[:, s, j, :], hot_lo[:, s, j, :], start=False, stop=False, skip_group_check=True)
                    last.then_inc(hot_free, 1)
                by_two(pe, NC, count)
                nc.tensor.matmul(p_deg[:, :], zero_b[:, 0:NT], zero_b[:, :], start=False, stop=True, skip_group_check=True).then_inc(deg_done, 1)
                pe.wait_ge(deg_ready, 1)
                pe.wait_ge(tri_ready, 2)
                nc.tensor.matmul(p_off[:, :], tri[:, :], first[:, P - 1:P], start=True, stop=True).then_inc(off_done, 1)
                pe.wait_ge(deg_ready, 2)
                nc.tensor.transpose(p_t[:, 0, :], deg[:, :], g.ident[0:NT, 0:NT]).then_inc(t_done, 1)
                nc.tensor.transpose(p_t[:, 1, :], first[:, :], g.ident[0:NT, 0:NT]).then_inc(t_done, 1)


def setup(nc, a, out):
    g = Store()
    nc.keep = ExitStack()
    sb = lambda n, s, d=F32: nc.keep.enter_context(nc.sbuf_tensor(n, s, d))
    dr = lambda n, s, d=F32: nc.dram_tensor(n, s, d, kind="Internal").ap()
    g.a, g.out = a, out
    g.x_dram, g.src_dram, g.dst_dram = a["x"], a["src"], a["dst"]
    g.ident, g.ones, g.iota, g.iota_i = sb("ident", [P, P]), sb("ones", [P, P]), sb("iota", [P, P]), sb("iota_i", [P, P], I32)
    g.x = sb("x", [P, NT, D])
    g.src_idx = sb("src_idx", [P, NC * J], I32)
    g.dstf = sb("dstf", [P, NC * J])
    g.fwd_reset, g.bwd_reset, g.fwd_block, g.bwd_block = (
        sb(n, [P, NC * J]) for n in ("fwd_reset", "bwd_reset", "fwd_block", "bwd_block"))
    g.chunk_tile = sb("chunk_tile", [1, NC + 1], I32)
    g.deg, g.no_edges, g.first_edge = sb("deg", [P, NT]), sb("no_edges", [P, NT]), sb("first_edge", [P, NT], I32)
    g.rstd, g.shift = sb("rstd", [P, NT]), sb("shift", [P, NT])
    g.agg = sb("agg", [P, NT, D + 16])
    g.table = dr("table", [NP, D + 8])
    g.inject8, g.inject4 = dr("inject8", [EP, 16]), dr("inject4", [EP, 8])
    g.resets_dram = dr("resets_dram", [NC, 2, P])
    g.first_hot_dram = dr("first_hot_dram", [1, NC * 2 * P])
    return g

R = 3


def layernorm_stats(nc, g):
    with Phase(nc, "ln") as ph:
        stats = ph.sb("stats", [P, NT, 6])
        mean, var, std, gap, eps = (ph.sb(n, [P, NT]) for n in ("mean", "var", "std", "gap", "eps"))
        st, ops, rooted = ph.sem("st"), ph.sem("ops"), ph.sem("rooted")
        with nc.Block() as block:
            @block.vector
            def _(dv):
                ch = Chain(dv, ops)
                ch.do(nc.vector.memset(eps[:, :], LN_EPS))
                with dv.Fori(0, NT) as i:
                    nc.vector.bn_stats(stats[:, bass.ds(i, 1), :].rearrange("p a d -> p (a d)"), g.x[:, bass.ds(i, 1), :].rearrange("p a d -> p (a d)")).then_inc(st, 1)
                dv.wait_ge(st, NT)
                ch.do(nc.vector.tensor_tensor(mean[:, :], stats[:, :, 1], stats[:, :, 4], ALU.add))
                ch.do(nc.vector.tensor_tensor(gap[:, :], stats[:, :, 1], stats[:, :, 4], ALU.subtract))
                ch.do(nc.vector.tensor_scalar(mean[:, :], mean[:, :], 0.5, None, ALU.mult))
                ch.do(nc.vector.tensor_tensor(var[:, :], stats[:, :, 2], stats[:, :, 5], ALU.add))
                ch.do(nc.vector.scalar_tensor_tensor(out=gap[:, :], in0=gap[:, :], scalar=0.25, in1=gap[:, :], op0=ALU.mult, op1=ALU.mult))
                ch.do(nc.vector.scalar_tensor_tensor(out=var[:, :], in0=var[:, :], scalar=1.0 / D, in1=gap[:, :], op0=ALU.mult, op1=ALU.add))
                dv.wait_ge(rooted, 1)
                ch.do(nc.vector.reciprocal(g.rstd[:, :], std[:, :]))
                ch.do(nc.vector.scalar_tensor_tensor(out=g.shift[:, :], in0=mean[:, :], scalar=-1.0, in1=g.rstd[:, :], op0=ALU.mult, op1=ALU.mult))

            @block.scalar
            def _(ac):
                ac.wait_ge(ops, 7)
                nc.scalar.activation(std[:, :], var[:, :], ACT.Sqrt, bias=eps[:, 0:1]).then_inc(rooted, 1)


def normalised(nc, g, out, i):
    return nc.scalar.activation(out, g.x[:, bass.ds(i, 1), :].rearrange("p a d -> p (a d)"), ACT.Identity,
                                scale=g.rstd[:, bass.ds(i, 1)], bias=g.shift[:, bass.ds(i, 1)])



def ahead(eng, n, first, second):
    first(0, 0)
    with eng.Fori(0, n // 2) as i:
        first(2 * i + 1, 1)
        second(2 * i, 0)
        first(2 * i + 2, 0)
        second(2 * i + 1, 1)
    second(n - 1, 0)


class Products:

    def __init__(self, nc, g, ph, kb, kp, cols, from_x):
        self.nc, self.g, self.kb, self.kp, self.from_x = nc, g, kb, kp, from_x
        self.xn = ph.sb("xn", [P, 2, kb * kp])
        self.xt = ph.sb("xt", [P, 2, kb, P])
        self.p_x = [ph.ps(f"p_x{s}", [P, kb, P]) for s in range(2)]
        self.out = [ph.ps(f"out{s}", [P, cols]) for s in range(2)]
        self.normal, self.turned, self.copied, self.multiplied, self.taken = (
            ph.sem(n) for n in ("normal", "turned", "copied", "multiplied", "taken"))

    def scalar(self, ac):
        nc, kp = self.nc, self.kp
        nc.scalar.sem_inc(self.copied, 2)
        nc.scalar.sem_inc(self.normal, 2)

        def normalise(i, s):
            ac.wait_ge(self.turned, i + 1)
            if self.from_x:
                normalised(nc, self.g, self.xn[:, s, :], i).then_inc(self.normal, 1)
            else:
                f = self.g.agg[:, bass.ds(i, 1), 0:self.kb * kp].rearrange("p a d -> p (a d)")
                nc.scalar.activation(self.xn[:, s, :], f, ACT.Identity).then_inc(self.normal, 1)

        def copy(i, s):
            ac.wait_ge(self.turned, i + 3)
            ac.wait_ge(self.multiplied, i + 1)
            nc.scalar.activation(self.xt[0:kp, s, :, :], self.p_x[s][0:kp, :, :], ACT.Identity).then_inc(self.copied, 1)
        ahead(ac, NT, normalise, copy)

    def tensor(self, pe, rhs):
        nc, kp, kb = self.nc, self.kp, self.kb
        nc.tensor.sem_inc(self.turned, 2)
        nc.tensor.sem_inc(self.multiplied, 2)

        def turn(i, s):
            pe.wait_ge(self.normal, i + 3)
            pe.wait_ge(self.copied, i + 1)
            if kp < P:
                pe.nop(nofuse=True)
            for b in range(kb):
                last = nc.tensor.transpose(self.p_x[s][0:kp, b, :], self.xn[:, s, b * kp:(b + 1) * kp], self.g.ident[:, :])
            last.then_inc(self.turned, 1)

        def multiply(i, s):
            pe.wait_ge(self.copied, i + 3)
            pe.wait_ge(self.taken, i + 1)
            for b in range(kb):
                last = nc.tensor.matmul(self.out[s][:, :], self.xt[0:kp, s, b, :], rhs[0:kp, b, :], start=(b == 0), stop=(b == kb - 1))
            last.then_inc(self.multiplied, 1)
        ahead(pe, NT, turn, multiply)


def gat_table(nc, g, name, w, a_left, a_right, heads, din, out_in, table, inject, from_x):
    H, C, KB = heads, D // heads, -(-din // P)
    kp = min(din, P)
    cols = D + 3 * H
    if from_x:
        layernorm_stats(nc, g)
    with Phase(nc, name) as ph:
        w_in = ph.sb("w_in", [P, 2, D])
        w_tr = ph.sb("w_tr", [P, 2, D])
        rhs = ph.sb("rhs", [P, KB, cols])
        acol = ph.sb("acol", [P, 2, 2])
        who = ph.sb("who", [P, 2, H], I32)
        whof = ph.sb("whof", [P, 2, H])
        mask = ph.sb("mask", [P, 2, H])
        blockdiag = ph.sb("blockdiag", [P, 2, 2 * H])
        row = ph.sb("row", [P, 2, cols])
        idx = ph.sb("idx", [P, 2], I32)
        p_w = ph.ps("p_w", [P, 4, P])
        p_a = ph.ps("p_a", [P, KB, 2 * H])
        prod = Products(nc, g, ph, KB, kp, cols, from_x)
        loaded, seq, ops, wt, wa = (ph.sem(n) for n in ("loaded", "seq", "ops", "wt", "wa"))
        idx_ready, weights = ph.sem("idx_ready"), ph.sem("weights")
        stored = [ph.sem(f"stored{s}") for s in range(2)]
        scattered = [ph.sem(f"scattered{s}") for s in range(2)]
        OB = 2 if out_in else KB
        rows = P if out_in else kp
        with nc.Block() as block:
            @block.sync
            def _(sp):
                sp.dma_start(w_in[0:rows, 0:OB, :], w.rearrange("(b p) n -> p b n", p=rows)).then_inc(loaded, 16)
                for side, a in enumerate((a_left, a_right)):
                    for ob in range(2):
                        sp.dma_start(acol[:, side, ob:ob + 1], dram_view(a, ob * P, [[1, P], [1, 1]])).then_inc(loaded, 16)

                def store(i, s):
                    sp.wait_ge(prod.taken, i + 3)
                    sp.dma_start(table[bass.ds(i * P, P), :], row[:, s, 0:D + H]).then_inc(stored[s], 16)
                by_two(sp, NT, store)
                sp.wait_ge(stored[0], 16 * (NT // 2 + 1))
                sp.wait_ge(stored[1], 16 * (NT // 2))

            @block.gpsimd
            def _(gp):
                nc.gpsimd.iota(who[:, :, :], [[P, 2], [-C, H]], base=0, channel_multiplier=1).then_inc(seq, 1)

                with gp.Fori(0, NT // 2) as i:
                    for s in range(2):
                        n = 2 * i + s
                        gp.wait_ge(prod.taken, n + 3)
                        nc.gpsimd.tensor_copy(idx[:, s:s + 1], g.first_edge[:, bass.ds(n, 1)]).then_inc(idx_ready, 1)
                        gp.wait_ge(idx_ready, n + 1)
                        gp.nop(nofuse=True)
                        gp.indirect_dma_start(inject, bass.IndirectOffsetOnAxis(idx[:, s:s + 1], 0), row[:, s, D + H:D + 3 * H], None,
                                              bounds_check=EP - 1, oob_is_err=False).then_inc(scattered[s], 16)
                    for s in range(2):
                        gp.wait_ge(scattered[s], 16 * (i + 1))
                gp.wait_ge(prod.taken, NT + 2)
                nc.gpsimd.tensor_copy(idx[:, 0:1], g.first_edge[:, NT - 1:NT]).then_inc(idx_ready, 1)
                gp.wait_ge(idx_ready, NT)
                gp.indirect_dma_start(inject, bass.IndirectOffsetOnAxis(idx[:, 0:1], 0), row[:, 0, D + H:D + 3 * H], None,
                                      bounds_check=EP - 1, oob_is_err=False).then_inc(scattered[0], 16)
                gp.wait_ge(scattered[0], 16 * (NT // 2 + 1))

            @block.vector
            def _(dv):
                ch = Chain(dv, ops)
                dv.wait_ge(seq, 1)
                ch.do(nc.vector.tensor_copy(whof[:, :, :], who[:, :, :]))
                ch.do(nc.vector.tensor_scalar(mask[:, :, :], whof[:, :, :], 0.0, None, ALU.is_ge))
                ch.do(nc.vector.scalar_tensor_tensor(out=mask[:, :, :], in0=whof[:, :, :], scalar=float(C), in1=mask[:, :, :], op0=ALU.is_lt, op1=ALU.mult))
                dv.wait_ge(loaded, 5 * 16)
                for side in range(2):
                    ch.do(nc.vector.tensor_tensor(blockdiag[:, :, side * H:(side + 1) * H], mask[:, :, :],
                                                  acol[:, side, :].unsqueeze(2).to_broadcast([P, 2, H]), ALU.mult))
                nc.vector.sem_inc(weights, 1)
                dv.wait_ge(wt, 4 if KB == 2 else 2)
                if out_in:
                    for ob in range(2):
                        for ib in range(2):
                            ch.do(nc.vector.tensor_copy(rhs[:, ib, ob * P:(ob + 1) * P], p_w[:, 2 * ob + ib, :]))
                else:
                    for ib in range(KB):
                        for ob in range(2):
                            ch.do(nc.vector.tensor_copy(w_tr[:, ob, ib * kp:(ib + 1) * kp], p_w[:, 2 * ib + ob, 0:kp]))
                        ch.do(nc.vector.tensor_copy(rhs[0:kp, ib, 0:D], w_in[0:kp, ib, :]))
                nc.vector.sem_inc(weights, 1)
                dv.wait_ge(wa, KB)
                for ib in range(KB):
                    ch.do(nc.vector.tensor_copy(rhs[0:kp, ib, D:D + 2 * H], p_a[0:kp, ib, :]))
                    ch.do(nc.vector.tensor_copy(rhs[0:kp, ib, D + 2 * H:cols], p_a[0:kp, ib, 0:H]))
                nc.vector.sem_inc(weights, 1)

                nc.vector.sem_inc(prod.taken, 2)

                def take(i, s):
                    dv.wait_ge(prod.multiplied, i + 3)
                    nc.vector.tensor_copy(row[:, s, :], prod.out[s][:, :]).then_inc(prod.taken, 1)
                for s in range(2):
                    take(s, s)
                with dv.Fori(1, NT // 2) as i:
                    for s in range(2):
                        dv.wait_ge(stored[s], 16 * i)
                        dv.wait_ge(scattered[s], 16 * i)
                        take(2 * i + s, s)
                dv.wait_ge(stored[0], 16 * (NT // 2))
                dv.wait_ge(scattered[0], 16 * (NT // 2))
                take(NT - 1, 0)

            @block.scalar
            def _(ac):
                prod.scalar(ac)

            @block.tensor
            def _(pe):
                pe.wait_ge(loaded, 5 * 16)
                for a in range(OB):
                    for b in range(2):
                        nc.tensor.transpose(p_w[:, 2 * a + b, 0:rows], w_in[0:rows, a, b * P:(b + 1) * P], g.ident[0:rows, 0:rows]).then_inc(wt, 1)
                pe.wait_ge(weights, 2)
                w_oi = w_in if out_in else w_tr
                for ib in range(KB):
                    for ob in range(2):
                        last = nc.tensor.matmul(p_a[0:kp, ib, :], w_oi[:, ob, ib * kp:(ib + 1) * kp], blockdiag[:, ob, :], start=(ob == 0), stop=(ob == 1))
                    last.then_inc(wa, 1)
                pe.wait_ge(weights, 3)
                prod.tensor(pe, rhs)


ATT = ("right", "left", "forward", "carry_old", "carry", "blocked", "merged", "backward", "carry_back", "blocked_back", "maximum",
       "z_left", "z_self", "z_maximum", "z_old", "leaky", "less", "less_old", "clamped", "weighted")


def gather_pass(nc, g, name, table, width, heads=0, inject=None):
    H = heads
    C = D // H if H else 0
    W = width + 2 * H
    HJ, Q = H * J, 2 * H
    n_att = len(ATT)
    step = {n: k + 1 for k, n in enumerate(ATT)}
    with Phase(nc, name) as ph:
        rows = ph.sb("rows", [P, R, J, W])
        idx = ph.sb("idx", [P, R, J], I32)
        hot = ph.sb("hot", [P, J, P])
        near = ph.sb("near", [P, J])
        base = ph.sb("base", [P, NT])
        base_i = ph.sb("base_i", [P, NT], I32)
        p_sum = ph.ps("p_sum", [P, W])
        copied, seq, setup_v, halves, used, near_ready, added, g_free = (
            ph.sem(n) for n in ("copied", "seq", "setup_v", "halves", "used", "near_ready", "added", "g_free"))
        got = [ph.sem(f"got{s}") for s in range(R)]
        if H:
            inj = ph.sb("inj", [P, R, J, Q])
            reset = ph.sb("reset", [Q, R, 2, P])
            first_hot = ph.sb("first_hot", [1, R, 2, P])
            v, a, tmp = ph.sb("v", [P, Q, J]), ph.sb("a", [P, Q, J]), ph.sb("tmp", [P, Q, J])
            b, m = ph.sb("b", [P, H, J]), ph.sb("m", [P, H, J])
            z, e = ph.sb("z", [P, 3 * HJ + H]), ph.sb("e", [P, 2 * HJ + H])
            carry = ph.sb("carry", [Q, R, P + 1])
            back = ph.sb("back", [H, P + 1])
            resets_f, resets_b = ph.sb("resets_f", [P, Q, J]), ph.sb("resets_b", [P, H, J])
            fold = ph.sb("fold", [1, H])
            p_1, p_3 = ph.ps("p_1", [Q, P]), ph.ps("p_3", [H, P])
            p_2, p_4 = ph.ps("p_2", [P, Q]), ph.ps("p_4", [P, H])
            p_f = ph.ps("p_f", [P, H])
            att, turned, exped, factor, scaled, spread = (ph.sem(n) for n in ("att", "turned", "exped", "factor", "scaled", "spread"))
            side = [ph.sem(f"side{s}") for s in range(R)]

        def chunks(eng, body):
            with eng.Fori(0, NC // R) as i:
                for s in range(R):
                    body(R * i + s, s)
            body(NC - 1, 0)

        def staggered(eng, one, two):
            one(0, 0)
            with eng.Fori(0, NC // R) as i:
                for s in range(R):
                    one(R * i + s + 1, (s + 1) % R)
                    two(R * i + s, s)
            two(NC - 1, 0)
        assert NC % R == 1

        with nc.Block() as block:
            @block.sync
            def _(sp):
                def load(c, s):
                    with_c = bass.ds(c, 1)
                    if H:
                        sp.wait_ge(g_free, c + 1)
                        sp.dma_start(inj[:, s, :, :], inject[bass.ds(c * CH, CH), :].rearrange("(p j) q -> p j q", j=J)).then_inc(side[s], 16)
                        sp.dma_start(reset[:, s, :, :].rearrange("q a p -> q (a p)"),
                                     g.resets_dram[with_c, :, :].rearrange("c a p -> c (a p)").to_broadcast([Q, 2 * P])).then_inc(side[s], 16)
                        sp.dma_start(first_hot[0:1, s, :, :].rearrange("o a p -> o (a p)"), g.first_hot_dram[0:1, bass.ds(c * 2 * P, 2 * P)]).then_inc(side[s], 16)
                if H:
                    chunks(sp, load)

            @block.gpsimd
            def _(gp):
                nc.gpsimd.iota(base_i[:, :], [[P, NT]], base=0, channel_multiplier=0).then_inc(seq, 1)

                def gather(c, s):
                    gp.wait_ge(g_free, c + 1)
                    nc.gpsimd.tensor_copy(idx[:, s, :], g.src_idx[:, bass.ds(c * J, J)]).then_inc(copied, 1)
                    gp.wait_ge(copied, c + 1)
                    gp.nop(nofuse=True)
                    for j in range(J):
                        gp.indirect_dma_start(rows[:, s, j, 0:width + H], None, table, bass.IndirectOffsetOnAxis(idx[:, s, j:j + 1], 0)).then_inc(got[s], 16)
                chunks(gp, gather)

            @block.vector
            def _(dv):
                once = Chain(dv, setup_v)
                dv.wait_ge(seq, 1)
                once.do(nc.vector.tensor_copy(base[:, :], base_i[:, :]))
                once.do(nc.vector.memset(g.agg[:, :, 0:W], 0.0))
                nc.vector.sem_inc(g_free, R)
                nc.vector.sem_inc(added, 1)
                if H:
                    nc.vector.sem_inc(scaled, 2)
                if H:
                    once.do(nc.vector.memset(z[:, :], 0.0))
                    once.do(nc.vector.memset(e[:, :], 0.0))
                    once.do(nc.vector.memset(carry[:, R - 1, P:P + 1], -BIG))
                    once.do(nc.vector.memset(back[:, P:P + 1], -BIG))
                grid = lambda t, n: t.rearrange("p (q j) -> p q j", q=n)

                def attention(c, s):
                    n = Chain(dv, att, c * n_att)

                    def do(what, ins):
                        assert ATT[n.n] == what
                        n.do(ins)
                    edges = bass.ds(c * J, J)
                    over = lambda t, q: t[:, edges].unsqueeze(1).to_broadcast([P, q, J])
                    use = c // R if isinstance(c, int) else None
                    dv.wait_ge(side[s], c_uses(c, s, 48))
                    right, own = inj[:, s, :, 0:H].rearrange("p j h -> p h j"), inj[:, s, :, H:Q].rearrange("p j h -> p h j")
                    do("right", nc.vector.tensor_copy(v[:, 0:H, :], right))
                    dv.wait_ge(got[s], c_uses(c, s, 16 * J))
                    left = rows[:, s, :, width:width + H].rearrange("p j h -> p h j")
                    do("left", nc.vector.tensor_tensor(v[:, H:Q, :], left, own, ALU.max))
                    dv.wait_ge(spread, 2 * c + 2)
                    do("forward", nc.vector.tensor_tensor_scan(a[:, :, :].rearrange("p q j -> p (q j)"), resets_f[:, :, :].rearrange("p q j -> p (q j)"), v[:, :, :].rearrange("p q j -> p (q j)"), -BIG, ALU.add, ALU.max))
                    do("carry_old", nc.vector.tensor_copy(carry[:, s, 0:1], carry[:, (s - 1) % R, P:P + 1]))
                    dv.wait_ge(turned, 4 * c + 1)
                    do("carry", nc.vector.tensor_tensor_scan(carry[:, s, 1:P + 1], reset[:, s, 0, :], p_1[:, :], carry[:, s, 0:1], ALU.add, ALU.max))
                    dv.wait_ge(turned, 4 * c + 2)
                    do("blocked", nc.vector.tensor_tensor(tmp[:, :, :], over(g.fwd_block, Q), p_2[:, :].unsqueeze(2).to_broadcast([P, Q, J]), ALU.add))
                    do("merged", nc.vector.tensor_tensor(a[:, :, :], a[:, :, :], tmp[:, :, :], ALU.max))
                    do("backward", nc.vector.tensor_tensor_scan(b[:, :, :].rearrange("p q j -> p (q j)")[:, ::-1], resets_b[:, :, :].rearrange("p q j -> p (q j)")[:, ::-1],
                                                                a[:, H:Q, :].rearrange("p q j -> p (q j)")[:, ::-1], -BIG, ALU.add, ALU.max))
                    dv.wait_ge(turned, 4 * c + 3)
                    do("carry_back", nc.vector.tensor_tensor_scan(back[:, 0:P][:, ::-1], reset[0:H, s, 1, ::-1], p_3[:, ::-1], -BIG, ALU.add, ALU.max))
                    dv.wait_ge(turned, 4 * c + 4)
                    do("blocked_back", nc.vector.tensor_tensor(tmp[:, 0:H, :], over(g.bwd_block, H), p_4[:, :].unsqueeze(2).to_broadcast([P, H, J]), ALU.add))
                    do("maximum", nc.vector.tensor_tensor(m[:, :, :], b[:, :, :], tmp[:, 0:H, :], ALU.max))
                    do("z_left", nc.vector.tensor_tensor(grid(z[:, 0:HJ], H), a[:, 0:H, :], left, ALU.add))
                    do("z_self", nc.vector.tensor_tensor(grid(z[:, HJ:2 * HJ], H), a[:, 0:H, :], own, ALU.add))
                    do("z_maximum", nc.vector.tensor_tensor(z[:, 2 * HJ:3 * HJ], a[:, 0:H, :].rearrange("p q j -> p (q j)"), m[:, :, :].rearrange("p q j -> p (q j)"), ALU.add))
                    do("z_old", nc.vector.tensor_tensor(z[0:1, 3 * HJ:], a[0:1, 0:H, 0], p_2[0:1, H:Q], ALU.add))
                    do("leaky", nc.vector.scalar_tensor_tensor(out=z[:, :], in0=z[:, :], scalar=0.2, in1=z[:, :], op0=ALU.mult, op1=ALU.max))
                    if not (isinstance(c, int) and c == 0):
                        dv.wait_ge(exped, 2 * c)
                    do("less", nc.vector.tensor_tensor(grid(e[:, 0:2 * HJ], 2), grid(z[:, 0:2 * HJ], 2), z[:, 2 * HJ:3 * HJ].unsqueeze(1).to_broadcast([P, 2, HJ]), ALU.subtract))
                    do("less_old", nc.vector.tensor_tensor(e[0:1, 2 * HJ:], z[0:1, 3 * HJ:], grid(z[0:1, 2 * HJ:3 * HJ], H)[:, :, 0], ALU.subtract))
                    do("clamped", nc.vector.tensor_scalar(e[0:1, 2 * HJ:], e[0:1, 2 * HJ:], 0.0, None, ALU.min))
                    dv.wait_ge(exped, 2 * c + 2)
                    w = rows[:, s, :, width:width + H].unsqueeze(3).to_broadcast([P, J, H, C])
                    x = rows[:, s, :, 0:width].rearrange("p j (h c) -> p j h c", h=H)
                    do("weighted", nc.vector.tensor_tensor(x, x, w, ALU.mult))

                def sums(c, s):
                    if H:
                        dv.nop(nofuse=True)
                        k0 = dv.value_load(g.chunk_tile[0:1, bass.ds(c, 1)], min_val=0, max_val=NT - 1)
                        dv.wait_ge(factor, c + 1)
                        kept = g.agg[:, bass.ds(k0, 1), 0:D].rearrange("p a (h c) -> p (a h) c", h=H)
                        nc.vector.tensor_tensor(kept, kept, p_f[:, :].unsqueeze(2).to_broadcast([P, H, C]), ALU.mult).then_inc(scaled, 1)
                        kept = g.agg[:, bass.ds(k0, 1), D:D + Q].rearrange("p a (b h) -> p (a b) h", h=H)
                        nc.vector.tensor_tensor(kept, kept, p_f[:, :].unsqueeze(1).to_broadcast([P, 2, H]), ALU.mult).then_inc(scaled, 1)
                        dv.wait_ge(scaled, 2 * c + 4)
                    else:
                        dv.wait_ge(got[s], c_uses(c, s, 16 * J))
                        dv.nop(nofuse=True)
                        k0 = dv.value_load(g.chunk_tile[0:1, bass.ds(c, 1)], min_val=0, max_val=NT - 1)
                    dv.nop(nofuse=True)
                    k1 = dv.value_load(g.chunk_tile[0:1, bass.ds(c + 1, 1)], min_val=0, max_val=NT - 1)
                    with dv.Fori(k0, k1 + 1) as k:
                        pair = k + c
                        nc.vector.tensor_scalar(near[:, :], g.dstf[:, bass.ds(c * J, J)], base[:, bass.ds(k, 1)], None, ALU.subtract).then_inc(near_ready, 1)
                        dv.wait_ge(near_ready, pair + 1)
                        for half in range(2):
                            js = slice(half * J // 2, (half + 1) * J // 2)
                            dv.wait_ge(used, 2 * pair + half + 1)
                            nc.vector.tensor_tensor(hot[:, js, :], g.iota[:, :].unsqueeze(1).to_broadcast([P, J // 2, P]),
                                                    near[:, js].unsqueeze(2).to_broadcast([P, J // 2, P]), ALU.is_equal).then_inc(halves, 1)
                        dv.wait_ge(used, 2 * pair + 4)
                        into = g.agg[:, bass.ds(k, 1), 0:W].rearrange("p a w -> p (a w)")
                        nc.vector.tensor_tensor(into, into, p_sum[:, :], ALU.add).then_inc(added, 1)
                        dv.wait_ge(added, pair + 2)
                    nc.vector.sem_inc(g_free, 1)
                if H:
                    staggered(dv, attention, sums)
                else:
                    chunks(dv, sums)

            @block.scalar
            def _(ac):
                def exps(c, s):
                    if not (isinstance(c, int) and c == 0):
                        ac.wait_ge(att, c * n_att)
                    for out, q, t in ((resets_f, Q, g.fwd_reset), (resets_b, H, g.bwd_reset)):
                        nc.scalar.activation(out[:, :, :], t[:, bass.ds(c * J, J)].unsqueeze(1).to_broadcast([P, q, J]), ACT.Identity).then_inc(spread, 1)
                    ac.wait_ge(att, c * n_att + step["clamped"])
                    if not (isinstance(c, int) and c == 0):
                        ac.wait_ge(factor, c)
                    nc.scalar.activation(fold[0:1, :], e[0:1, 2 * HJ:], ACT.Exp).then_inc(exped, 1)
                    nc.scalar.activation(rows[:, s, :, width:W].rearrange("p j (b h) -> p b h j", b=2), e[:, 0:2 * HJ].rearrange("p (b h j) -> p b h j", b=2, h=H), ACT.Exp).then_inc(exped, 1)
                if H:
                    exps(0, 0)
                    with ac.Fori(0, NC // R) as i:
                        for s in range(R):
                            exps(R * i + s + 1, (s + 1) % R)

            @block.tensor
            def _(pe):
                nc.tensor.sem_inc(used, 2)

                def turns(c, s):
                    for out, src, rows_in, ready in ((p_1, lambda: a[:, :, J - 1], P, "forward"), (p_2, lambda: carry[:, s, 0:P], Q, "carry"),
                                                     (p_3, lambda: b[:, :, 0], P, "backward"), (p_4, lambda: back[:, 1:P + 1], H, "carry_back")):
                        pe.wait_ge(att, c * n_att + step[ready])
                        pe.nop(nofuse=True)
                        nc.tensor.transpose(out[:, :], src(), g.ident[0:rows_in, 0:rows_in]).then_inc(turned, 1)

                def sums(c, s):
                    if H:
                        pe.wait_ge(exped, 2 * c + 2)
                        pe.wait_ge(scaled, 2 * c + 2)
                        nc.tensor.matmul(p_f[:, :], first_hot[0:1, s, 0, :], fold[0:1, :], start=True, stop=False)
                        nc.tensor.matmul(p_f[:, :], first_hot[0:1, s, 1, :], g.ones[0:1, 0:H], start=False, stop=True).then_inc(factor, 1)
                        pe.wait_ge(att, c * n_att + n_att)
                    else:
                        pe.wait_ge(got[s], c_uses(c, s, 16 * J))
                    pe.nop(nofuse=True)
                    k0 = pe.value_load(g.chunk_tile[0:1, bass.ds(c, 1)], min_val=0, max_val=NT - 1)
                    k1 = pe.value_load(g.chunk_tile[0:1, bass.ds(c + 1, 1)], min_val=0, max_val=NT - 1)
                    with pe.Fori(k0, k1 + 1) as k:
                        pair = k + c
                        for half in range(2):
                            pe.wait_ge(halves, 2 * pair + half + 1)
                            if half == 0:
                                pe.wait_ge(added, pair + 1)
                            for j in range(half * J // 2, (half + 1) * J // 2):
                                last = nc.tensor.matmul(p_sum[:, :], hot[:, j, :], rows[:, s, j, :], start=(j == 0), stop=(j == J - 1))
                            last.then_inc(used, 1)
                if H:
                    staggered(pe, turns, sums)
                else:
                    chunks(pe, sums)


def c_uses(c, s, n):
    return n * (c // R + 1) if isinstance(c, int) else n * ((c - s) // R + 1)


def gat_finish(nc, g, name, table, heads, eps):
    H, C = heads, D // heads
    with Phase(nc, name) as ph:
        own = ph.sb("own", [P, 2, D])
        total, inv = ph.sb("total", [P, NT, H]), ph.sb("inv", [P, NT, H])
        seq = ph.sem("seq")
        prod, mixed, scaled = ph.sem("prod"), ph.sem("mixed"), ph.sem("scaled")
        loaded = [ph.sem(f"loaded{s}") for s in range(2)]
        with nc.Block() as block:
            @block.sync
            def _(sp):
                def load(i, s):
                    sp.dma_start(own[:, s, :], table[bass.ds(i * P, P), 0:D]).then_inc(loaded[s], 16)
                for s in range(2):
                    load(s, s)
                with sp.Fori(1, NT // 2) as i:
                    for s in range(2):
                        sp.wait_ge(mixed, 2 * i + s - 1)
                        load(2 * i + s, s)
                sp.wait_ge(mixed, NT - 2)
                load(NT - 1, 0)

            @block.vector
            def _(dv):
                ch = Chain(dv, seq)
                weights, selfs = g.agg[:, :, D:D + H], g.agg[:, :, D + H:D + 2 * H]
                ch.do(nc.vector.tensor_tensor(selfs, selfs, g.no_edges[:, :].unsqueeze(2).to_broadcast([P, NT, H]), ALU.add))
                ch.do(nc.vector.tensor_tensor(total[:, :, :], weights, selfs, ALU.add))
                ch.do(nc.vector.tensor_scalar(total[:, :, :], total[:, :, :], eps, None, ALU.add))
                ch.do(nc.vector.reciprocal(inv[:, :, :], total[:, :, :]))

                def tile(i, s):
                    dv.wait_ge(loaded[s], 16 * (((i - s) // 2) + 1))
                    one = bass.ds(i, 1)
                    heads_of = lambda t: t.rearrange("p a (h c) -> p (a h) c", h=H)
                    wide = lambda t: t.rearrange("p a h -> p (a h)").unsqueeze(2).to_broadcast([P, H, C])
                    o = own[:, s:s + 1, :]
                    nc.vector.tensor_tensor(heads_of(o), heads_of(o), wide(g.agg[:, one, D + H:D + 2 * H]), ALU.mult).then_inc(prod, 1)
                    dv.wait_ge(prod, i + 1)
                    nc.vector.tensor_tensor(g.agg[:, one, 0:D], g.agg[:, one, 0:D], o, ALU.add).then_inc(mixed, 1)
                    dv.wait_ge(mixed, i + 1)
                    nc.vector.tensor_tensor(heads_of(g.agg[:, one, 0:D]), heads_of(g.agg[:, one, 0:D]), wide(inv[:, one, :]), ALU.mult).then_inc(scaled, 1)
                by_two(dv, NT, tile)


def turned_weights(nc, g, w, name):
    with Phase(nc, name) as ph:
        w_in = ph.sb("w_in", [P, 2, D])
        p_w = ph.ps("p_w", [P, 4, P])
        loaded, turned, placed = ph.sem("loaded"), ph.sem("turned"), ph.sem("placed")
        with nc.Block() as block:
            @block.sync
            def _(sp):
                sp.dma_start(w_in[:, :, :], w.rearrange("(b p) n -> p b n", p=P)).then_inc(loaded, 16)

            @block.tensor
            def _(pe):
                pe.wait_ge(loaded, 16)
                for ob in range(2):
                    for ib in range(2):
                        nc.tensor.transpose(p_w[:, 2 * ob + ib, :], w_in[:, ob, ib * P:(ib + 1) * P], g.ident[:, :]).then_inc(turned, 1)

            @block.vector
            def _(dv):
                dv.wait_ge(turned, 4)
                for ob in range(2):
                    for ib in range(2):
                        nc.vector.tensor_copy(g.wt[:, ib, ob * P:(ob + 1) * P], p_w[:, 2 * ob + ib, :]).then_inc(placed, 1)
                dv.wait_ge(placed, 4)


def tile_of(t, i, n):
    return t[:, bass.ds(i, 1), 0:n].rearrange("p a d -> p (a d)")


def x_plus_product(nc, g, name, rhs, bias=None):
    layernorm_stats(nc, g)
    with Phase(nc, name) as ph:
        prod = Products(nc, g, ph, 2, P, D, True)
        wide = ph.sb("wide", [P, D])
        loaded, biased = ph.sem("loaded"), ph.sem("biased")
        with nc.Block() as block:
            @block.sync
            def _(sp):
                if bias is not None:
                    sp.dma_start(wide[:, :], bias.rearrange("(o n) -> o n", o=1).to_broadcast([P, D])).then_inc(loaded, 16)

            @block.scalar
            def _(ac):
                prod.scalar(ac)

            @block.tensor
            def _(pe):
                prod.tensor(pe, rhs)

            @block.vector
            def _(dv):
                nc.vector.sem_inc(prod.taken, 2)
                if bias is not None:
                    dv.wait_ge(loaded, 16)

                def take(i, s):
                    x = tile_of(g.x, i, D)
                    dv.wait_ge(prod.multiplied, i + 3)
                    nc.vector.tensor_tensor(x, x, prod.out[s][:, :], ALU.add).then_inc(prod.taken, 1)
                    if bias is not None:
                        dv.wait_ge(prod.taken, i + 3)
                        nc.vector.tensor_tensor(x, x, wide[:, :], ALU.add).then_inc(biased, 1)
                by_two(dv, NT, take)


def ln_rows(nc, g, name, table=None):
    layernorm_stats(nc, g)
    with Phase(nc, name) as ph:
        row = ph.sb("row", [P, 2, D])
        made, added = ph.sem("made"), ph.sem("added")
        stored = [ph.sem(f"stored{s}") for s in range(2)]
        with nc.Block() as block:
            @block.scalar
            def _(ac):
                for s in range(2):
                    normalised(nc, g, row[:, s, :], s).then_inc(made, 1)
                with ac.Fori(1, NT // 2) as i:
                    for s in range(2):
                        if table is not None:
                            ac.wait_ge(stored[s], 16 * i)
                        else:
                            ac.wait_ge(added, 2 * i + s - 1)
                        ac.nop(nofuse=True)
                        normalised(nc, g, row[:, s, :], 2 * i + s).then_inc(made, 1)
                if table is not None:
                    ac.wait_ge(stored[0], 16 * (NT // 2))
                else:
                    ac.wait_ge(added, NT - 2)
                normalised(nc, g, row[:, 0, :], NT - 1).then_inc(made, 1)

            @block.sync
            def _(sp):
                if table is not None:
                    def store(i, s):
                        sp.wait_ge(made, i + 1)
                        sp.dma_start(table[bass.ds(i * P, P), :], row[:, s, :]).then_inc(stored[s], 16)
                    by_two(sp, NT, store)
                    sp.wait_ge(stored[0], 16 * (NT // 2 + 1))
                    sp.wait_ge(stored[1], 16 * (NT // 2))

            @block.vector
            def _(dv):
                if table is None:
                    def add(i, s):
                        dv.wait_ge(made, i + 1)
                        nc.vector.tensor_tensor(tile_of(g.agg, i, D), tile_of(g.agg, i, D), row[:, s, :], ALU.add).then_inc(added, 1)
                    by_two(dv, NT, add)


def agg_product(nc, g, name, rhs):
    with Phase(nc, name) as ph:
        prod = Products(nc, g, ph, 2, P, D, False)
        with nc.Block() as block:
            @block.scalar
            def _(ac):
                prod.scalar(ac)

            @block.tensor
            def _(pe):
                prod.tensor(pe, rhs)

            @block.vector
            def _(dv):
                nc.vector.sem_inc(prod.taken, 2)

                def take(i, s):
                    dv.wait_ge(prod.multiplied, i + 3)
                    nc.vector.tensor_copy(tile_of(g.agg, i, D), prod.out[s][:, :]).then_inc(prod.taken, 1)
                by_two(dv, NT, take)


def batch_norm(nc, g, name, cols, bias, gamma, beta, into_x, elu=False, gcn=False):
    EPS = 1e-5
    with Phase(nc, name) as ph:
        wide = ph.sb("wide", [P, 3, cols])
        mean, scale, eps = ph.sb("mean", [P, cols]), ph.sb("scale", [P, cols]), ph.sb("eps", [P, 1])
        sq = ph.sb("sq", [P, 2, cols])
        y = ph.sb("y", [P, 2, cols])
        low = ph.sb("low", [P, 2, cols])
        p_m, p_v = ph.ps("p_m", [P, cols]), ph.ps("p_v", [P, cols])
        loaded, ops, biased, summed, less, squared, pre, var_done, rooted, done, lows, exped = (
            ph.sem(n) for n in ("loaded", "ops", "biased", "summed", "less", "squared", "pre", "var_done", "rooted", "done", "lows", "exped"))
        steps_per = 3 if gcn else 1

        def rows(i):
            return LAST if isinstance(i, int) and i == NT - 1 else P
        with nc.Block() as block:
            @block.sync
            def _(sp):
                for n, v in enumerate((bias, gamma, beta)):
                    sp.dma_start(wide[:, n, :], v.rearrange("(o n) -> o n", o=1).to_broadcast([P, cols])).then_inc(loaded, 16)

            @block.tensor
            def _(pe):
                def add_up(out, src, i, sem, k):
                    nc.tensor.matmul(out[:, :], g.ones[0:k, :], src, start=False, stop=False, skip_group_check=True).then_inc(sem, 1)
                pe.wait_ge(ops, 1)
                nc.tensor.matmul(p_m[:, :], g.ones[:, :], mean[:, :], start=True, stop=False, skip_group_check=True)
                nc.tensor.matmul(p_v[:, :], g.ones[:, :], mean[:, :], start=True, stop=False, skip_group_check=True).then_inc(summed, 1)

                def mean_of(i, s):
                    pe.wait_ge(biased, steps_per * (i + 1))
                    k = rows(i)
                    add_up(p_m, tile_of(g.agg, i, cols)[0:k, :], i, summed, k)
                by_two(pe, NT, mean_of)

                def var_of(i, s):
                    pe.wait_ge(squared, i + 1)
                    k = rows(i)
                    add_up(p_v, sq[0:k, s, :], i, var_done, k)
                by_two(pe, NT, var_of)

            @block.scalar
            def _(ac):
                for s in range(2):
                    ac.wait_ge(less, s + 1)
                    nc.scalar.activation(sq[:, s, :], tile_of(g.agg, s, cols), ACT.Square).then_inc(squared, 1)
                with ac.Fori(1, NT // 2) as i:
                    for s in range(2):
                        ac.wait_ge(less, 2 * i + s + 1)
                        ac.wait_ge(var_done, 2 * i + s - 1)
                        ac.nop(nofuse=True)
                        nc.scalar.activation(sq[:, s, :], tile_of(g.agg, 2 * i + s, cols), ACT.Square).then_inc(squared, 1)
                ac.wait_ge(less, NT)
                ac.wait_ge(var_done, NT - 2)
                nc.scalar.activation(sq[:, 0, :], tile_of(g.agg, NT - 1, cols), ACT.Square).then_inc(squared, 1)
                ac.wait_ge(var_done, NT)
                nc.scalar.activation(scale[:, :], p_v[:, :], ACT.Sqrt, scale=1.0 / N_NODES, bias=eps[:, 0:1]).then_inc(rooted, 1)
                if elu:
                    def exp(i, s):
                        ac.wait_ge(lows, i + 1)
                        nc.scalar.activation(low[:, s, :], low[:, s, :], ACT.Exp).then_inc(exped, 1)
                    by_two(ac, NT, exp)

            @block.vector
            def _(dv):
                ch = Chain(dv, ops)
                ch.do(nc.vector.memset(mean[:, :], 0.0))
                dv.wait_ge(loaded, 48)

                def bias_in(i, s):
                    h = tile_of(g.agg, i, cols)
                    n = Chain(dv, biased, steps_per * i)
                    if gcn:
                        own = g.agg[:, bass.ds(i, 1), cols:2 * cols].rearrange("p a d -> p (a d)")
                        n.do(nc.vector.tensor_tensor(h, h, own, ALU.add))
                        n.do(nc.vector.scalar_tensor_tensor(out=h, in0=h, scalar=g.dinv[:, bass.ds(i, 1)], in1=wide[:, 0, :], op0=ALU.mult, op1=ALU.add))
                        n.do(nc.vector.tensor_scalar(h, h, 0.0, None, ALU.max))
                    else:
                        n.do(nc.vector.tensor_tensor(h, h, wide[:, 0, :], ALU.add))
                by_two(dv, NT, bias_in)
                dv.wait_ge(summed, NT + 1)
                ch.do(nc.vector.tensor_scalar(mean[:, :], p_m[:, :], 1.0 / N_NODES, None, ALU.mult))
                ch.do(nc.vector.memset(eps[:, :], EPS))

                def center(i, s):
                    h = tile_of(g.agg, i, cols)
                    nc.vector.tensor_tensor(h, h, mean[:, :], ALU.subtract).then_inc(less, 1)
                by_two(dv, NT, center)
                dv.wait_ge(rooted, 1)
                ch.do(nc.vector.reciprocal(mean[:, :], scale[:, :]))
                ch.do(nc.vector.tensor_tensor(scale[:, :], mean[:, :], wide[:, 1, :], ALU.mult))

                def apply(i, s):
                    h = tile_of(g.agg, i, cols)
                    n = Chain(dv, done, n_apply * i)
                    out = h if not into_x else y[:, s, :]
                    n.do(nc.vector.tensor_tensor(out, h, scale[:, :], ALU.mult))
                    n.do(nc.vector.tensor_tensor(out, out, wide[:, 2, :], ALU.add))
                    if elu:
                        nc.vector.tensor_scalar(low[:, s, :], out, 0.0, None, ALU.min).then_inc(lows, 1)
                        n.do(nc.vector.tensor_scalar(out, out, 0.0, -1.0, ALU.max, ALU.add))
                        dv.wait_ge(exped, i + 1)
                        n.do(nc.vector.tensor_tensor(out, out, low[:, s, :], ALU.add))
                    if into_x:
                        x = tile_of(g.x, i, cols)
                        n.do(nc.vector.tensor_tensor(x, x, out, ALU.add))
                n_apply = 2 + 2 * elu + into_x
                by_two(dv, NT, apply)


def gcn_table(nc, g, name, w):
    layernorm_stats(nc, g)
    F = 64
    with Phase(nc, name) as ph:
        prod = Products(nc, g, ph, 2, P, F, True)
        wsb = ph.sb("wsb", [P, 2, F])
        std = ph.sb("std", [P, NT])
        row = ph.sb("row", [P, 2, F])
        loaded, ops, rooted = ph.sem("loaded"), ph.sem("ops"), ph.sem("rooted")
        stored = [ph.sem(f"stored{s}") for s in range(2)]
        with nc.Block() as block:
            @block.sync
            def _(sp):
                sp.dma_start(wsb[:, :, :], w.rearrange("(b p) n -> p b n", p=P)).then_inc(loaded, 16)

                def store(i, s):
                    sp.wait_ge(prod.taken, i + 3)
                    sp.dma_start(g.table64[bass.ds(i * P, P), :], g.agg[:, bass.ds(i, 1), F:2 * F].rearrange("p a d -> p (a d)")).then_inc(stored[s], 16)
                by_two(sp, NT, store)
                sp.wait_ge(stored[0], 16 * (NT // 2 + 1))
                sp.wait_ge(stored[1], 16 * (NT // 2))

            @block.scalar
            def _(ac):
                nc.scalar.activation(std[:, :], g.deg[:, :], ACT.Sqrt, bias=g.ones[:, 0:1]).then_inc(rooted, 1)
                prod.scalar(ac)

            @block.tensor
            def _(pe):
                pe.wait_ge(loaded, 16)
                prod.tensor(pe, wsb)

            @block.vector
            def _(dv):
                dv.wait_ge(rooted, 1)
                nc.vector.reciprocal(g.dinv[:, :], std[:, :]).then_inc(ops, 1)
                dv.wait_ge(ops, 1)
                nc.vector.sem_inc(prod.taken, 2)

                def take(i, s):
                    dv.wait_ge(prod.multiplied, i + 3)
                    nc.vector.tensor_scalar(g.agg[:, bass.ds(i, 1), F:2 * F].rearrange("p a d -> p (a d)"), prod.out[s][:, :],
                                            g.dinv[:, bass.ds(i, 1)], None, ALU.mult).then_inc(prod.taken, 1)
                by_two(dv, NT, take)


def setup3(nc, g):
    sb = lambda n, s, d=F32: nc.keep.enter_context(nc.sbuf_tensor(n, s, d))
    dr = lambda n, s, d=F32: nc.dram_tensor(n, s, d, kind="Internal").ap()
    g.wt = sb("wt", [P, 2, D])
    g.dinv = sb("dinv", [P, NT])
    g.table64 = dr("table64", [NP, 64])
    g.rows256 = dr("rows256", [NP, D])
    g.table4 = dr("table4", [NP, D + 4])


def l3_gnn(nc, g, p):
    gcn_table(nc, g, "gcn", p["W_gcn"])
    gather_pass(nc, g, "gcnp", g.table64, 64)
    batch_norm(nc, g, "bn0", 64, p["b_gcn"], p["g0"], p["beta0"], False, gcn=True)
    gat_table(nc, g, "t2", p["W1"], p["a_src1"], p["a_dst1"], 4, 64, False, g.table4, g.inject4, False)
    gather_pass(nc, g, "g2", g.table4, D, 4, g.inject4)
    gat_finish(nc, g, "f2", g.table4, 4, 0.0)
    batch_norm(nc, g, "bn1", D, p["b1"], p["g1"], p["beta1"], False, elu=True)
    gat_table(nc, g, "t3", p["W2"], p["a_src2"], p["a_dst2"], 4, D, False, g.table4, g.inject4, False)
    gather_pass(nc, g, "g3", g.table4, D, 4, g.inject4)
    gat_finish(nc, g, "f3", g.table4, 4, 0.0)
    batch_norm(nc, g, "bn2", D, p["b2"], p["g2"], p["beta2"], True, elu=True)

E = 8
CAP = 977
ROOM = 1024
TILES = (2 * N_NODES + E * (P - 1)) // P
SLOTS = TILES * P
OUT = 1000000.0
assert CAP == -(-5 * N_NODES // (4 * E)) and TILES % 2 == 1


def pipeline(eng, n, stages):
    leads = [k for k, _ in stages]
    a, b = -min(leads), n - max(leads)
    pairs = (b - a) // 2

    def step(t):
        for lead, f in stages:
            if 0 <= t + lead < n:
                f(t + lead, (t + lead) % 2)
    for t in range(-max(leads), a):
        step(t)
    with eng.Fori(0, pairs) as r:
        for u in range(2):
            for lead, f in stages:
                f(2 * r + (a + u + lead), (a + u + lead) % 2)
    for t in range(a + 2 * pairs, n - min(leads)):
        step(t)


def two_slots(eng, n, wait_free, body):
    body(0, 0)
    body(1, 1)
    with eng.Fori(1, n // 2) as i:
        for s in range(2):
            wait_free(i, s)
            body(2 * i + s, s)
    if n % 2:
        wait_free(n // 2, 0)
        body(n - 1, 0)


def route(nc, g, name, w, bias, top2, softmax):
    layernorm_stats(nc, g)
    with Phase(nc, name) as ph:
        prod = Products(nc, g, ph, 2, P, E, True)
        wsb, gb = ph.sb("wsb", [P, 2, E]), ph.sb("gb", [P, E])
        big = lambda n: ph.sb(n, [P, E, NT])
        score, first, second, both, eq, tmp, pos, place, later = (
            big(n) for n in ("score", "first", "second", "both", "eq", "tmp", "pos", "place", "later"))
        small = lambda n: ph.sb(n, [P, NT])
        best, best2, left, valid, slot, kept = (small(n) for n in ("best", "best2", "left", "valid", "slot", "kept"))
        node, node_i, tri = small("node"), ph.sb("node_i", [P, NT], I32), ph.sb("tri", [P, P])
        count_i, tiles, bases, base = ph.sb("count_i", [P, E], I32), ph.sb("tiles", [P, E]), ph.sb("bases", [P, E]), ph.sb("base", [P, E])
        at, te = ph.sb("at", [1, 2, TILES]), ph.sb("te", [1, TILES])
        at_i = ph.sb("at_i", [1, TILES], I32)
        p_in, p_tot = ph.ps("p_in", [P, E * NT]), ph.ps("p_tot", [P, E * NT])
        loaded, seq, tri_ready, ops, counted, exped = (ph.sem(n) for n in ("loaded", "seq", "tri_ready", "ops", "counted", "exped"))
        marks, marks_pe = [], []
        by_node = lambda t: t[:, :, :].rearrange("p e t -> p t e")
        flat = lambda t: t[:, :, :].rearrange("p e t -> p (e t)")
        with nc.Block() as block:
            @block.sync
            def _(sp):
                sp.dma_start(wsb[:, :, :], w.rearrange("(b p) n -> p b n", p=P)).then_inc(loaded, 16)
                sp.dma_start(gb[:, :], bias.rearrange("(o n) -> o n", o=1).to_broadcast([P, E])).then_inc(loaded, 16)

            @block.gpsimd
            def _(gp):
                nc.gpsimd.iota(node_i[:, :], [[P, NT]], base=0, channel_multiplier=1).then_inc(seq, 1)
                nc.gpsimd.iota(at_i[:, :], [[1, TILES]], base=0, channel_multiplier=0).then_inc(seq, 1)
                nc.gpsimd.memset(tri[:, :], 0.0).then_inc(tri_ready, 1)
                gp.wait_ge(tri_ready, 1)
                nc.gpsimd.affine_select(out=tri[:, :], in_=tri[:, :], compare_op=ALU.is_ge, fill=1.0,
                                        base=0, pattern=[[-1, P]], channel_multiplier=1).then_inc(tri_ready, 1)

            @block.scalar
            def _(ac):
                prod.scalar(ac)

            @block.tensor
            def _(pe):
                pe.wait_ge(loaded, 32)
                prod.tensor(pe, wsb)

            @block.vector
            def _(dv):
                dv.wait_ge(loaded, 32)
                nc.vector.sem_inc(prod.taken, 2)

                def take(i, s):
                    dv.wait_ge(prod.multiplied, i + 3)
                    nc.vector.tensor_tensor(score[:, :, bass.ds(i, 1)].rearrange("p e a -> p (e a)"), prod.out[s][:, :], gb[:, :], ALU.add).then_inc(prod.taken, 1)
                by_two(dv, NT, take)
                dv.wait_ge(prod.taken, NT + 2)

        with nc.Block() as block:
            @block.vector
            def _(dv):
                ch = Chain(dv, ops)
                V = nc.vector

                def pick(out, scores, peak):
                    ch.do(V.tensor_reduce(out=peak[:, :], in_=by_node(scores), axis=AX.X, op=ALU.max))
                    ch.do(V.tensor_tensor(eq[:, :, :], scores[:, :, :], peak[:, :].unsqueeze(1).to_broadcast([P, E, NT]), ALU.is_equal))
                    ch.do(V.tensor_copy(left[:, :], valid[:, :]))
                    for e in range(E):
                        ch.do(V.tensor_tensor(out[:, e, :], eq[:, e, :], left[:, :], ALU.mult))
                        if e < E - 1:
                            ch.do(V.tensor_tensor(left[:, :], left[:, :], out[:, e, :], ALU.subtract))

                def chosen(out, mask, values):
                    ch.do(V.tensor_tensor(tmp[:, :, :], mask[:, :, :], values[:, :, :], ALU.mult))
                    ch.do(V.tensor_reduce(out=out[:, :], in_=by_node(tmp), axis=AX.X, op=ALU.add))
                dv.wait_ge(seq, 2)
                ch.do(V.tensor_copy(node[:, :], node_i[:, :]))
                ch.do(V.tensor_copy(at[0:1, 0, :], at_i[0:1, :]))
                ch.do(V.tensor_scalar(valid[:, :], node[:, :], float(N_NODES), None, ALU.is_lt))
                pick(first, score, best)
                if softmax:
                    ch.do(V.tensor_tensor(tmp[:, :, :], score[:, :, :], best[:, :].unsqueeze(1).to_broadcast([P, E, NT]), ALU.subtract))
                    marks.append(ch.n)
                    dv.wait_ge(exped, 1)
                    ch.do(V.tensor_reduce(out=slot[:, :], in_=by_node(eq), axis=AX.X, op=ALU.add))
                    ch.do(V.reciprocal(g.weight1[:, :], slot[:, :]))
                else:
                    ch.do(V.memset(g.weight1[:, :], 1.0))
                    ch.do(V.memset(g.weight2[:, :], 1.0))
                if top2:
                    ch.do(V.scalar_tensor_tensor(out=later[:, :, :], in0=first[:, :, :], scalar=-BIG, in1=score[:, :, :], op0=ALU.mult, op1=ALU.add))
                    pick(second, later, best2)
                    ch.do(V.tensor_tensor(both[:, :, :], first[:, :, :], second[:, :, :], ALU.add))
                    if softmax:
                        ch.do(V.tensor_tensor(kept[:, :], best2[:, :], best[:, :], ALU.subtract))
                        marks.append(ch.n)
                        dv.wait_ge(exped, 2)
                        ch.do(V.tensor_tensor(g.weight2[:, :], slot[:, :], g.weight1[:, :], ALU.mult))
                else:
                    ch.do(V.tensor_copy(both[:, :, :], first[:, :, :]))
                marks_pe.append(ch.n)
                dv.wait_ge(counted, 2)
                ch.do(V.memset(eq[:, :, :], 1.0))
                ch.do(V.memset(eq[:, :, 0:1], 0.0))
                ch.do(V.tensor_copy(tmp[:, :, :].rearrange("p e t -> p (e t)"), p_tot[:, :]))
                ch.do(V.tensor_tensor_scan(flat(later), flat(eq), flat(tmp), 0.0, ALU.mult, ALU.add))
                ch.do(V.tensor_tensor(flat(pos), flat(later), p_tot[:, :], ALU.subtract))
                ch.do(V.tensor_tensor(flat(pos), flat(pos), p_in[:, :], ALU.add))
                if top2:
                    ch.do(V.tensor_scalar(tiles[:, :], later[:, :, NT - 1], float(P - 1), None, ALU.add))
                    ch.do(V.tensor_copy(count_i[:, :], tiles[:, :]))
                    ch.do(V.tensor_scalar(count_i[:, :], count_i[:, :], 7, None, ALU.arith_shift_right))
                    ch.do(V.tensor_copy(tiles[:, :], count_i[:, :]))
                    ch.do(V.tensor_tensor_scan(bases[:, :], tiles[:, :], tiles[:, :], 0.0, ALU.add, ALU.bypass))
                    ch.do(V.tensor_tensor(bases[:, :], bases[:, :], tiles[:, :], ALU.subtract))
                    ch.do(V.tensor_scalar(base[:, :], bases[:, :], float(P), None, ALU.mult))
                    ch.do(V.tensor_tensor(place[:, :, :], pos[:, :, :], base[:, :].unsqueeze(2).to_broadcast([P, E, NT]), ALU.add))
                    ch.do(V.memset(te[:, :], 0.0))
                    for e in range(1, E):
                        ch.do(V.tensor_scalar(at[0:1, 1, :], at[0:1, 0, :], bases[0:1, e:e + 1], None, ALU.is_ge))
                        ch.do(V.tensor_tensor(te[:, :], te[:, :], at[0:1, 1, :], ALU.add))
                    ch.do(V.tensor_copy(g.tile_expert[:, :], te[:, :]))
                else:
                    for e in range(E):
                        ch.do(V.tensor_scalar(place[:, e, :], pos[:, e, :], float(CAP - 1), float(e * ROOM), ALU.min, ALU.add))
                    ch.do(V.tensor_scalar(eq[:, :, :], pos[:, :, :], float(CAP), None, ALU.is_lt))
                for mask, put, get in ((first, g.put1, g.get1), (second, g.put2, g.get2))[:1 + top2]:
                    chosen(slot, mask, place)
                    if top2:
                        ch.do(V.tensor_copy(kept[:, :], valid[:, :]))
                    else:
                        chosen(kept, mask, eq)
                        ch.do(V.tensor_tensor(g.weight1[:, :], g.weight1[:, :], kept[:, :], ALU.mult))
                    ch.do(V.tensor_copy(get[:, :], slot[:, :]))
                    ch.do(V.tensor_scalar(kept[:, :], kept[:, :], -OUT, OUT, ALU.mult, ALU.add))
                    ch.do(V.tensor_tensor(slot[:, :], slot[:, :], kept[:, :], ALU.add))
                    ch.do(V.tensor_copy(put[:, :], slot[:, :]))

            @block.scalar
            def _(ac):
                if softmax:
                    ac.wait_ge(ops, marks[0])
                    nc.scalar.activation(eq[:, :, :], tmp[:, :, :], ACT.Exp).then_inc(exped, 1)
                    if top2:
                        ac.wait_ge(ops, marks[1])
                        nc.scalar.activation(slot[:, :], kept[:, :], ACT.Exp).then_inc(exped, 1)

            @block.tensor
            def _(pe):
                pe.wait_ge(tri_ready, 2)
                pe.wait_ge(ops, marks_pe[0])
                nc.tensor.matmul(p_in[:, :], tri[:, :], flat(both), start=True, stop=True).then_inc(counted, 1)
                nc.tensor.matmul(p_tot[:, :], g.ones[:, :], flat(both), start=True, stop=True).then_inc(counted, 1)


def dispatch(nc, g, name, puts):
    with Phase(nc, name) as ph:
        row = ph.sb("row", [P, 2, D])
        idx = ph.sb("idx", [P, 2, 2], I32)
        made, placed = ph.sem("made"), ph.sem("placed")
        scattered = [ph.sem(f"scattered{s}") for s in range(2)]
        K = len(puts)
        with nc.Block() as block:
            @block.scalar
            def _(ac):
                def free(uses, s):
                    ac.wait_ge(scattered[s], 16 * K * uses)
                    ac.nop(nofuse=True)
                two_slots(ac, NT, free, lambda i, s: normalised(nc, g, row[:, s, :], i).then_inc(made, 1))

            @block.gpsimd
            def _(gp):
                def free(uses, s):
                    gp.wait_ge(scattered[s], 16 * K * uses)

                def scatter(i, s):
                    for k, put in enumerate(puts):
                        nc.gpsimd.tensor_copy(idx[:, s, k:k + 1], put[:, bass.ds(i, 1)]).then_inc(placed, 1)
                    gp.wait_ge(placed, K * (i + 1))
                    gp.wait_ge(made, i + 1)
                    gp.nop(nofuse=True)
                    for k in range(K):
                        gp.indirect_dma_start(g.expert_rows, bass.IndirectOffsetOnAxis(idx[:, s, k:k + 1], 0), row[:, s, :], None,
                                              bounds_check=SLOTS - 1, oob_is_err=False).then_inc(scattered[s], 16)
                two_slots(gp, NT, free, scatter)
                gp.wait_ge(scattered[0], 16 * K * (NT // 2 + 1))
                gp.wait_ge(scattered[1], 16 * K * (NT // 2))


def experts_by_room(nc, g, name, w1, b1, w2, b2):
    F = w1.shape[2]
    HB, RT = F // P, ROOM // P
    NH = ROOM // 512
    with Phase(nc, name) as ph:
        w1s, w2s = ph.sb("w1s", [P, 2, 2, F]), ph.sb("w2s", [P, 2, HB, D])
        b1s, b2s = ph.sb("b1s", [P, 2, HB]), ph.sb("b2s", [P, 2, D])
        xin = ph.sb("xin", [P, RT, D])
        spare = g.agg[:, :, :].rearrange("p t w -> p (t w)")
        ht = spare[:, 0:HB * ROOM].rearrange("p (b r) -> p b r", b=HB)
        xt = spare[:, HB * ROOM:HB * ROOM + 2 * ROOM].rearrange("p (k r) -> p k r", k=2)
        b1r = ph.sb("b1r", [E * HB, P])
        b1t = ph.sb("b1t", [P, E * HB])
        y = ph.sb("y", [P, 2, D])
        p_x = [ph.ps(f"p_x{s}", [P, 2, P]) for s in range(2)]
        p_h = [ph.ps(f"p_h{s}", [P, 512]) for s in range(2)]
        p_y = [ph.ps(f"p_y{s}", [P, D]) for s in range(2)]
        p_b = ph.ps("p_b", [P, E * HB])
        b_in, b_turned, b_ready = ph.sem("b_in"), ph.sem("b_turned"), ph.sem("b_ready")
        x_in = ph.sem("x_in")
        w_in = [ph.sem(f"w_in{s}") for s in range(2)]
        turned, copied, up, hidden, down, made = (ph.sem(n) for n in ("turned", "copied", "up", "hidden", "down", "made"))
        stored = [ph.sem(f"stored{s}") for s in range(2)]
        NU = HB * NH
        with nc.Block() as block:
            @block.sync
            def _(sp):
                sp.dma_start(b1r[:, :], b1.rearrange("e (b p) -> (e b) p", p=P)).then_inc(b_in, 16)

                def weights(e, s):
                    one = bass.ds(e, 1)
                    sp.dma_start(w1s[:, s, :, :], w1[one, :, :].rearrange("e (k p) f -> p (e k) f", p=P)).then_inc(w_in[s], 16)
                    sp.dma_start(w2s[:, s, :, :], w2[one, :, :].rearrange("e (b p) d -> p (e b) d", p=P)).then_inc(w_in[s], 16)
                    sp.dma_start(b2s[:, s, :], b2[one, :].to_broadcast([P, D])).then_inc(w_in[s], 16)

                def rows(e):
                    sp.dma_start(xin[:, :, :], g.expert_rows[bass.ds(e * ROOM, ROOM), :].rearrange("(t p) d -> p t d", p=P)).then_inc(x_in, 16)
                weights(0, 0)
                rows(0)
                weights(1, 1)

                def store(e, s):
                    for t in range(RT):
                        sp.wait_ge(made, e * RT + t + 3)
                        sp.dma_start(g.expert_out[bass.ds(e * ROOM + t * P, P), :], y[:, t % 2, :]).then_inc(stored[t % 2], 16)
                with sp.Fori(0, E // 2 - 1) as i:
                    for s in range(2):
                        e = 2 * i + s
                        sp.wait_ge(turned, RT * e + RT + 2)
                        rows(e + 1)
                        store(e, s)
                        sp.wait_ge(down, RT * e + RT + 2)
                        weights(e + 2, s)
                sp.wait_ge(turned, RT * (E - 1) + 2)
                rows(E - 1)
                store(E - 2, 0)
                store(E - 1, 1)
                for s in range(2):
                    sp.wait_ge(stored[s], 16 * E * RT // 2)

            @block.tensor
            def _(pe):
                nc.tensor.sem_inc(turned, 2)
                nc.tensor.sem_inc(up, 2)
                nc.tensor.sem_inc(down, 2)
                pe.wait_ge(b_in, 16)
                nc.tensor.transpose(p_b[:, :], b1r[:, :], g.ident[0:E * HB, 0:E * HB]).then_inc(b_turned, 1)

                def expert(e, s):
                    pe.wait_ge(x_in, 16 * (e + 1))
                    for t in range(RT):
                        pe.wait_ge(copied, RT * e + t + 1)
                        for k in range(2):
                            last = nc.tensor.transpose(p_x[t % 2][:, k, :], xin[:, t, k * P:(k + 1) * P], g.ident[:, :])
                        last.then_inc(turned, 1)
                    pe.wait_ge(copied, RT * e + RT + 2)
                    pe.wait_ge(w_in[s], 48 * ((e - s) // 2 + 1))
                    for b in range(HB):
                        for h in range(NH):
                            u = b * NH + h
                            pe.wait_ge(hidden, NU * e + u + 1)
                            for k in range(2):
                                last = nc.tensor.matmul(p_h[u % 2][:, :], w1s[:, s, k, b * P:(b + 1) * P], xt[:, k, h * 512:(h + 1) * 512], start=(k == 0), stop=(k == 1))
                            last.then_inc(up, 1)
                    for t in range(RT):
                        pe.wait_ge(hidden, NU * e + NU + 2)
                        pe.wait_ge(made, RT * e + t + 1)
                        for b in range(HB):
                            last = nc.tensor.matmul(p_y[t % 2][:, :], ht[:, b, t * P:(t + 1) * P], w2s[:, s, b, :], start=(b == 0), stop=(b == HB - 1))
                        last.then_inc(down, 1)
                by_two(pe, E, expert)

            @block.scalar
            def _(ac):
                nc.scalar.sem_inc(hidden, 2)
                ac.wait_ge(b_ready, 1)

                def expert(e, s):
                    ac.wait_ge(down, RT * e + 2)
                    for b in range(HB):
                        for h in range(NH):
                            u = b * NH + h
                            ac.wait_ge(up, NU * e + u + 3)
                            ac.nop(nofuse=True)
                            nc.scalar.activation(ht[:, b, h * 512:(h + 1) * 512], p_h[u % 2][:, :], ACT.Relu, bias=b1t[:, bass.ds(e * HB + b, 1)]).then_inc(hidden, 1)
                by_two(ac, E, expert)

            @block.vector
            def _(dv):
                nc.vector.sem_inc(copied, 2)
                nc.vector.sem_inc(made, 2)
                dv.wait_ge(b_turned, 1)
                nc.vector.tensor_copy(b1t[:, :], p_b[:, :]).then_inc(b_ready, 1)

                def expert(e, s):
                    dv.wait_ge(up, NU * e + 2)
                    for t in range(RT):
                        dv.wait_ge(turned, RT * e + t + 3)
                        nc.vector.tensor_copy(xt[:, :, t * P:(t + 1) * P], p_x[t % 2][:, :, :]).then_inc(copied, 1)
                    dv.wait_ge(w_in[s], 48 * ((e - s) // 2 + 1))
                    for t in range(RT):
                        dv.wait_ge(down, RT * e + t + 3)
                        if not (isinstance(e, int) and e == 0 and t < 2):
                            dv.wait_ge(stored[t % 2], 16 * (RT // 2 * e + t // 2))
                        nc.vector.tensor_tensor(y[:, t % 2, :], p_y[t % 2][:, :], b2s[:, s, :], ALU.add).then_inc(made, 1)
                expert(0, 0)
                with dv.Fori(0, E // 2 - 1) as i:
                    expert(2 * i + 1, 1)
                    expert(2 * i + 2, 0)
                expert(E - 1, 1)


def experts_by_tile(nc, g, name, w1, b1, w2, b2):
    F = w1.shape[2]
    HB = F // P
    with Phase(nc, name) as ph:
        spare = g.agg[:, :, :].rearrange("p t w -> p (t w)")
        w1s = spare[:, 0:E * 2 * F].rearrange("p (e k f) -> p e (k f)", e=E, k=2)
        b1s = spare[:, E * 2 * F:E * 3 * F].rearrange("p (e f) -> p e f", e=E)
        w2s, b2s = ph.sb("w2s", [P, E, HB * D]), ph.sb("b2s", [P, E, D])
        xin = ph.sb("xin", [P, 2, D])
        xt = ph.sb("xt", [P, 2, 2, P])
        hb, hg, ht = ph.sb("hb", [P, 2, F]), ph.sb("hg", [P, 2, F]), ph.sb("ht", [P, 2, HB, P])
        y = ph.sb("y", [P, 2, D])
        p_x = [ph.ps(f"p_x{s}", [P, 2, P]) for s in range(2)]
        p_h = [ph.ps(f"p_h{s}", [P, F]) for s in range(2)]
        p_t = [ph.ps(f"p_t{s}", [P, HB, P]) for s in range(2)]
        p_y = [ph.ps(f"p_y{s}", [P, D]) for s in range(2)]
        w_in = ph.sem("w_in")
        turned, copied, up, biased, curved, h_turned, h_copied, down, made = (
            ph.sem(n) for n in ("turned", "copied", "up", "biased", "curved", "h_turned", "h_copied", "down", "made"))
        x_in = [ph.sem(f"x_in{s}") for s in range(2)]
        stored = [ph.sem(f"stored{s}") for s in range(2)]
        uses = lambda i, s: 16 * ((i - s) // 2 + 1)
        expert_of = lambda eng, i: eng.value_load(g.tile_expert[0:1, bass.ds(i, 1)], min_val=0, max_val=E - 1)
        with nc.Block() as block:
            @block.sync
            def _(sp):
                def load(i, s):
                    sp.wait_ge(turned, i + 1)
                    sp.dma_start(xin[:, s, :], g.expert_rows[bass.ds(i * P, P), :]).then_inc(x_in[s], 16)

                def store(i, s):
                    sp.wait_ge(made, i + 3)
                    sp.dma_start(g.expert_out[bass.ds(i * P, P), :], y[:, s, :]).then_inc(stored[s], 16)
                pipeline(sp, TILES, [(2, load), (-1, store)])
                sp.wait_ge(stored[0], 16 * (TILES // 2 + 1))
                sp.wait_ge(stored[1], 16 * (TILES // 2))

            @block.gpsimd
            def _(gp):
                gp.dma_start(w1s.rearrange("p e (k f) -> p e k f", k=2), w1.rearrange("e (k p) f -> p e k f", p=P)).then_inc(w_in, 16)
                gp.dma_start(w2s[:, :, :].rearrange("p e (b d) -> p e b d", b=HB), w2.rearrange("e (b p) d -> p e b d", p=P)).then_inc(w_in, 16)
                gp.dma_start(b1s.rearrange("p e f -> p (e f)"), b1.rearrange("(o e) f -> o (e f)", o=1).to_broadcast([P, E * F])).then_inc(w_in, 16)
                gp.dma_start(b2s[:, :, :].rearrange("p e f -> p (e f)"), b2.rearrange("(o e) f -> o (e f)", o=1).to_broadcast([P, E * D])).then_inc(w_in, 16)
                gp.wait_ge(w_in, 64)

            @block.tensor
            def _(pe):
                for s in (turned, up, h_turned, down):
                    nc.tensor.sem_inc(s, 2)

                def turn(i, s):
                    pe.wait_ge(x_in[s], uses(i, s))
                    pe.wait_ge(copied, i + 1)
                    for k in range(2):
                        last = nc.tensor.transpose(p_x[s][:, k, :], xin[:, s, k * P:(k + 1) * P], g.ident[:, :])
                    last.then_inc(turned, 1)

                def first(i, s):
                    e = expert_of(pe, i)
                    pe.wait_ge(copied, i + 3)
                    pe.wait_ge(biased, i + 1)
                    for k in range(2):
                        last = nc.tensor.matmul(p_h[s][:, :], xt[:, s, k, :], w1s[:, bass.ds(e, 1), k * F:(k + 1) * F].rearrange("p a f -> p (a f)"), start=(k == 0), stop=(k == 1))
                    last.then_inc(up, 1)

                def turn_hidden(i, s):
                    pe.wait_ge(curved, i + 3)
                    pe.wait_ge(h_copied, i + 1)
                    for b in range(HB):
                        last = nc.tensor.transpose(p_t[s][:, b, :], hg[:, s, b * P:(b + 1) * P], g.ident[:, :])
                    last.then_inc(h_turned, 1)

                def second(i, s):
                    e = expert_of(pe, i)
                    pe.wait_ge(h_copied, i + 3)
                    pe.wait_ge(made, i + 1)
                    for b in range(HB):
                        last = nc.tensor.matmul(p_y[s][:, :], ht[:, s, b, :], w2s[:, bass.ds(e, 1), b * D:(b + 1) * D].rearrange("p a f -> p (a f)"), start=(b == 0), stop=(b == HB - 1))
                    last.then_inc(down, 1)
                pe.wait_ge(w_in, 64)
                pipeline(pe, TILES, [(2, turn), (1, first), (-1, second), (0, turn_hidden)])

            @block.scalar
            def _(ac):
                nc.scalar.sem_inc(copied, 2)
                nc.scalar.sem_inc(curved, 2)

                def copy(i, s):
                    ac.wait_ge(turned, i + 3)
                    ac.wait_ge(up, i + 1)
                    nc.scalar.activation(xt[:, s, :, :], p_x[s][:, :, :], ACT.Identity).then_inc(copied, 1)

                def curve(i, s):
                    ac.wait_ge(biased, i + 3)
                    ac.wait_ge(h_turned, i + 1)
                    nc.scalar.activation(hg[:, s, :], hb[:, s, :], ACT.Gelu).then_inc(curved, 1)
                pipeline(ac, TILES, [(2, copy), (1, curve)])

            @block.vector
            def _(dv):
                for s in (biased, h_copied, made):
                    nc.vector.sem_inc(s, 2)
                dv.wait_ge(w_in, 64)

                def bias(i, s):
                    e = expert_of(dv, i)
                    dv.wait_ge(up, i + 3)
                    dv.wait_ge(curved, i + 1)
                    nc.vector.tensor_tensor(hb[:, s, :], p_h[s][:, :], b1s[:, bass.ds(e, 1), :].rearrange("p a f -> p (a f)"), ALU.add).then_inc(biased, 1)

                def out(i, s):
                    e = expert_of(dv, i)
                    dv.wait_ge(down, i + 3)
                    if not (isinstance(i, int) and i < 2):
                        dv.wait_ge(stored[s], 16 * ((i - s) // 2))
                    nc.vector.tensor_tensor(y[:, s, :], p_y[s][:, :], b2s[:, bass.ds(e, 1), :].rearrange("p a f -> p (a f)"), ALU.add).then_inc(made, 1)

                def copy_hidden(i, s):
                    dv.wait_ge(h_turned, i + 3)
                    dv.wait_ge(down, i + 1)
                    nc.vector.tensor_copy(ht[:, s, :, :], p_t[s][:, :, :]).then_inc(h_copied, 1)
                bias(0, 0)
                for t in range(4):
                    bias(t + 1, (t + 1) % 2)
                    if t:
                        out(t - 1, (t - 1) % 2)
                    copy_hidden(t, t % 2)
                with dv.Fori(2, (TILES - 1) // 2) as r:
                    for u in range(2):
                        t = 2 * r + u
                        bias(t + 1, 1 - u)
                        out(t - 1, 1 - u)
                        copy_hidden(t, u)
                out(TILES - 2, 1)
                copy_hidden(TILES - 1, 0)
                out(TILES - 1, 0)


def combine(nc, g, name, gets, weights, guard):
    K = len(gets)
    with Phase(nc, name) as ph:
        row = ph.sb("row", [P, 2, K, D])
        idx = ph.sb("idx", [P, 2, K], I32)
        bad = ph.sb("bad", [P, D], I32)
        fill = ph.sb("fill", [P, 3, D])
        placed, used, ops, filled = ph.sem("placed"), ph.sem("used"), ph.sem("ops"), ph.sem("filled")
        got = [ph.sem(f"got{s}") for s in range(2)]
        MOST = float(np.finfo(np.float32).max)
        with nc.Block() as block:
            @block.gpsimd
            def _(gp):
                def gather(i, s):
                    gp.wait_ge(used, K * i + K)
                    for k, get in enumerate(gets):
                        nc.gpsimd.tensor_copy(idx[:, s, k:k + 1], get[:, bass.ds(i, 1)]).then_inc(placed, 1)
                    gp.wait_ge(placed, K * (i + 1))
                    gp.nop(nofuse=True)
                    for k in range(K):
                        gp.indirect_dma_start(row[:, s, k, :], None, g.expert_out, bass.IndirectOffsetOnAxis(idx[:, s, k:k + 1], 0)).then_inc(got[s], 16)
                by_two(gp, NT, gather)

            @block.vector
            def _(dv):
                fl = Chain(dv, filled)
                if guard:
                    for n, v in enumerate((0.0, 10000.0, -10000.0)):
                        fl.do(nc.vector.memset(fill[:, n, :], v))
                nc.vector.sem_inc(used, 2 * K)
                n_guard = 7

                def add(i, s):
                    x = tile_of(g.x, i, D)
                    dv.wait_ge(got[s], 16 * K * ((i - s) // 2 + 1))
                    if guard:
                        r = row[:, s, 0, :]
                        n = Chain(dv, ops, n_guard * i)
                        n.do(nc.vector.tensor_scalar(r, r, weights[0][:, bass.ds(i, 1)], None, ALU.mult))
                        for k, (against, op) in enumerate(((r, ALU.not_equal), (MOST, ALU.is_gt), (-MOST, ALU.is_lt))):
                            if k == 0:
                                n.do(nc.vector.tensor_tensor(bad[:, :], r, against, op))
                            else:
                                n.do(nc.vector.tensor_scalar(bad[:, :], r, against, None, op))
                            dv.nop(nofuse=True)
                            n.do(nc.vector.copy_predicated(r, bad[:, :], fill[:, k, :]))
                        nc.vector.tensor_tensor(x, x, r, ALU.add).then_inc(used, 1)
                    else:
                        for k in range(K):
                            nc.vector.scalar_tensor_tensor(out=x, in0=row[:, s, k, :], scalar=weights[k][:, bass.ds(i, 1)], in1=x, op0=ALU.mult, op1=ALU.add).then_inc(used, 1)
                            dv.wait_ge(used, K * i + k + 1 + 2 * K)
                by_two(dv, NT, add)


def setup4(nc, g):
    sb = lambda n, s, d=F32: nc.keep.enter_context(nc.sbuf_tensor(n, s, d))
    dr = lambda n, s, d=F32: nc.dram_tensor(n, s, d, kind="Internal").ap()
    g.put1, g.put2, g.get1, g.get2 = (sb(n, [P, NT], I32) for n in ("put1", "put2", "get1", "get2"))
    g.weight1, g.weight2 = sb("weight1", [P, NT]), sb("weight2", [P, NT])
    g.tile_expert = sb("tile_expert", [1, TILES], I32)
    g.expert_rows, g.expert_out = dr("expert_rows", [SLOTS, D]), dr("expert_out", [SLOTS, D])


def clear_rows(nc, g):
    with Phase(nc, "clear") as ph:
        cleared, zeroed = ph.sem("cleared"), ph.sem("zeroed")
        z = g.agg[:, :, :].rearrange("p t w -> p (t w)")[:, 0:15 * D]
        with nc.Block() as block:
            @block.vector
            def _(dv):
                nc.vector.memset(z, 0.0).then_inc(zeroed, 1)

            @block.sync
            def _(sp):
                sp.wait_ge(zeroed, 1)
                for rows in (g.expert_rows, g.expert_out):
                    v = rows.rearrange("(p r) d -> p (r d)", p=P)
                    for q in range(TILES // 15):
                        sp.dma_start(v[:, q * 15 * D:(q + 1) * 15 * D], z).then_inc(cleared, 16)
                sp.wait_ge(cleared, 2 * 16 * (TILES // 15))


def l0_ffn(nc, g, a):
    route(nc, g, "r0", a["L0_ffn_gate_w"], a["L0_ffn_gate_b"], False, True)
    dispatch(nc, g, "d0", [g.put1])
    experts_by_room(nc, g, "e0", a["L0_ffn_w1"], a["L0_ffn_b1"], a["L0_ffn_w2"], a["L0_ffn_b2"])
    combine(nc, g, "c0", [g.get1], [g.weight1], True)


def top2_ffn(nc, g, gw, gb, w1, b1, w2, b2, softmax):
    route(nc, g, "r2", gw, gb, True, softmax)
    dispatch(nc, g, "d2", [g.put1, g.put2])
    experts_by_tile(nc, g, "e2", w1, b1, w2, b2)
    combine(nc, g, "c2", [g.get1, g.get2], [g.weight1, g.weight2], False)

TP = EP // P
QC = 512
NQ = EP // QC
LISTED = 8
ALPHA, BETA, COS, SIN, READ, WRITE, ROW, LATE = range(LISTED)
NONE = 512.0
TWO_PI = 6.283185307179586
TWO_PI_HI = 6.28125
ROUND = 12582912.0


def rotation_list(nc, g):
    with Phase(nc, "list") as ph:
        src_i, dst_i, w = ph.sb("src_i", [P, TP], I32), ph.sb("dst_i", [P, TP], I32), ph.sb("w", [P, TP])
        spare = g.agg[:, :, :].rearrange("p t w -> p (t w)").rearrange("p (k t) -> p k t", t=TP)
        rec = g.agg[:, :, :].rearrange("p t w -> p (t w)")[:, 0:TP * LISTED].rearrange("p (t f) -> p t f", f=LISTED)
        turns, half, early, inside, event, late, psn, d1, pc = (spare[:, LISTED + k, :] for k in range(9))
        srcf, dstf, cos, sin, listed, tmp, tmp2, reset = (
            ph.sb(n, [P, TP]) for n in ("srcf", "dstf", "cos", "sin", "listed", "tmp", "tmp2", "reset"))
        back_i, back, first_i, firstf = ph.sb("back_i", [P, TP], I32), ph.sb("back", [P, TP]), ph.sb("first_i", [P, 1], I32), ph.sb("firstf", [P, 1])
        keys = ph.sb("keys", [P, TP + 16])
        rank_i, rank, key8 = ph.sb("rank_i", [P, TP + 16], I32), ph.sb("rank", [P, TP + 16]), ph.sb("key8", [P, 8])
        edge, place = ph.sb("edge", [P, TP + 16], I32), ph.sb("place", [P, TP + 16], I32)
        counts = ph.sb("counts", [P, 2])
        base = ph.sb("base", [P, 1])
        most = ph.sb("most", [1, 3])
        tri = ph.sb("tri", [P, P])
        fill = ph.sb("fill", [P, TP * LISTED // 4])
        got = ph.sb("got", [P, 2, 8, LISTED])
        ids, tos = ph.sb("ids", [P, 2, 8], I32), ph.sb("tos", [P, 2, 8], I32)
        p_cnt = ph.ps("p_cnt", [1, P])
        p_tot = ph.ps("p_tot", [P, 2])
        p_base = ph.ps("p_base", [P, 1])
        blank, din, seq, ops, waves, squared, tri_ready, summed, stored, chunks = (
            ph.sem(n) for n in ("blank", "din", "seq", "ops", "waves", "squared", "tri_ready", "summed", "stored", "chunks"))
        set_up, copied = ph.sem("set_up"), ph.sem("copied")
        fetched = [ph.sem(f"fetched{s}") for s in range(2)]
        placed = [ph.sem(f"placed{s}") for s in range(2)]
        fill_ready = ph.sem("fill_ready")
        mark = {}
        last = N_EDGES - (P - 1) * TP
        with nc.Block() as block:
            @block.sync
            def _(sp):
                sp.wait_ge(blank, 3)
                for dram, t in ((g.src_dram, src_i), (g.dst_dram, dst_i), (g.w_dram, w)):
                    sp.dma_start(t[0:P - 1, :], dram_view(dram, 0, [[TP, P - 1], [1, TP]])).then_inc(din, 16)
                    sp.dma_start(t[P - 1:P, 0:last], dram_view(dram, (P - 1) * TP, [[TP, 1], [1, last]])).then_inc(din, 16)
                sp.wait_ge(fill_ready, 1)
                n = TP * LISTED // 4
                for q in range(4):
                    sp.dma_start(g.steps.rearrange("(p r) q -> p (r q)", p=P)[:, q * n:(q + 1) * n], fill[:, :]).then_inc(stored, 16)

            @block.gpsimd
            def _(gp):
                nc.gpsimd.iota(back_i[:, :], [[-1, TP]], base=TP, channel_multiplier=0).then_inc(seq, 1)
                nc.gpsimd.iota(first_i[:, :], [[1, 1]], base=TP, channel_multiplier=TP).then_inc(seq, 1)
                nc.gpsimd.iota(rank_i[:, :], [[1, TP + 16]], base=0, channel_multiplier=0).then_inc(seq, 1)
                nc.gpsimd.memset(fill[:, :], NONE).then_inc(fill_ready, 1)
                nc.gpsimd.memset(tri[:, :], 0.0).then_inc(tri_ready, 1)
                gp.wait_ge(tri_ready, 1)
                nc.gpsimd.affine_select(out=tri[:, :], in_=tri[:, :], compare_op=ALU.is_ge, fill=1.0,
                                        base=0, pattern=[[-1, P]], channel_multiplier=1).then_inc(tri_ready, 1)

            @block.vector
            def _(dv):
                V = nc.vector
                V.memset(src_i[:, :], NP - 1).then_inc(blank, 1)
                V.memset(dst_i[:, :], NP - 1).then_inc(blank, 1)
                V.memset(w[:, :], 0.0).then_inc(blank, 1)
                ch = Chain(dv, ops)
                dv.wait_ge(seq, 3)
                dv.wait_ge(din, 6 * 16)
                ch.do(V.tensor_scalar(turns[:, :], w[:, :], 1.0 / TWO_PI, ROUND, ALU.mult, ALU.add))
                ch.do(V.tensor_scalar(turns[:, :], turns[:, :], ROUND, None, ALU.subtract))
                ch.do(V.scalar_tensor_tensor(out=w[:, :], in0=turns[:, :], scalar=-TWO_PI_HI, in1=w[:, :], op0=ALU.mult, op1=ALU.add))
                ch.do(V.scalar_tensor_tensor(out=w[:, :], in0=turns[:, :], scalar=-(TWO_PI - TWO_PI_HI), in1=w[:, :], op0=ALU.mult, op1=ALU.add))
                ch.do(V.tensor_scalar(w[:, :], w[:, :], TWO_PI / 2 - 1e-6, -TWO_PI / 2 + 1e-6, ALU.min, ALU.max))
                mark["angle"] = ch.n
                ch.do(V.tensor_copy(srcf[:, :], src_i[:, :]))
                ch.do(V.tensor_copy(dstf[:, :], dst_i[:, :]))
                ch.do(V.tensor_copy(back[:, :], back_i[:, :]))
                ch.do(V.tensor_copy(firstf[:, :], first_i[:, :]))
                ch.do(V.tensor_copy(rank[:, :], rank_i[:, :]))
                ch.do(V.memset(keys[:, :], 0.0))
                ch.do(V.tensor_scalar(early[:, :], dstf[:, :], float(D), None, ALU.is_lt))
                ch.do(V.tensor_scalar(inside[:, :], srcf[:, :], float(D), None, ALU.is_lt))
                ch.do(V.memset(event[:, :], 1.0))
                ch.do(V.tensor_tensor(event[:, 0:TP - 1], dstf[:, 1:TP], dstf[:, 0:TP - 1], ALU.not_equal))
                ch.do(V.tensor_tensor(event[:, :], event[:, :], inside[:, :], ALU.max))
                ch.do(V.tensor_tensor(event[:, :], event[:, :], early[:, :], ALU.mult))
                ch.do(V.tensor_tensor(tmp[:, :], inside[:, :], early[:, :], ALU.mult))
                ch.do(V.tensor_tensor(late[:, :], inside[:, :], tmp[:, :], ALU.subtract))
                ch.do(V.tensor_tensor(listed[:, :], event[:, :], late[:, :], ALU.add))
                ch.do(V.tensor_reduce(out=counts[:, 0:1], in_=listed[:, :], axis=AX.X, op=ALU.add))
                ch.do(V.tensor_reduce(out=counts[:, 1:2], in_=event[:, :], axis=AX.X, op=ALU.add))
                mark["counts"] = ch.n
                ch.do(V.tensor_tensor(listed[:, :], listed[:, :], back[:, :], ALU.mult))
                plain = tmp2
                ch.do(V.tensor_tensor(plain[:, :], early[:, :], tmp[:, :], ALU.subtract))
                ch.do(V.memset(reset[:, 0:1], 1.0))
                ch.do(V.tensor_copy(reset[:, 1:TP], event[:, 0:TP - 1]))
                dv.wait_ge(waves, 2)
                ch.do(V.tensor_scalar(cos[:, :], half[:, :], -2.0, 1.0, ALU.mult, ALU.add))
                ch.do(V.tensor_scalar(tmp[:, :], dstf[:, :], float(D - 1), None, ALU.is_equal))
                ch.do(V.tensor_tensor(d1[:, :], tmp[:, :], sin[:, :], ALU.mult))
                ch.do(V.tensor_tensor(pc[:, :], cos[:, :], d1[:, :], ALU.add))
                ch.do(V.tensor_tensor(psn[:, :], sin[:, :], d1[:, :], ALU.subtract))
                ch.do(V.tensor_tensor(psn[:, :], psn[:, :], plain[:, :], ALU.mult))
                ch.do(V.scalar_tensor_tensor(out=pc[:, :], in0=pc[:, :], scalar=-1.0, in1=plain[:, :], op0=ALU.add, op1=ALU.mult))
                ch.do(V.tensor_scalar(pc[:, :], pc[:, :], 1.0, None, ALU.add))
                ch.do(V.tensor_tensor(d1[:, :], pc[:, :], reset[:, :], ALU.mult))
                ch.do(V.tensor_tensor(pc[:, :], pc[:, :], d1[:, :], ALU.subtract))
                ch.do(V.tensor_tensor_scan(tmp[:, :], pc[:, :], d1[:, :], 0.0, ALU.mult, ALU.add))
                ch.do(V.tensor_tensor_scan(tmp2[:, :], pc[:, :], psn[:, :], 0.0, ALU.mult, ALU.add))
                ch.do(V.tensor_copy(rec[:, :, ALPHA], tmp[:, :]))
                ch.do(V.tensor_copy(rec[:, :, BETA], tmp2[:, :]))
                ch.do(V.scalar_tensor_tensor(out=tmp[:, :], in0=cos[:, :], scalar=-1.0, in1=inside[:, :], op0=ALU.add, op1=ALU.mult))
                ch.do(V.tensor_scalar(rec[:, :, COS], tmp[:, :], 1.0, None, ALU.add))
                ch.do(V.tensor_tensor(rec[:, :, SIN], sin[:, :], inside[:, :], ALU.mult))
                ch.do(V.tensor_scalar(rec[:, :, READ], srcf[:, :], float(D - 1), None, ALU.min))
                ch.do(V.tensor_tensor(tmp[:, :], srcf[:, :], dstf[:, :], ALU.is_equal))
                ch.do(V.tensor_scalar(tmp[:, :], tmp[:, :], float(D), None, ALU.mult))
                ch.do(V.scalar_tensor_tensor(out=rec[:, :, WRITE], in0=srcf[:, :], scalar=float(D), in1=tmp[:, :], op0=ALU.min, op1=ALU.max))
                ch.do(V.tensor_scalar(rec[:, :, ROW], dstf[:, :], float(D - 1), None, ALU.min))
                ch.do(V.scalar_tensor_tensor(out=tmp[:, :], in0=srcf[:, :], scalar=-NONE, in1=late[:, :], op0=ALU.add, op1=ALU.mult))
                ch.do(V.tensor_scalar(rec[:, :, LATE], tmp[:, :], NONE, None, ALU.add))
                mark["rec"] = ch.n
                dv.wait_ge(summed, 3)
                ch.do(V.tensor_reduce(out=most[0:1, 0:1], in_=p_cnt[0:1, :], axis=AX.X, op=ALU.max))
                ch.do(V.tensor_copy(most[0:1, 1:3], p_tot[0:1, :]))
                ch.do(V.tensor_copy(base[:, :], p_base[:, :]))
                ch.do(V.tensor_scalar(most[0:1, 0:1], most[0:1, 0:1], 15.0, None, ALU.add))
                ch.do(V.tensor_copy(g.sizes[0:1, 0:3], most[0:1, :]))
                ch.do(V.tensor_scalar(g.sizes[0:1, 0:1], g.sizes[0:1, 0:1], 4, None, ALU.arith_shift_right))
                for k in (1, 2):
                    ch.do(V.tensor_scalar(most[0:1, k:k + 1], most[0:1, k:k + 1], float(QC - 1), None, ALU.add))
                ch.do(V.tensor_copy(g.sizes[0:1, 3:5], most[0:1, 1:3]))
                ch.do(V.tensor_scalar(g.sizes[0:1, 3:5], g.sizes[0:1, 3:5], 9, None, ALU.arith_shift_right))
                ch.do(V.tensor_copy(tmp[0:1, 0:NQ], g.sizes[0:1, 2:3].to_broadcast([1, NQ])))
                ch.do(V.scalar_tensor_tensor(out=tmp[0:1, 0:NQ], in0=rank[0:1, 0:NQ], scalar=-float(QC), in1=tmp[0:1, 0:NQ], op0=ALU.mult, op1=ALU.add))
                ch.do(V.tensor_scalar(tmp[0:1, 0:NQ], tmp[0:1, 0:NQ], 0.0, float(QC), ALU.max, ALU.min))
                ch.do(V.tensor_copy(g.chunk_early[0:1, :], tmp[0:1, 0:NQ]))
                V.sem_inc(set_up, 1)
                dv.nop(nofuse=True)
                n = dv.value_load(g.sizes[0:1, 0:1], min_val=0, max_val=TP // 16)
                with dv.Fori(0, n) as i:
                    for u in range(2):
                        c = Chain(dv, chunks, 6 * i + 3 * u)
                        dv.nop(nofuse=True)
                        c.do(V.max(key8[:, :], listed[:, :]))
                        c.do(V.tensor_copy(keys[:, bass.ds(16 * i + 8 * u, 8)], key8[:, :]))
                        dv.nop(nofuse=True)
                        c.do(V.match_replace(listed[:, :], key8[:, :], listed[:, :], 0.0))
                ch.do(V.tensor_scalar(keys[:, :], keys[:, :], -1.0, firstf[:, 0:1], ALU.mult, ALU.add))
                ch.do(V.tensor_scalar(keys[:, :], keys[:, :], float(EP - 1), None, ALU.min))
                ch.do(V.tensor_copy(edge[:, :], keys[:, :]))
                ch.do(V.tensor_scalar(keys[:, :], rank[:, :], counts[:, 0:1], OUT, ALU.is_ge, ALU.mult))
                ch.do(V.scalar_tensor_tensor(out=keys[:, :], in0=rank[:, :], scalar=base[:, 0:1], in1=keys[:, :], op0=ALU.add, op1=ALU.add))
                ch.do(V.tensor_copy(place[:, :], keys[:, :]))
                V.sem_inc(set_up, 1)

            @block.scalar
            def _(ac):
                ac.wait_ge(ops, mark["angle"])
                nc.scalar.activation(sin[:, :], w[:, :], ACT.Sin).then_inc(waves, 1)
                nc.scalar.activation(half[:, :], w[:, :], ACT.Sin, scale=0.5).then_inc(squared, 1)
                ac.wait_ge(squared, 1)
                nc.scalar.activation(half[:, :], half[:, :], ACT.Square).then_inc(waves, 1)
                ac.wait_ge(ops, mark["rec"])
                ac.dma_start(g.records.rearrange("(p t) f -> p (t f)", p=P), rec[:, :, :].rearrange("p t f -> p (t f)")).then_inc(stored, 16)
                ac.wait_ge(stored, 5 * 16)

            @block.tensor
            def _(pe):
                pe.wait_ge(tri_ready, 2)
                pe.wait_ge(ops, mark["counts"])
                nc.tensor.transpose(p_cnt[:, :], counts[:, 0:1], g.ident[:, :]).then_inc(summed, 1)
                nc.tensor.matmul(p_tot[:, :], g.ones[:, :], counts[:, :], start=True, stop=True).then_inc(summed, 1)
                nc.tensor.matmul(p_base[:, :], tri[:, :], counts[:, 0:1], start=True, stop=True).then_inc(summed, 1)

        with nc.Block() as block:
            @block.gpsimd
            def _(gp):
                def fetch(i, s):
                    G = nc.gpsimd
                    G.tensor_copy(ids[:, s, :], edge[:, bass.ds(i * 8, 8)]).then_inc(copied, 1)
                    G.tensor_copy(tos[:, s, :], place[:, bass.ds(i * 8, 8)]).then_inc(copied, 1)
                    gp.wait_ge(copied, 2 * (i + 1))
                    gp.nop(nofuse=True)
                    for k in range(8):
                        gp.indirect_dma_start(got[:, s, k, :], None, g.records, bass.IndirectOffsetOnAxis(ids[:, s, k:k + 1], 0)).then_inc(fetched[s], 16)

                def put(s):
                    for k in range(8):
                        gp.indirect_dma_start(g.steps, bass.IndirectOffsetOnAxis(tos[:, s, k:k + 1], 0), got[:, s, k, :], None,
                                              bounds_check=EP - 1, oob_is_err=False).then_inc(placed[s], 16)
                n = gp.value_load(g.sizes[0:1, 0:1], min_val=0, max_val=TP // 16)
                fetch(0, 0)
                with gp.Fori(0, n) as i:
                    fetch(2 * i + 1, 1)
                    gp.wait_ge(fetched[0], 128 * (i + 1))
                    gp.nop(nofuse=True)
                    put(0)
                    gp.wait_ge(placed[0], 128 * (i + 1))
                    fetch(2 * i + 2, 0)
                    gp.wait_ge(fetched[1], 128 * (i + 1))
                    gp.nop(nofuse=True)
                    put(1)
                    gp.wait_ge(placed[1], 128 * (i + 1))
                gp.wait_ge(fetched[0], 128 * (n + 1))


def early_steps(nc, g):
    with Phase(nc, "early") as ph:
        entry = ph.sb("entry", [1, QC, LISTED])
        at = ph.sb("at", [1, QC, 3], I32)
        fac = ph.sb("fac", [P, 4, QC])
        t0, t1, t2 = ph.sb("t0", [P, 2]), ph.sb("t1", [P, 2]), ph.sb("t2", [P, 2])
        p_f = [ph.ps(f"p_f{f}", [P, QC]) for f in range(4)]
        loaded, spread, used, ops, ready, init = (ph.sem(n) for n in ("loaded", "spread", "used", "ops", "ready", "init"))
        row = lambda n: g.mt[:, :, bass.ds(n, 1)].rearrange("p b a -> p (b a)")
        last_row = g.mt[:, :, D - 1]
        with nc.Block() as block:
            @block.sync
            def _(sp):
                n = sp.value_load(g.sizes[0:1, 4:5], min_val=0, max_val=NQ)
                with sp.Fori(0, n) as q:
                    sp.wait_ge(used, q + 1)
                    sp.dma_start(entry[:, :, :], g.steps[bass.ds(q * QC, QC), :].rearrange("(o e) f -> o e f", o=1)).then_inc(loaded, 16)

            @block.tensor
            def _(pe):
                n = pe.value_load(g.sizes[0:1, 4:5], min_val=0, max_val=NQ)
                with pe.Fori(0, n) as q:
                    pe.wait_ge(loaded, 16 * (q + 1))
                    for f in range(4):
                        nc.tensor.matmul(p_f[f][:, :], g.ones[0:1, :], entry[0:1, :, f], start=True, stop=True).then_inc(spread, 1)

            @block.vector
            def _(dv):
                V = nc.vector
                V.sem_inc(used, 1)
                c0 = Chain(dv, init)
                c0.do(V.memset(g.mt[:, :, :], 0.0))
                for b in range(2):
                    c0.do(V.tensor_copy(g.mt[:, b, b * P:(b + 1) * P], g.ident[:, :]))
                n = dv.value_load(g.sizes[0:1, 4:5], min_val=0, max_val=NQ)
                with dv.Fori(0, n) as q:
                    dv.wait_ge(loaded, 16 * (q + 1))
                    V.tensor_copy(at[:, :, :], entry[:, :, READ:READ + 3]).then_inc(ready, 1)
                    dv.wait_ge(spread, 4 * (q + 1))
                    for f in range(4):
                        V.tensor_copy(fac[:, f, :], p_f[f][:, :]).then_inc(ready, 1)
                    dv.wait_ge(ready, 5 * (q + 1))
                    dv.nop(nofuse=True)
                    m = dv.value_load(g.chunk_early[0:1, bass.ds(q, 1)], min_val=0, max_val=QC)
                    with dv.Fori(0, m) as e:
                        _, (i, wi, j) = nc.values_load_multi_w_load_instructions(at[0:1, bass.ds(e, 1), :].rearrange("o a f -> o (a f)"), engines=DVE_ONLY, min_val=0, max_val=D)
                        f = lambda k: fac[:, k, bass.ds(e, 1)]
                        s = Chain(dv, ops, 6 * QC * q + 6 * e)
                        s.do(V.tensor_scalar(t0[:, :], last_row, f(BETA), None, ALU.mult))
                        s.do(V.scalar_tensor_tensor(out=row(j), in0=row(j), scalar=f(ALPHA), in1=t0[:, :], op0=ALU.mult, op1=ALU.add))
                        s.do(V.tensor_scalar(t1[:, :], row(j), f(SIN), None, ALU.mult), wait=False)
                        s.do(V.tensor_scalar(t2[:, :], row(i), f(SIN), None, ALU.mult))
                        s.do(V.scalar_tensor_tensor(out=row(wi), in0=row(i), scalar=f(COS), in1=t1[:, :], op0=ALU.mult, op1=ALU.subtract), wait=False)
                        s.do(V.scalar_tensor_tensor(out=row(j), in0=row(j), scalar=f(COS), in1=t2[:, :], op0=ALU.mult, op1=ALU.add))
                    V.sem_inc(used, 1)


def late_steps(nc, g):
    with Phase(nc, "late") as ph:
        entry = ph.sb("entry", [1, 2, QC, LISTED])
        who_i, who = ph.sb("who_i", [P, 2], I32), ph.sb("who", [P, 2])
        cos, sin, is_last, scale, other = (ph.sb(n, [P, QC]) for n in ("cos", "sin", "is_last", "scale", "other"))
        late = ph.sb("late", [P, QC])
        grown = ph.sb("grown", [P, QC + 1])
        mine, factor, term, out_a, out_b = (ph.sb(n, [P, 2, QC]) for n in ("mine", "factor", "term", "out_a", "out_b"))
        state = ph.sb("state", [P, 4])
        wide = ph.sb("wide", [P, 4, P])
        p_f = [ph.ps(f"p_f{f}", [P, QC]) for f in range(3)]
        p_s = ph.ps("p_s", [P, 4, P])
        seq, spread, used, ops, init, ready, turned = (ph.sem(n) for n in ("seq", "spread", "used", "ops", "init", "ready", "turned"))
        final = ph.sem("final")
        loaded = ph.sem("loaded")
        per = 22
        with nc.Block() as block:
            @block.sync
            def _(sp):
                n = sp.value_load(g.sizes[0:1, 3:4], min_val=0, max_val=NQ)
                with sp.Fori(0, n) as q:
                    sp.wait_ge(spread, 3 * q + 3)
                    sp.dma_start(entry[:, 0, :, :], g.steps[bass.ds(q * QC, QC), :].rearrange("(o e) f -> o e f", o=1)).then_inc(loaded, 16)

            @block.gpsimd
            def _(gp):
                nc.gpsimd.iota(who_i[:, :], [[P, 2]], base=0, channel_multiplier=1).then_inc(seq, 1)

            @block.tensor
            def _(pe):
                nc.tensor.sem_inc(spread, 3)
                n = pe.value_load(g.sizes[0:1, 3:4], min_val=0, max_val=NQ)
                with pe.Fori(0, n) as q:
                    pe.wait_ge(loaded, 16 * (q + 1))
                    pe.wait_ge(used, q + 1)
                    for k, f in enumerate((COS, SIN, LATE)):
                        nc.tensor.matmul(p_f[k][:, :], g.ones[0:1, :], entry[0:1, 0, :, f], start=True, stop=True).then_inc(spread, 1)
                pe.wait_ge(ready, 1)
                for k in range(4):
                    nc.tensor.matmul(p_s[:, k, :], wide[:, k, :], g.ident[:, :], start=True, stop=True).then_inc(turned, 1)

            @block.vector
            def _(dv):
                V = nc.vector
                V.sem_inc(used, 1)
                c0 = Chain(dv, init)
                dv.wait_ge(seq, 1)
                c0.do(V.tensor_copy(who[:, :], who_i[:, :]))
                c0.do(V.memset(grown[:, QC:QC + 1], 1.0))
                c0.do(V.memset(state[:, 0:2], 1.0))
                c0.do(V.memset(state[:, 2:4], 0.0))
                n = dv.value_load(g.sizes[0:1, 3:4], min_val=0, max_val=NQ)
                with dv.Fori(0, n) as q:
                    dv.wait_ge(spread, 3 * q + 6)
                    s = Chain(dv, ops, per * q)
                    s.do(V.tensor_copy(cos[:, :], p_f[0][:, :]), wait=False)
                    s.do(V.tensor_copy(late[:, :], p_f[2][:, :]), wait=False)
                    s.do(V.tensor_copy(sin[:, :], p_f[1][:, :]))
                    V.sem_inc(used, 1)
                    s.do(V.tensor_copy(grown[:, 0:1], grown[:, QC:QC + 1]), wait=False)
                    s.do(V.tensor_scalar(is_last[:, :], late[:, :], float(D - 1), None, ALU.is_equal), wait=False)
                    s.do(V.tensor_tensor(scale[:, :], cos[:, :], sin[:, :], ALU.subtract))
                    s.do(V.scalar_tensor_tensor(out=scale[:, :], in0=scale[:, :], scalar=-1.0, in1=is_last[:, :], op0=ALU.add, op1=ALU.mult))
                    s.do(V.tensor_scalar(scale[:, :], scale[:, :], 1.0, None, ALU.add))
                    s.do(V.tensor_tensor_scan(grown[:, 1:QC + 1], scale[:, :], scale[:, :], grown[:, 0:1], ALU.mult, ALU.bypass), wait=False)
                    for h in range(2):
                        s.do(V.tensor_scalar(mine[:, h, :], late[:, :], who[:, h:h + 1], None, ALU.is_equal), wait=h == 1)
                    s.do(V.scalar_tensor_tensor(out=other[:, :], in0=sin[:, :], scalar=-1.0, in1=grown[:, 0:QC], op0=ALU.mult, op1=ALU.mult), wait=False)
                    for h in range(2):
                        s.do(V.scalar_tensor_tensor(out=factor[:, h, :], in0=cos[:, :], scalar=-1.0, in1=mine[:, h, :], op0=ALU.add, op1=ALU.mult), wait=h == 1)
                    s.do(V.tensor_tensor(term[:, :, :], mine[:, :, :], other[:, :].unsqueeze(1).to_broadcast([P, 2, QC]), ALU.mult), wait=False)
                    s.do(V.tensor_scalar(factor[:, :, :], factor[:, :, :], 1.0, None, ALU.add))
                    for h in range(2):
                        s.do(V.tensor_tensor_scan(out_a[:, h, :], factor[:, h, :], factor[:, h, :], state[:, h:h + 1], ALU.mult, ALU.bypass), wait=False)
                        s.do(V.tensor_tensor_scan(out_b[:, h, :], factor[:, h, :], term[:, h, :], state[:, 2 + h:3 + h], ALU.mult, ALU.add), wait=h == 1)
                    s.do(V.tensor_copy(state[:, 0:2], out_a[:, :, QC - 1]), wait=False)
                    s.do(V.tensor_copy(state[:, 2:4], out_b[:, :, QC - 1]))
                    assert s.n == per, s.n
                for k in range(4):
                    c0.do(V.tensor_copy(wide[:, k, :], state[:, k:k + 1].to_broadcast([P, P])))
                V.sem_inc(ready, 1)
                dv.wait_ge(turned, 4)
                by_row = lambda h: p_s[:, 2 * h:2 * h + 2, :].rearrange("p k n -> p (k n)")[:, 0:D - 1]
                f = Chain(dv, final)
                tmp = out_a[:, :, 0:D - 1]
                for b in range(2):
                    f.do(V.tensor_scalar(out_a[:, b, 0:D - 1], by_row(1), g.mt[:, b, D - 1:D], None, ALU.mult))
                    f.do(V.tensor_tensor(g.mt[:, b, 0:D - 1], g.mt[:, b, 0:D - 1], by_row(0), ALU.mult))
                    f.do(V.tensor_tensor(g.mt[:, b, 0:D - 1], g.mt[:, b, 0:D - 1], out_a[:, b, 0:D - 1], ALU.add))
                f.do(V.tensor_scalar(g.mt[:, :, D - 1], g.mt[:, :, D - 1], grown[:, QC:QC + 1], None, ALU.mult))


def l0_gnn(nc, g):
    with ExitStack() as own:
        sb = lambda n, s, d=F32: own.enter_context(nc.sbuf_tensor(n, s, d))
        dr = lambda n, s, d=F32: nc.dram_tensor(n, s, d, kind="Internal").ap()
        g.w_dram = g.a["edge_weight"]
        g.sizes, g.chunk_early = sb("sizes", [1, 5], I32), sb("chunk_early", [1, NQ], I32)
        g.mt = sb("mt", [P, 2, D + 1])
        g.records, g.steps = dr("records", [EP, LISTED]), dr("steps", [EP, LISTED])
        rotation_list(nc, g)
        early_steps(nc, g)
        late_steps(nc, g)
        x_plus_product(nc, g, "l0g", g.mt[:, :, 0:D])


def add_agg(nc, g):
    with Phase(nc, "add") as ph:
        added = ph.sem("added")
        with nc.Block() as block:
            @block.vector
            def _(dv):
                nc.vector.tensor_tensor(g.x[:, :, :], g.x[:, :, :], g.agg[:, :, 0:D], ALU.add).then_inc(added, 1)
                dv.wait_ge(added, 1)


def store_x(nc, g):
    with Phase(nc, "out") as ph:
        stored = ph.sem("stored")
        with nc.Block() as block:
            @block.sync
            def _(sp):
                sp.dma_start(g.out[0:(NT - 1) * P, :].rearrange("(t p) d -> p t d", p=P), g.x[:, 0:NT - 1, :]).then_inc(stored, 16)
                sp.dma_start(g.out[(NT - 1) * P:N_NODES, :], g.x[0:LAST, NT - 1, :]).then_inc(stored, 16)
                sp.wait_ge(stored, 32)


def gnn_ffn_stack(nc, a, out):
    g = setup(nc, a, out)
    setup3(nc, g)
    setup4(nc, g)
    constants(nc, g)
    clear_rows(nc, g)
    l0_gnn(nc, g)
    l0_ffn(nc, g, a)
    edge_tables(nc, g)
    gat_table(nc, g, "t1", a["L1_gnn_W"], a["L1_gnn_a_left"], a["L1_gnn_a_right"], 8, D, True, g.table, g.inject8, True)
    gather_pass(nc, g, "g1", g.table, D, 8, g.inject8)
    gat_finish(nc, g, "f1", g.table, 8, 1e-16)
    add_agg(nc, g)
    turned_weights(nc, g, a["L1_ffn_weight"], "wt1")
    x_plus_product(nc, g, "l1f", g.wt, a["L1_ffn_bias"])
    ln_rows(nc, g, "lnr", table=g.rows256)
    gather_pass(nc, g, "g2p", g.rows256, D)
    ln_rows(nc, g, "lna")
    turned_weights(nc, g, a["L2_gnn_W"], "wt2")
    agg_product(nc, g, "l2w", g.wt)
    batch_norm(nc, g, "bnl2", D, a["L2_gnn_b"], a["L2_gnn_bn_w"], a["L2_gnn_bn_b"], True)
    top2_ffn(nc, g, *(a["L2_ffn_" + n] for n in ("gate_w", "gate_b", "W1", "b1", "W2", "b2")), True)
    l3_gnn(nc, g, {n: a["L3_gnn_" + n] for n in ("W_gcn", "b_gcn", "g0", "beta0", "W1", "a_src1", "a_dst1", "b1", "g1", "beta1",
                                                 "W2", "a_src2", "a_dst2", "b2", "g2", "beta2")})
    top2_ffn(nc, g, *(a["L3_ffn_" + n] for n in ("Wg", "bg", "W1", "b1", "W2", "b2")), False)
    store_x(nc, g)
    nc.keep.close()


def kernel(**inputs):
    import concourse.bacc as bacc
    from concourse.bass_utils import run_bass_kernel_spmd

    nc = bacc.Bacc("TRN2", target_bir_lowering=False, num_devices=1)
    arrays = {f"in_{name}_dram": np.ascontiguousarray(value) for name, value in inputs.items()}
    args = {name: nc.dram_tensor(f"in_{name}_dram", value.shape, mybir.dt.from_np(value.dtype), kind="ExternalInput").ap()
            for name, value in ((n, arrays[f"in_{n}_dram"]) for n in inputs)}
    out = nc.dram_tensor("out_0_dram", (N_NODES, D), F32, kind="ExternalOutput").ap()
    gnn_ffn_stack(nc, args, out)
    result = run_bass_kernel_spmd(nc, [arrays], core_ids=[0])
    return result.results[0]["out_0_dram"]
```

```python
import numpy as np
import concourse.bass as bass
from concourse import mybir
from contextlib import ExitStack

F32 = mybir.dt.float32
BF16 = mybir.dt.bfloat16
I32 = mybir.dt.int32
ALU = mybir.AluOpType
ACT = mybir.ActivationFunctionType
AX = mybir.AxisListType
DVE, PE = mybir.EngineType.DVE, mybir.EngineType.PE

P = 128
N_NODES, D, N_EDGES = 6250, 256, 100000
NT = -(-N_NODES // P)
GROUP = 7
NP = NT * P
LAST = N_NODES - (NT - 1) * P
J = 16
CH = P * J
NC = -(-N_EDGES // CH)
EP = NC * CH
LC = N_EDGES - (NC - 1) * CH
INFO = 5
BIG = 1e30
LN_EPS = 1e-5
assert LC % J == 0 and NC == NT and NT % GROUP == 0


class Phase:

    def __init__(self, nc, name):
        self.nc, self.name, self.stack, self.sems = nc, f"{name}_{nc.next_id()}", ExitStack(), []

    def __enter__(self):
        return self

    def __exit__(self, *failed):
        self.stack.close()
        if failed[0] is None:
            self.nc.clear_and_free_semaphores(self.sems)
            self.nc.all_engine_barrier()

    def sb(self, name, shape, dt=F32):
        return self.stack.enter_context(self.nc.sbuf_tensor(f"{self.name}_{name}", shape, dt))

    def ps(self, name, shape, dt=F32):
        return self.stack.enter_context(self.nc.psum_tensor(f"{self.name}_{name}", shape, dt))

    def sem(self, name):
        self.sems.append(self.nc.alloc_semaphore(f"{self.name}_{name}"))
        return self.sems[-1]


class Chain:

    def __init__(self, eng, sem, base=0):
        self.eng, self.sem, self.base, self.n = eng, sem, base, 0

    def do(self, ins, wait=True):
        ins.then_inc(self.sem, 1)
        self.n += 1
        if wait:
            self.eng.wait_ge(self.sem, self.base + self.n)


def by_two(eng, n, body):
    with eng.Fori(0, n // 2) as i:
        body(2 * i, 0)
        body(2 * i + 1, 1)
    if n % 2:
        body(n - 1, 0)


def dram_view(ap, offset, dims):
    return bass.AP(tensor=ap.tensor, offset=offset, ap=[list(d) for d in dims])


def registers(nc, engine, values, most, waited):
    if waited:
        _, loaded = nc.values_load_multi_w_load_instructions(values, engines=(engine,), min_val=0, max_val=most)
    else:
        _, loaded = nc.values_load_multi_w_load_instructions(values, engines=(engine,), min_val=0, max_val=most,
                                                             skip_runtime_bounds_check_because="the program has made them itself, in this range")
    return loaded


class Store:
    pass


def constants(nc, g):
    with Phase(nc, "const") as ph:
        zeroed, placed, seq = ph.sem("zeroed"), ph.sem("placed"), ph.sem("seq")
        x_in, pad = ph.sem("x_in"), ph.sem("pad")
        with nc.Block() as block:
            @block.gpsimd
            def _(gp):
                nc.gpsimd.memset(g.ident[:, :], 0.0).then_inc(zeroed, 1)
                nc.gpsimd.memset(g.ones[:, :], 1.0).then_inc(placed, 1)
                gp.wait_ge(zeroed, 1)
                nc.gpsimd.affine_select(out=g.ident[:, :], in_=g.ident[:, :], compare_op=ALU.not_equal, fill=1.0,
                                        base=0, pattern=[[-1, P]], channel_multiplier=1).then_inc(placed, 1)
                nc.gpsimd.iota(g.iota_i[:, :], [[1, P]], base=0, channel_multiplier=0).then_inc(seq, 1)

            @block.vector
            def _(dv):
                nc.vector.memset(g.x[:, NT - 1, :], 0.0).then_inc(pad, 1)
                dv.wait_ge(seq, 1)
                nc.vector.tensor_copy(g.iota[:, :], g.iota_i[:, :]).then_inc(placed, 1)

            @block.sync
            def _(sp):
                sp.dma_start(g.x[:, 0:NT - 1, :], g.x_dram[0:(NT - 1) * P, :].rearrange("(t p) d -> p t d", p=P)).then_inc(x_in, 16)
                sp.wait_ge(pad, 1)
                sp.dma_start(g.x[0:LAST, NT - 1, :], g.x_dram[(NT - 1) * P:N_NODES, :]).then_inc(x_in, 16)
                sp.wait_ge(x_in, 32)


def edge_tables(nc, g):
    with Phase(nc, "edge") as ph:
        around = ph.sb("around", [P, NC, J + 2], I32)
        dst_i = ph.sb("dst_i", [P, NC * J], I32)
        hi_i = ph.sb("hi_i", [P, NC * J], I32)
        lo_i = ph.sb("lo_i", [P, NC * J], I32)
        hi = ph.sb("hi", [P, NC, J], BF16)
        lo = ph.sb("lo", [P, NC, J], BF16)
        iota_b = ph.sb("iota_b", [P, P], BF16)
        start = ph.sb("start", [P, NC, J])
        start_next = ph.sb("start_next", [P, NC, J])
        not_first = ph.sb("not_first", [P, NC, J])
        not_last = ph.sb("not_last", [P, NC, J])
        seen = ph.sb("seen", [P, NC, J])
        seen_b = ph.sb("seen_b", [P, NC, J])
        tmp = ph.sb("tmp", [P, NC, J])
        resets = ph.sb("resets", [P, 2, NC])
        reset_rows = ph.sb("reset_rows", [NC, 2, P])
        first_lof = ph.sb("first_lof", [1, NC])
        tile_at, further, further_to, further_from = ph.sb("tile_at", [1, NC + 1]), ph.sb("further", [1, NC]), ph.sb("further_to", [1, NC]), ph.sb("further_from", [1, NC])
        first_hot = g.agg[0:1, :, :].rearrange("o t w -> o (t w)")[:, 0:NC * 2 * P].rearrange("o (c a p) -> o c a p", c=NC, a=2)
        hot_lo = ph.sb("hot_lo", [P, 2, J, P], BF16)
        hot_hi = ph.sb("hot_hi", [P, 2, J, NT], BF16)
        zero_b = ph.sb("zero_b", [P, P], BF16)
        tri = ph.sb("tri", [NT, NT])
        deg = ph.sb("deg", [NT, P])
        first = ph.sb("first", [NT, P])
        none = ph.sb("none", [NT, P])
        offs = ph.sb("offs", [NT, 1])
        p_rs = ph.ps("p_rs", [NC, 2, P])
        p_deg = ph.ps("p_deg", [NT, P])
        p_off = ph.ps("p_off", [NT, 1])
        p_t = ph.ps("p_t", [P, 2, NT])
        blank, d_in, s_in, no_src, rs_done = (ph.sem(n) for n in ("blank", "d_in", "s_in", "no_src", "rs_done"))
        ops, rs_t, rs_ready = ph.sem("ops"), ph.sem("rs_t"), ph.sem("rs_ready")
        hot, hot_free, deg_done, deg_ready, off_done, t_done = (ph.sem(n) for n in ("hot", "hot_free", "deg_done", "deg_ready", "off_done", "t_done"))
        stored, tri_ready, hot_row = ph.sem("stored"), ph.sem("tri_ready"), ph.sem("hot_row")
        dst, src = g.dst_dram, g.src_dram
        full = NC - 1
        lp = LC // J
        flat = lambda t: t[:, :, :].rearrange("p c j -> p (c j)")
        with nc.Block() as block:
            @block.sync
            def _(sp):
                sp.wait_ge(blank, 2)
                sp.wait_ge(no_src, 1)
                e0 = full * CH
                sp.dma_start(around[:, 1:full, :], dram_view(dst, CH - 1, [[J, P], [CH, full - 1], [1, J + 2]])).then_inc(d_in, 16)
                sp.dma_start(around[1:P, 0, :], dram_view(dst, J - 1, [[J, P - 1], [1, J + 2]])).then_inc(d_in, 16)
                sp.dma_start(around[0:1, 0, 1:J + 2], dram_view(dst, 0, [[J, 1], [1, J + 1]])).then_inc(d_in, 16)
                sp.dma_start(around[0:lp - 1, full, :], dram_view(dst, e0 - 1, [[J, lp - 1], [1, J + 2]])).then_inc(d_in, 16)
                sp.dma_start(around[lp - 1:lp, full, 0:J + 1], dram_view(dst, e0 + (lp - 1) * J - 1, [[J, 1], [1, J + 1]])).then_inc(d_in, 16)
                sp.dma_start(around[lp:lp + 1, full, 0:1], dram_view(dst, N_EDGES - 1, [[1, 1], [1, 1]])).then_inc(d_in, 16)
                sp.dma_start(g.src_idx[:, 0:full * J].rearrange("p (c j) -> p c j", j=J),
                             dram_view(src, 0, [[J, P], [CH, full], [1, J]])).then_inc(s_in, 16)
                sp.dma_start(g.src_idx[0:lp, full * J:NC * J], dram_view(src, e0, [[J, lp], [1, J]])).then_inc(s_in, 16)
                sp.wait_ge(rs_ready, 1)
                sp.dma_start(g.resets_dram, reset_rows[:, :, :]).then_inc(stored, 16)
                sp.wait_ge(hot_row, 1)
                sp.dma_start(g.first_hot_dram, first_hot.rearrange("o c a p -> o (c a p)")).then_inc(stored, 16)
                sp.wait_ge(s_in, 32)
                sp.wait_ge(stored, 32)

            @block.gpsimd
            def _(gp):
                nc.gpsimd.memset(g.src_idx[:, :], 0).then_inc(no_src, 1)
                nc.gpsimd.memset(tri[:, :], 0.0).then_inc(tri_ready, 1)
                gp.wait_ge(tri_ready, 1)
                nc.gpsimd.affine_select(out=tri[:, :], in_=tri[:, :], compare_op=ALU.is_ge, fill=1.0,
                                        base=0, pattern=[[-1, NT]], channel_multiplier=1).then_inc(tri_ready, 1)

            @block.vector
            def _(dv):
                nc.vector.memset(around[:, :, :], NP - 1).then_inc(blank, 1)
                dv.wait_ge(blank, 1)
                ch = Chain(dv, ops)
                ch.do(nc.vector.memset(zero_b[:, :], 0.0))
                nc.vector.memset(around[0:1, 0, 0:1], -1).then_inc(blank, 1)
                ch.do(nc.vector.memset(not_first[:, :, :], 1.0), wait=False)
                ch.do(nc.vector.memset(not_last[:, :, :], 1.0))
                ch.do(nc.vector.memset(not_first[:, :, 0:1], 0.0), wait=False)
                ch.do(nc.vector.memset(not_last[:, :, J - 1:J], 0.0), wait=False)
                ch.do(nc.vector.tensor_copy(iota_b[:, :], g.iota[:, :]), wait=False)
                dv.wait_ge(d_in, 6 * 16)
                ch.do(nc.vector.tensor_tensor(start[:, :, :], around[:, :, 1:J + 1], around[:, :, 0:J], ALU.not_equal), wait=False)
                ch.do(nc.vector.tensor_tensor(start_next[:, :, :], around[:, :, 2:J + 2], around[:, :, 1:J + 1], ALU.not_equal), wait=False)
                ch.do(nc.vector.tensor_copy(dst_i[:, :].rearrange("p (c j) -> p c j", j=J), around[:, :, 1:J + 1]))
                ch.do(nc.vector.tensor_copy(g.dstf[:, :], dst_i[:, :]), wait=False)
                ch.do(nc.vector.tensor_scalar(hi_i[:, :], dst_i[:, :], 7, None, ALU.arith_shift_right), wait=False)
                ch.do(nc.vector.tensor_scalar(lo_i[:, :], dst_i[:, :], P - 1, None, ALU.bitwise_and))
                ch.do(nc.vector.tensor_copy(flat(hi), hi_i[:, :]), wait=False)
                ch.do(nc.vector.tensor_copy(flat(lo), lo_i[:, :]), wait=False)
                ch.do(nc.vector.tensor_scalar(tmp[:, :, :], not_first[:, :, :], -1.0, 1.0, ALU.mult, ALU.add))
                ch.do(nc.vector.tensor_tensor(seen[:, :, :], tmp[:, :, :], start[:, :, :], ALU.max))
                ch.do(nc.vector.tensor_scalar(tmp[:, :, :], not_last[:, :, :], -1.0, 1.0, ALU.mult, ALU.add))
                ch.do(nc.vector.tensor_scalar(g.fwd_reset[:, :], flat(seen), -BIG, None, ALU.mult))
                ch.do(nc.vector.tensor_tensor(seen_b[:, :, :], tmp[:, :, :], start_next[:, :, :], ALU.max))
                ch.do(nc.vector.tensor_scalar(g.bwd_reset[:, :], flat(seen_b), -BIG, None, ALU.mult))
                ch.do(nc.vector.tensor_tensor_scan(flat(seen), flat(not_first), flat(start), 0.0, ALU.mult, ALU.max), wait=False)
                ch.do(nc.vector.tensor_tensor_scan(flat(seen_b)[:, ::-1], flat(not_last)[:, ::-1], flat(start_next)[:, ::-1], 0.0, ALU.mult, ALU.max))
                ch.do(nc.vector.tensor_scalar(g.fwd_block[:, :], flat(seen), -BIG, None, ALU.mult), wait=False)
                ch.do(nc.vector.tensor_scalar(g.bwd_block[:, :], flat(seen_b), -BIG, None, ALU.mult), wait=False)
                ch.do(nc.vector.tensor_copy(resets[:, 0, :], seen[:, :, J - 1]), wait=False)
                ch.do(nc.vector.tensor_tensor(resets[:, 1, :], seen[:, :, J - 1], start_next[:, :, J - 1], ALU.max))
                nc.vector.sem_inc(rs_t, 1)
                ch.do(nc.vector.memset(tile_at[0:1, :], float(NT - 1)))
                ch.do(nc.vector.tensor_copy(tile_at[0:1, 0:NC], hi_i[0:1, :].rearrange("p (c j) -> p c j", j=J)[:, :, 0]))
                ch.do(nc.vector.tensor_tensor(further[0:1, :], tile_at[0:1, 1:NC + 1], tile_at[0:1, 0:NC], ALU.subtract))
                ch.do(nc.vector.tensor_scalar(further[0:1, :], further[0:1, :], -1.0, 0.0, ALU.add, ALU.max))
                ch.do(nc.vector.tensor_tensor_scan(further_to[0:1, :], further[0:1, :], further[0:1, :], 0.0, ALU.add, ALU.bypass))
                info = lambda k: g.chunk_info[0:1, :, k]
                ch.do(nc.vector.tensor_copy(info(0), tile_at[0:1, 0:NC]), wait=False)
                ch.do(nc.vector.tensor_copy(info(2), tile_at[0:1, 1:NC + 1]), wait=False)
                ch.do(nc.vector.tensor_copy(info(4), further_to[0:1, :]), wait=False)
                ch.do(nc.vector.tensor_tensor(further_from[0:1, :], further_to[0:1, :], further[0:1, :], ALU.subtract))
                ch.do(nc.vector.tensor_scalar(further[0:1, :], tile_at[0:1, 0:NC], 1.0, float(NT - 1), ALU.add, ALU.min))
                ch.do(nc.vector.tensor_copy(info(1), further[0:1, :]), wait=False)
                ch.do(nc.vector.tensor_copy(info(3), further_from[0:1, :]), wait=False)
                ch.do(nc.vector.tensor_copy(first_lof[0:1, :], lo_i[0:1, :].rearrange("p (c j) -> p c j", j=J)[:, :, 0]))
                ch.do(nc.vector.tensor_tensor(first_hot[0:1, :, 0, :], g.iota[0:1, :].unsqueeze(1).to_broadcast([1, NC, P]),
                                              first_lof[0:1, :].unsqueeze(2).to_broadcast([1, NC, P]), ALU.is_equal))
                nc.vector.tensor_scalar(first_hot[0:1, :, 1, :], first_hot[0:1, :, 0, :], -1.0, 1.0, ALU.mult, ALU.add).then_inc(hot_row, 1)
                dv.wait_ge(rs_done, 2)
                nc.vector.tensor_scalar(reset_rows[:, :, :], p_rs[:, :, :], -BIG, None, ALU.mult).then_inc(rs_ready, 1)
                nc.vector.sem_inc(hot_free, 2)

                def hots(c, s):
                    dv.wait_ge(hot_free, c + 1)
                    nc.vector.tensor_tensor(hot_lo[:, s, :, :], iota_b[:, :].unsqueeze(1).to_broadcast([P, J, P]),
                                            lo[:, bass.ds(c, 1), :].rearrange("p a j -> p (a j)").unsqueeze(2).to_broadcast([P, J, P]), ALU.is_equal).then_inc(hot, 1)
                    nc.vector.tensor_tensor(hot_hi[:, s, :, :], iota_b[:, 0:NT].unsqueeze(1).to_broadcast([P, J, NT]),
                                            hi[:, bass.ds(c, 1), :].rearrange("p a j -> p (a j)").unsqueeze(2).to_broadcast([P, J, NT]), ALU.is_equal).then_inc(hot, 1)
                by_two(dv, NC, hots)
                dv.wait_ge(deg_done, 1)
                ch.do(nc.vector.tensor_copy(deg[:, :], p_deg[:, :]))
                ch.do(nc.vector.tensor_tensor_scan(first[:, :], deg[:, :], deg[:, :], 0.0, ALU.add, ALU.bypass))
                nc.vector.sem_inc(deg_ready, 1)
                dv.wait_ge(off_done, 1)
                ch.do(nc.vector.tensor_copy(offs[:, :], p_off[:, :]))
                ch.do(nc.vector.tensor_tensor(first[:, :], first[:, :], deg[:, :], ALU.subtract), wait=False)
                ch.do(nc.vector.tensor_scalar(none[:, :], deg[:, :], 0.0, 2.0 * EP, ALU.is_equal, ALU.mult))
                ch.do(nc.vector.scalar_tensor_tensor(out=first[:, :], in0=first[:, :], scalar=offs[:, 0:1], in1=none[:, :], op0=ALU.add, op1=ALU.add))
                nc.vector.sem_inc(deg_ready, 1)
                dv.wait_ge(t_done, 2)
                ch.do(nc.vector.tensor_copy(g.deg[:, :], p_t[:, 0, :]), wait=False)
                ch.do(nc.vector.tensor_copy(g.first_edge[:, :], p_t[:, 1, :]))
                ch.do(nc.vector.tensor_scalar(g.no_edges[:, :], g.deg[:, :], 0.0, None, ALU.is_equal))

            @block.tensor
            def _(pe):
                pe.wait_ge(rs_t, 1)
                for a in range(2):
                    nc.tensor.transpose(p_rs[:, a, :], resets[:, a, :], g.ident[:, :]).then_inc(rs_done, 1)
                pe.wait_ge(ops, 1)
                nc.tensor.matmul(p_deg[:, :], zero_b[:, 0:NT], zero_b[:, :], start=True, stop=False, skip_group_check=True)

                def count(c, s):
                    pe.wait_ge(hot, 2 * (c + 1))
                    for j in range(J):
                        last = nc.tensor.matmul(p_deg[:, :], hot_hi[:, s, j, :], hot_lo[:, s, j, :], start=False, stop=False, skip_group_check=True)
                    last.then_inc(hot_free, 1)
                by_two(pe, NC, count)
                nc.tensor.matmul(p_deg[:, :], zero_b[:, 0:NT], zero_b[:, :], start=False, stop=True, skip_group_check=True).then_inc(deg_done, 1)
                pe.wait_ge(deg_ready, 1)
                pe.wait_ge(tri_ready, 2)
                nc.tensor.matmul(p_off[:, :], tri[:, :], first[:, P - 1:P], start=True, stop=True).then_inc(off_done, 1)
                pe.wait_ge(deg_ready, 2)
                nc.tensor.transpose(p_t[:, 0, :], deg[:, :], g.ident[0:NT, 0:NT]).then_inc(t_done, 1)
                nc.tensor.transpose(p_t[:, 1, :], first[:, :], g.ident[0:NT, 0:NT]).then_inc(t_done, 1)


def setup(nc, a, out):
    g = Store()
    nc.keep = ExitStack()
    sb = lambda n, s, d=F32: nc.keep.enter_context(nc.sbuf_tensor(n, s, d))
    dr = lambda n, s, d=F32: nc.dram_tensor(n, s, d, kind="Internal").ap()
    g.a, g.out = a, out
    g.x_dram, g.src_dram, g.dst_dram = a["x"], a["src"], a["dst"]
    g.ident, g.ones, g.iota, g.iota_i = sb("ident", [P, P]), sb("ones", [P, P]), sb("iota", [P, P]), sb("iota_i", [P, P], I32)
    g.x = sb("x", [P, NT, D])
    g.src_idx = sb("src_idx", [P, NC * J], I32)
    g.dstf = sb("dstf", [P, NC * J])
    g.fwd_reset, g.bwd_reset, g.fwd_block, g.bwd_block = (
        sb(n, [P, NC * J]) for n in ("fwd_reset", "bwd_reset", "fwd_block", "bwd_block"))
    g.chunk_info = sb("chunk_info", [1, NC, INFO], I32)
    g.deg, g.no_edges, g.first_edge = sb("deg", [P, NT]), sb("no_edges", [P, NT]), sb("first_edge", [P, NT], I32)
    g.rstd, g.shift = sb("rstd", [P, NT]), sb("shift", [P, NT])
    g.agg = sb("agg", [P, NT, D + 16])
    g.table = dr("table", [NP, D + 8])
    g.inject8, g.inject4 = dr("inject8", [EP, 16]), dr("inject4", [EP, 8])
    g.resets_dram = dr("resets_dram", [NC, 2, P])
    g.first_hot_dram = dr("first_hot_dram", [1, NC * 2 * P])
    return g

R = 3


def layernorm_stats(nc, g):
    with Phase(nc, "ln") as ph:
        stats = ph.sb("stats", [P, NT, 6])
        mean, var, std, gap, eps = (ph.sb(n, [P, NT]) for n in ("mean", "var", "std", "gap", "eps"))
        st, ops, rooted = ph.sem("st"), ph.sem("ops"), ph.sem("rooted")
        with nc.Block() as block:
            @block.vector
            def _(dv):
                ch = Chain(dv, ops)
                ch.do(nc.vector.memset(eps[:, :], LN_EPS))
                with dv.Fori(0, NT // GROUP) as i:
                    for u in range(GROUP):
                        one = bass.ds(GROUP * i + u, 1)
                        nc.vector.bn_stats(stats[:, one, :].rearrange("p a d -> p (a d)"), g.x[:, one, :].rearrange("p a d -> p (a d)")).then_inc(st, 1)
                dv.wait_ge(st, NT)
                ch.do(nc.vector.tensor_tensor(mean[:, :], stats[:, :, 1], stats[:, :, 4], ALU.add))
                ch.do(nc.vector.tensor_tensor(gap[:, :], stats[:, :, 1], stats[:, :, 4], ALU.subtract))
                ch.do(nc.vector.tensor_scalar(mean[:, :], mean[:, :], 0.5, None, ALU.mult))
                ch.do(nc.vector.tensor_tensor(var[:, :], stats[:, :, 2], stats[:, :, 5], ALU.add))
                ch.do(nc.vector.scalar_tensor_tensor(out=gap[:, :], in0=gap[:, :], scalar=0.25, in1=gap[:, :], op0=ALU.mult, op1=ALU.mult))
                ch.do(nc.vector.scalar_tensor_tensor(out=var[:, :], in0=var[:, :], scalar=1.0 / D, in1=gap[:, :], op0=ALU.mult, op1=ALU.add))
                dv.wait_ge(rooted, 1)
                ch.do(nc.vector.reciprocal(g.rstd[:, :], std[:, :]))
                ch.do(nc.vector.scalar_tensor_tensor(out=g.shift[:, :], in0=mean[:, :], scalar=-1.0, in1=g.rstd[:, :], op0=ALU.mult, op1=ALU.mult))

            @block.scalar
            def _(ac):
                ac.wait_ge(ops, 7)
                nc.scalar.activation(std[:, :], var[:, :], ACT.Sqrt, bias=eps[:, 0:1]).then_inc(rooted, 1)


def normalised(nc, g, out, i):
    return nc.scalar.activation(out, g.x[:, bass.ds(i, 1), :].rearrange("p a d -> p (a d)"), ACT.Identity,
                                scale=g.rstd[:, bass.ds(i, 1)], bias=g.shift[:, bass.ds(i, 1)])



def ahead(eng, n, first, second):
    first(0, 0)
    with eng.Fori(0, n // 2) as i:
        first(2 * i + 1, 1)
        second(2 * i, 0)
        first(2 * i + 2, 0)
        second(2 * i + 1, 1)
    second(n - 1, 0)


class Products:

    def __init__(self, nc, g, ph, kb, kp, cols, from_x):
        self.nc, self.g, self.kb, self.kp, self.from_x = nc, g, kb, kp, from_x
        self.xn = ph.sb("xn", [P, 2, kb * kp])
        self.xt = ph.sb("xt", [P, 2, kb, P])
        self.p_x = [ph.ps(f"p_x{s}", [P, kb, P]) for s in range(2)]
        self.out = [ph.ps(f"out{s}", [P, cols]) for s in range(2)]
        self.normal, self.turned, self.copied, self.multiplied, self.taken = (
            ph.sem(n) for n in ("normal", "turned", "copied", "multiplied", "taken"))

    def scalar(self, ac):
        nc, kp = self.nc, self.kp
        nc.scalar.sem_inc(self.copied, 2)
        nc.scalar.sem_inc(self.normal, 2)

        def normalise(i, s):
            ac.wait_ge(self.turned, i + 1)
            if self.from_x:
                normalised(nc, self.g, self.xn[:, s, :], i).then_inc(self.normal, 1)
            else:
                f = self.g.agg[:, bass.ds(i, 1), 0:self.kb * kp].rearrange("p a d -> p (a d)")
                nc.scalar.activation(self.xn[:, s, :], f, ACT.Identity).then_inc(self.normal, 1)

        def copy(i, s):
            ac.wait_ge(self.turned, i + 3)
            ac.wait_ge(self.multiplied, i + 1)
            nc.scalar.activation(self.xt[0:kp, s, :, :], self.p_x[s][0:kp, :, :], ACT.Identity).then_inc(self.copied, 1)
        ahead(ac, NT, normalise, copy)

    def tensor(self, pe, rhs):
        nc, kp, kb = self.nc, self.kp, self.kb
        nc.tensor.sem_inc(self.turned, 2)
        nc.tensor.sem_inc(self.multiplied, 2)

        def turn(i, s):
            pe.wait_ge(self.normal, i + 3)
            pe.wait_ge(self.copied, i + 1)
            if kp < P:
                pe.nop(nofuse=True)
            for b in range(kb):
                last = nc.tensor.transpose(self.p_x[s][0:kp, b, :], self.xn[:, s, b * kp:(b + 1) * kp], self.g.ident[:, :])
            last.then_inc(self.turned, 1)

        def multiply(i, s):
            pe.wait_ge(self.copied, i + 3)
            pe.wait_ge(self.taken, i + 1)
            for b in range(kb):
                last = nc.tensor.matmul(self.out[s][:, :], self.xt[0:kp, s, b, :], rhs[0:kp, b, :], start=(b == 0), stop=(b == kb - 1))
            last.then_inc(self.multiplied, 1)
        ahead(pe, NT, turn, multiply)


def gat_table(nc, g, name, w, a_left, a_right, heads, din, out_in, table, inject, from_x):
    H, C, KB = heads, D // heads, -(-din // P)
    kp = min(din, P)
    cols = D + 3 * H
    if from_x:
        layernorm_stats(nc, g)
    with Phase(nc, name) as ph:
        w_in = ph.sb("w_in", [P, 2, D])
        w_tr = ph.sb("w_tr", [P, 2, D])
        rhs = ph.sb("rhs", [P, KB, cols])
        acol = ph.sb("acol", [P, 2, 2])
        who = ph.sb("who", [P, 2, H], I32)
        whof = ph.sb("whof", [P, 2, H])
        mask = ph.sb("mask", [P, 2, H])
        blockdiag = ph.sb("blockdiag", [P, 2, 2 * H])
        row = ph.sb("row", [P, 2, GROUP, cols])
        idx = ph.sb("idx", [P, 2, GROUP], I32)
        p_w = ph.ps("p_w", [P, 4, P])
        p_a = ph.ps("p_a", [P, KB, 2 * H])
        prod = Products(nc, g, ph, KB, kp, cols, from_x)
        loaded, seq, ops, wt, wa = (ph.sem(n) for n in ("loaded", "seq", "ops", "wt", "wa"))
        idx_ready, weights = ph.sem("idx_ready"), ph.sem("weights")
        stored = [ph.sem(f"stored{s}") for s in range(2)]
        scattered = [ph.sem(f"scattered{s}") for s in range(2)]
        OB = 2 if out_in else KB
        NG = NT // GROUP

        def in_groups(eng, body):
            body(0, 0)
            body(1, 1)
            with eng.Fori(1, NG // 2) as i:
                body(2 * i, 0)
                body(2 * i + 1, 1)
            body(NG - 1, 0)
        rows = P if out_in else kp
        with nc.Block() as block:
            @block.sync
            def _(sp):
                sp.dma_start(w_in[0:rows, 0:OB, :], w.rearrange("(b p) n -> p b n", p=rows)).then_inc(loaded, 16)
                for side, a in enumerate((a_left, a_right)):
                    for ob in range(2):
                        sp.dma_start(acol[:, side, ob:ob + 1], dram_view(a, ob * P, [[1, P], [1, 1]])).then_inc(loaded, 16)

                def store(n, s):
                    sp.wait_ge(prod.taken, GROUP * n + GROUP + 2)
                    sp.dma_start(table[bass.ds(n * GROUP * P, GROUP * P), :].rearrange("(t p) d -> p t d", p=P), row[:, s, :, 0:D + H]).then_inc(stored[s], 16)
                by_two(sp, NG, store)
                sp.wait_ge(stored[0], 16 * (NG // 2 + 1))
                sp.wait_ge(stored[1], 16 * (NG // 2))

            @block.gpsimd
            def _(gp):
                nc.gpsimd.iota(who[:, :, :], [[P, 2], [-C, H]], base=0, channel_multiplier=1).then_inc(seq, 1)

                def scatter(n, s):
                    if not (isinstance(n, int) and n < 2):
                        gp.wait_ge(scattered[s], 16 * GROUP * ((n - s) // 2))
                    nc.gpsimd.tensor_copy(idx[:, s, :], g.first_edge[:, bass.ds(n * GROUP, GROUP)]).then_inc(idx_ready, 1)
                    gp.wait_ge(idx_ready, n + 1)
                    for u in range(GROUP):
                        gp.wait_ge(prod.taken, GROUP * n + u + 3)
                        gp.nop(nofuse=True)
                        gp.indirect_dma_start(inject, bass.IndirectOffsetOnAxis(idx[:, s, u:u + 1], 0), row[:, s, u, D + H:D + 3 * H], None,
                                              bounds_check=EP - 1, oob_is_err=False).then_inc(scattered[s], 16)
                in_groups(gp, scatter)
                gp.wait_ge(scattered[0], 16 * GROUP * (NG // 2 + 1))
                gp.wait_ge(scattered[1], 16 * GROUP * (NG // 2))

            @block.vector
            def _(dv):
                ch = Chain(dv, ops)
                dv.wait_ge(seq, 1)
                ch.do(nc.vector.tensor_copy(whof[:, :, :], who[:, :, :]))
                ch.do(nc.vector.tensor_scalar(mask[:, :, :], whof[:, :, :], 0.0, None, ALU.is_ge))
                ch.do(nc.vector.scalar_tensor_tensor(out=mask[:, :, :], in0=whof[:, :, :], scalar=float(C), in1=mask[:, :, :], op0=ALU.is_lt, op1=ALU.mult))
                dv.wait_ge(loaded, 5 * 16)
                for side in range(2):
                    ch.do(nc.vector.tensor_tensor(blockdiag[:, :, side * H:(side + 1) * H], mask[:, :, :],
                                                  acol[:, side, :].unsqueeze(2).to_broadcast([P, 2, H]), ALU.mult))
                nc.vector.sem_inc(weights, 1)
                dv.wait_ge(wt, 4 if KB == 2 else 2)
                if out_in:
                    for ob in range(2):
                        for ib in range(2):
                            ch.do(nc.vector.tensor_copy(rhs[:, ib, ob * P:(ob + 1) * P], p_w[:, 2 * ob + ib, :]))
                else:
                    for ib in range(KB):
                        for ob in range(2):
                            ch.do(nc.vector.tensor_copy(w_tr[:, ob, ib * kp:(ib + 1) * kp], p_w[:, 2 * ib + ob, 0:kp]))
                        ch.do(nc.vector.tensor_copy(rhs[0:kp, ib, 0:D], w_in[0:kp, ib, :]))
                nc.vector.sem_inc(weights, 1)
                dv.wait_ge(wa, KB)
                for ib in range(KB):
                    ch.do(nc.vector.tensor_copy(rhs[0:kp, ib, D:D + 2 * H], p_a[0:kp, ib, :]))
                    ch.do(nc.vector.tensor_copy(rhs[0:kp, ib, D + 2 * H:cols], p_a[0:kp, ib, 0:H]))
                nc.vector.sem_inc(weights, 1)

                nc.vector.sem_inc(prod.taken, 2)

                def take(n, s):
                    if not (isinstance(n, int) and n < 2):
                        dv.wait_ge(stored[s], 16 * ((n - s) // 2))
                        dv.wait_ge(scattered[s], 16 * GROUP * ((n - s) // 2))
                    for u in range(GROUP):
                        i = n * GROUP + u
                        dv.wait_ge(prod.multiplied, i + 3)
                        nc.vector.tensor_copy(row[:, s, u, :], prod.out[(s * GROUP + u) % 2][:, :]).then_inc(prod.taken, 1)
                in_groups(dv, take)

            @block.scalar
            def _(ac):
                prod.scalar(ac)

            @block.tensor
            def _(pe):
                pe.wait_ge(loaded, 5 * 16)
                for a in range(OB):
                    for b in range(2):
                        nc.tensor.transpose(p_w[:, 2 * a + b, 0:rows], w_in[0:rows, a, b * P:(b + 1) * P], g.ident[0:rows, 0:rows]).then_inc(wt, 1)
                pe.wait_ge(weights, 2)
                w_oi = w_in if out_in else w_tr
                for ib in range(KB):
                    for ob in range(2):
                        last = nc.tensor.matmul(p_a[0:kp, ib, :], w_oi[:, ob, ib * kp:(ib + 1) * kp], blockdiag[:, ob, :], start=(ob == 0), stop=(ob == 1))
                    last.then_inc(wa, 1)
                pe.wait_ge(weights, 3)
                prod.tensor(pe, rhs)


ATT = ("right", "left", "forward", "carry_old", "carry", "blocked", "merged", "backward", "carry_back", "blocked_back", "maximum",
       "z_left", "z_self", "z_maximum", "z_old", "leaky", "less", "less_old", "clamped", "weighted")


TRANSPOSES = (3, 6, 9, 12)


def gather_pass(nc, g, name, table, width, heads=0, inject=None):
    H = heads
    C = D // H if H else 0
    W = width + 2 * H
    HJ, Q = H * J, 2 * H
    n_att = len(ATT)
    step = {n: k + 1 for k, n in enumerate(ATT)}
    with Phase(nc, name) as ph:
        rows = ph.sb("rows", [P, R, J, W])
        idx = ph.sb("idx", [P, R, J], I32)
        hot = ph.sb("hot", [P, J, P])
        near = ph.sb("near", [P, 3, J])
        base = ph.sb("base", [P, NT + 1])
        base_i = ph.sb("base_i", [P, NT + 1], I32)
        p_sum = [ph.ps(f"p_sum{k}", [P, W]) for k in range(3)]
        copied, seq, setup_v, halves, used, near_ready, added, g_free = (
            ph.sem(n) for n in ("copied", "seq", "setup_v", "halves", "used", "near_ready", "added", "g_free"))
        got = [ph.sem(f"got{s}") for s in range(R)]
        if H:
            inj = ph.sb("inj", [P, R, J, Q])
            reset = ph.sb("reset", [Q, R, 2, P])
            first_hot = ph.sb("first_hot", [1, R, 2, P])
            v, a, tmp = ph.sb("v", [P, Q, J]), ph.sb("a", [P, Q, J]), ph.sb("tmp", [P, Q, J])
            b, m = ph.sb("b", [P, H, J]), ph.sb("m", [P, H, J])
            z, e = ph.sb("z", [P, 3 * HJ + H]), ph.sb("e", [P, 2 * HJ + H])
            carry = ph.sb("carry", [Q, R, P + 1])
            back = ph.sb("back", [H, P + 1])
            resets_f, resets_b = ph.sb("resets_f", [P, Q, J]), ph.sb("resets_b", [P, H, J])
            fold = ph.sb("fold", [1, H])
            p_1, p_3 = ph.ps("p_1", [Q, P]), ph.ps("p_3", [H, P])
            p_2, p_4 = ph.ps("p_2", [P, Q]), ph.ps("p_4", [P, H])
            p_f = ph.ps("p_f", [P, H])
            att, turned, exped, factor, scaled, spread = (ph.sem(n) for n in ("att", "turned", "exped", "factor", "scaled", "spread"))
            side = [ph.sem(f"side{s}") for s in range(R)]

        def chunks(eng, body):
            with eng.Fori(0, NC // R) as i:
                for s in range(R):
                    body(R * i + s, s)
            body(NC - 1, 0)

        def turns_of(eng, first, body):
            first(0, 0)
            with eng.Fori(0, NC // R - 1) as i:
                for s in range(R):
                    body(R * i + s, s, 2)
            for c in range(NC - 1 - R, NC):
                body(c, c % R, min(2, NC - 1 - c))
        assert NC % R == 1

        def info(engine, c):
            of = lambda k, n: g.chunk_info[0:1, bass.ds(c, 1), k:k + n].rearrange("p a k -> p (a k)")
            return (*registers(nc, engine, of(0, 3), NT - 1, waited=False), *registers(nc, engine, of(3, 2), NT - 1, waited=True))

        with nc.Block() as block:
            @block.sync
            def _(sp):
                def load(c, s):
                    with_c = bass.ds(c, 1)
                    sp.wait_ge(g_free, c + 1)
                    sp.dma_start(inj[:, s, :, :], inject[bass.ds(c * CH, CH), :].rearrange("(p j) q -> p j q", j=J)).then_inc(side[s], 16)
                    sp.dma_start(reset[:, s, :, :].rearrange("q a p -> q (a p)"),
                                 g.resets_dram[with_c, :, :].rearrange("c a p -> c (a p)").to_broadcast([Q, 2 * P])).then_inc(side[s], 16)
                    sp.dma_start(first_hot[0:1, s, :, :].rearrange("o a p -> o (a p)"), g.first_hot_dram[0:1, bass.ds(c * 2 * P, 2 * P)]).then_inc(side[s], 16)
                if H:
                    chunks(sp, load)

            @block.gpsimd
            def _(gp):
                nc.gpsimd.iota(base_i[:, :], [[P, NT + 1]], base=0, channel_multiplier=0).then_inc(seq, 1)

                def gather(c, s):
                    gp.wait_ge(g_free, c + 1)
                    nc.gpsimd.tensor_copy(idx[:, s, :], g.src_idx[:, bass.ds(c * J, J)]).then_inc(copied, 1)
                    gp.wait_ge(copied, c + 1)
                    gp.nop(nofuse=True)
                    for j in range(J):
                        gp.indirect_dma_start(rows[:, s, j, 0:width + H], None, table, bass.IndirectOffsetOnAxis(idx[:, s, j:j + 1], 0)).then_inc(got[s], 16)
                chunks(gp, gather)

            @block.vector
            def _(dv):
                V = nc.vector
                once = Chain(dv, setup_v)
                dv.wait_ge(seq, 1)
                once.do(V.tensor_copy(base[:, :], base_i[:, :]))
                once.do(V.memset(g.agg[:, :, 0:W], 0.0))
                V.sem_inc(added, 2)
                if H:
                    V.sem_inc(scaled, 2)
                    once.do(V.memset(z[:, :], 0.0))
                    once.do(V.memset(e[:, :], 0.0))
                    once.do(V.memset(carry[:, R - 1, P:P + 1], -BIG))
                    once.do(V.memset(back[:, P:P + 1], -BIG))
                grid = lambda t, n: t.rearrange("p (q j) -> p q j", q=n)

                def attention(c, s, started=False):
                    n = Chain(dv, att, c * n_att)
                    if started:
                        n.n = step["carry_old"]

                    def do(what, ins):
                        assert ATT[n.n] == what
                        n.do(ins)
                    edges = bass.ds(c * J, J)
                    over = lambda t, q: t[:, edges].unsqueeze(1).to_broadcast([P, q, J])
                    right, own = inj[:, s, :, 0:H].rearrange("p j h -> p h j"), inj[:, s, :, H:Q].rearrange("p j h -> p h j")
                    left = rows[:, s, :, width:width + H].rearrange("p j h -> p h j")

                    def start():
                        dv.wait_ge(side[s], c_uses(c, s, 48))
                        do("right", V.tensor_copy(v[:, 0:H, :], right))
                        dv.wait_ge(got[s], c_uses(c, s, 16 * J))
                        do("left", V.tensor_tensor(v[:, H:Q, :], left, own, ALU.max))
                        dv.wait_ge(spread, 2 * c + 2)
                        do("forward", V.tensor_tensor_scan(a[:, :, :].rearrange("p q j -> p (q j)"), resets_f[:, :, :].rearrange("p q j -> p (q j)"), v[:, :, :].rearrange("p q j -> p (q j)"), -BIG, ALU.add, ALU.max))
                        do("carry_old", V.tensor_copy(carry[:, s, 0:1], carry[:, (s - 1) % R, P:P + 1]))

                    def carried():
                        dv.wait_ge(turned, 4 * c + 1)
                        do("carry", V.tensor_tensor_scan(carry[:, s, 1:P + 1], reset[:, s, 0, :], p_1[:, :], carry[:, s, 0:1], ALU.add, ALU.max))

                    def backward():
                        dv.wait_ge(turned, 4 * c + 2)
                        do("blocked", V.tensor_tensor(tmp[:, :, :], over(g.fwd_block, Q), p_2[:, :].unsqueeze(2).to_broadcast([P, Q, J]), ALU.add))
                        do("merged", V.tensor_tensor(a[:, :, :], a[:, :, :], tmp[:, :, :], ALU.max))
                        do("backward", V.tensor_tensor_scan(b[:, :, :].rearrange("p q j -> p (q j)")[:, ::-1], resets_b[:, :, :].rearrange("p q j -> p (q j)")[:, ::-1],
                                                            a[:, H:Q, :].rearrange("p q j -> p (q j)")[:, ::-1], -BIG, ALU.add, ALU.max))

                    def carried_back():
                        dv.wait_ge(turned, 4 * c + 3)
                        do("carry_back", V.tensor_tensor_scan(back[:, 0:P][:, ::-1], reset[0:H, s, 1, ::-1], p_3[:, ::-1], -BIG, ALU.add, ALU.max))

                    def exponents():
                        dv.wait_ge(turned, 4 * c + 4)
                        do("blocked_back", V.tensor_tensor(tmp[:, 0:H, :], over(g.bwd_block, H), p_4[:, :].unsqueeze(2).to_broadcast([P, H, J]), ALU.add))
                        do("maximum", V.tensor_tensor(m[:, :, :], b[:, :, :], tmp[:, 0:H, :], ALU.max))
                        do("z_left", V.tensor_tensor(grid(z[:, 0:HJ], H), a[:, 0:H, :], left, ALU.add))
                        do("z_self", V.tensor_tensor(grid(z[:, HJ:2 * HJ], H), a[:, 0:H, :], own, ALU.add))
                        do("z_maximum", V.tensor_tensor(z[:, 2 * HJ:3 * HJ], a[:, 0:H, :].rearrange("p q j -> p (q j)"), m[:, :, :].rearrange("p q j -> p (q j)"), ALU.add))
                        do("z_old", V.tensor_tensor(z[0:1, 3 * HJ:], a[0:1, 0:H, 0], p_2[0:1, H:Q], ALU.add))
                        do("leaky", V.scalar_tensor_tensor(out=z[:, :], in0=z[:, :], scalar=0.2, in1=z[:, :], op0=ALU.mult, op1=ALU.max))
                        if not (isinstance(c, int) and c == 0):
                            dv.wait_ge(exped, 2 * c)
                        do("less", V.tensor_tensor(grid(e[:, 0:2 * HJ], 2), grid(z[:, 0:2 * HJ], 2), z[:, 2 * HJ:3 * HJ].unsqueeze(1).to_broadcast([P, 2, HJ]), ALU.subtract))
                        do("less_old", V.tensor_tensor(e[0:1, 2 * HJ:], z[0:1, 3 * HJ:], grid(z[0:1, 2 * HJ:3 * HJ], H)[:, :, 0], ALU.subtract))
                        do("clamped", V.tensor_scalar(e[0:1, 2 * HJ:], e[0:1, 2 * HJ:], 0.0, None, ALU.min))

                    def weighted():
                        dv.wait_ge(exped, 2 * c + 2)
                        w = rows[:, s, :, width:width + H].unsqueeze(3).to_broadcast([P, J, H, C])
                        x = rows[:, s, :, 0:width].rearrange("p j (h c) -> p j h c", h=H)
                        do("weighted", V.tensor_tensor(x, x, w, ALU.mult))
                    return start, carried, backward, carried_back, exponents, weighted

                def make_near(c, k, kind, nth):
                    V.tensor_scalar(near[:, kind, :], g.dstf[:, bass.ds(c * J, J)], base[:, bass.ds(k, 1)], None, ALU.subtract).then_inc(near_ready, 1)
                    dv.wait_ge(near_ready, nth + 1)

                def make_hot(kind, half, nth):
                    js = slice(half * J // 2, (half + 1) * J // 2)
                    dv.wait_ge(used, 2 * nth + half + 1)
                    V.tensor_tensor(hot[:, js, :], g.iota[:, :].unsqueeze(1).to_broadcast([P, J // 2, P]),
                                    near[:, kind, js].unsqueeze(2).to_broadcast([P, J // 2, P]), ALU.is_equal).then_inc(halves, 1)

                def add(kind, k, nth_sum):
                    into = g.agg[:, bass.ds(k, 1), 0:W].rearrange("p a w -> p (a w)")
                    V.tensor_tensor(into, into, p_sum[kind][:, :], ALU.add).then_inc(added, 1)
                    dv.wait_ge(added, nth_sum + 3)

                def first(c, s):
                    if H:
                        for part in attention(c, s):
                            part()
                    dv.nop(nofuse=True)
                    one, = registers(nc, DVE, g.chunk_info[0:1, c, 0:1], NT - 1, waited=False)
                    make_near(c, one, 0, 0)
                    make_hot(0, 0, 0)
                    make_hot(0, 1, 0)
                    if H:
                        attention(1, 1)[0]()

                def turn(c, s, left):
                    last = left == 0
                    dv.nop(nofuse=True)
                    one, two, after, before, upto = info(DVE, c)
                    nth = 2 * c + before
                    nxt = (s + 1) % R
                    if H and not last:
                        _, carried, backward, carried_back, exponents, weighted = attention(c + 1, nxt, started=True)
                    if H and not last:
                        carried()
                    make_near(c, one + 1, 1, nth + 1)
                    if H and not last:
                        backward()
                    if H:
                        dv.wait_ge(factor, c + 1)
                        kept = g.agg[:, bass.ds(one, 1), 0:D].rearrange("p a (h c) -> p (a h) c", h=H)
                        V.tensor_tensor(kept, kept, p_f[:, :].unsqueeze(2).to_broadcast([P, H, C]), ALU.mult).then_inc(scaled, 1)
                        kept = g.agg[:, bass.ds(one, 1), D:D + Q].rearrange("p a (b h) -> p (a b) h", h=H)
                        V.tensor_tensor(kept, kept, p_f[:, :].unsqueeze(1).to_broadcast([P, 2, H]), ALU.mult).then_inc(scaled, 1)
                        dv.wait_ge(scaled, 2 * c + 4)
                    make_hot(1, 0, nth + 1)
                    if H and not last:
                        carried_back()
                        exponents()
                    make_hot(1, 1, nth + 1)
                    dv.wait_ge(used, 2 * nth + 4)
                    add(0, one, nth)
                    if H and not last:
                        weighted()
                    dv.nop(nofuse=True)
                    with dv.If(one + 1 < after):
                        with dv.Fori(0, after - one - 1) as r:
                            k = nc.s_assert_within(one + 2 + r, 2, NT - 1, skip_runtime_bounds_check_because="the loop ends at tile `after`")
                            q = nth + 2 + r
                            make_near(c, k, 2, q)
                            make_hot(2, 0, q)
                            make_hot(2, 1, q)
                            dv.wait_ge(used, 2 * q + 4)
                            add(2, k, q - 1)
                            dv.nop(nofuse=True)
                    if not last:
                        nth_next = 2 * c + 2 + upto
                        if not H:
                            dv.wait_ge(got[nxt], c_uses(c + 1, nxt, 16 * J))
                        make_near(c + 1, after, 0, nth_next)
                        make_hot(0, 0, nth_next)
                        make_hot(0, 1, nth_next)
                    if H and left == 2:
                        attention(c + 2, (s + 2) % R)[0]()
                    dv.wait_ge(used, 2 * nth + 6)
                    add(1, two, 2 * c + 1 + upto)
                    dv.nop(nofuse=True)
                turns_of(dv, first, turn)

            @block.scalar
            def _(ac):
                def exps(c, s):
                    if not (isinstance(c, int) and c == 0):
                        ac.wait_ge(att, (c - 1) * n_att + step["backward"])
                    for out, q, t in ((resets_f, Q, g.fwd_reset), (resets_b, H, g.bwd_reset)):
                        nc.scalar.activation(out[:, :, :], t[:, bass.ds(c * J, J)].unsqueeze(1).to_broadcast([P, q, J]), ACT.Identity).then_inc(spread, 1)
                    ac.wait_ge(att, c * n_att + step["clamped"])
                    if not (isinstance(c, int) and c == 0):
                        ac.wait_ge(factor, c)
                    nc.scalar.activation(fold[0:1, :], e[0:1, 2 * HJ:], ACT.Exp).then_inc(exped, 1)
                    nc.scalar.activation(rows[:, s, :, width:W].rearrange("p j (b h) -> p b h j", b=2), e[:, 0:2 * HJ].rearrange("p (b h j) -> p b h j", b=2, h=H), ACT.Exp).then_inc(exped, 1)
                if H:
                    exps(0, 0)
                    with ac.Fori(0, NC // R) as i:
                        for s in range(R):
                            exps(R * i + s + 1, (s + 1) % R)

            @block.tensor
            def _(pe):
                nc.tensor.sem_inc(used, 2)
                nc.tensor.sem_inc(g_free, R)

                def turn_of(c, s, k):
                    out, src, rows_in, ready = ((p_1, a[:, :, J - 1], P, "forward"), (p_2, carry[:, s, 0:P], Q, "carry"),
                                                (p_3, b[:, :, 0], P, "backward"), (p_4, back[:, 1:P + 1], H, "carry_back"))[k]
                    pe.wait_ge(att, c * n_att + step[ready])
                    pe.nop(nofuse=True)
                    nc.tensor.transpose(out[:, :], src, g.ident[0:rows_in, 0:rows_in]).then_inc(turned, 1)

                def sums(kind, s, half, nth, between=None):
                    pe.wait_ge(halves, 2 * nth + half + 1)
                    for j in range(half * J // 2, (half + 1) * J // 2):
                        if between and j in TRANSPOSES:
                            between(TRANSPOSES.index(j))
                        last = nc.tensor.matmul(p_sum[kind][:, :], hot[:, j, :], rows[:, s, j, :], start=(j == 0), stop=(j == J - 1))
                    last.then_inc(used, 1)

                def first(c, s):
                    if H:
                        for k in range(4):
                            turn_of(c, s, k)

                def turn(c, s, left):
                    nxt, last = (s + 1) % R, left == 0
                    t = (lambda k: turn_of(c + 1, nxt, k)) if H and not last else (lambda k: None)
                    pe.nop(nofuse=True)
                    one, two, after, before, upto = info(PE, c)
                    nth = 2 * c + before
                    if H:
                        pe.wait_ge(exped, 2 * c + 2)
                        pe.wait_ge(scaled, 2 * c + 2)
                        nc.tensor.matmul(p_f[:, :], first_hot[0:1, s, 0, :], fold[0:1, :], start=True, stop=False)
                        nc.tensor.matmul(p_f[:, :], first_hot[0:1, s, 1, :], g.ones[0:1, 0:H], start=False, stop=True).then_inc(factor, 1)
                        pe.wait_ge(att, c * n_att + n_att)
                    else:
                        pe.wait_ge(got[s], c_uses(c, s, 16 * J))
                    pe.wait_ge(added, nth + 1)
                    sums(0, s, 0, nth, t)
                    sums(0, s, 1, nth, t)
                    pe.wait_ge(added, nth + 2)
                    for half in range(2):
                        sums(1, s, half, nth + 1)
                    with pe.If(one + 1 < after):
                        with pe.Fori(0, after - one - 1) as r:
                            q = nth + 2 + r
                            pe.wait_ge(added, q + 1)
                            for half in range(2):
                                sums(2, s, half, q)
                    pe.wait_ge(used, 2 * (2 * c + 2 + upto) + 2)
                    nc.tensor.sem_inc(g_free, 1)
                turns_of(pe, first, turn)


def c_uses(c, s, n):
    return n * (c // R + 1) if isinstance(c, int) else n * ((c - s) // R + 1)


def gat_finish(nc, g, name, table, heads, eps):
    H, C = heads, D // heads
    with Phase(nc, name) as ph:
        own = ph.sb("own", [P, 2, GROUP, D])
        total, inv = ph.sb("total", [P, NT, H]), ph.sb("inv", [P, NT, H])
        seq = ph.sem("seq")
        prod, mixed, scaled = ph.sem("prod"), ph.sem("mixed"), ph.sem("scaled")
        loaded = [ph.sem(f"loaded{s}") for s in range(2)]
        with nc.Block() as block:
            @block.sync
            def _(sp):
                for n in range(NT // GROUP):
                    if n >= 2:
                        sp.wait_ge(mixed, n - 1)
                    sp.dma_start(own[:, n % 2, :, :], table[n * GROUP * P:(n + 1) * GROUP * P, 0:D].rearrange("(t p) d -> p t d", p=P)).then_inc(loaded[n % 2], 16)

            @block.vector
            def _(dv):
                ch = Chain(dv, seq)
                weights, selfs = g.agg[:, :, D:D + H], g.agg[:, :, D + H:D + 2 * H]
                ch.do(nc.vector.tensor_tensor(selfs, selfs, g.no_edges[:, :].unsqueeze(2).to_broadcast([P, NT, H]), ALU.add))
                ch.do(nc.vector.tensor_tensor(total[:, :, :], weights, selfs, ALU.add))
                ch.do(nc.vector.tensor_scalar(total[:, :, :], total[:, :, :], eps, None, ALU.add))
                ch.do(nc.vector.reciprocal(inv[:, :, :], total[:, :, :]))

                heads_of = lambda t: t.rearrange("p a (h c) -> p a h c", h=H)
                wide = lambda t: t.unsqueeze(3).to_broadcast([P, GROUP, H, C])
                for n in range(NT // GROUP):
                    dv.wait_ge(loaded[n % 2], 16 * (n // 2 + 1))
                    group = slice(n * GROUP, (n + 1) * GROUP)
                    o, sums = own[:, n % 2, :, :], g.agg[:, group, 0:D]
                    nc.vector.tensor_tensor(heads_of(o), heads_of(o), wide(g.agg[:, group, D + H:D + 2 * H]), ALU.mult).then_inc(prod, 1)
                    dv.wait_ge(prod, n + 1)
                    nc.vector.tensor_tensor(sums, sums, o, ALU.add).then_inc(mixed, 1)
                    dv.wait_ge(mixed, n + 1)
                    nc.vector.tensor_tensor(heads_of(sums), heads_of(sums), wide(inv[:, group, :]), ALU.mult).then_inc(scaled, 1)


def turned_weights(nc, g, w, name):
    with Phase(nc, name) as ph:
        w_in = ph.sb("w_in", [P, 2, D])
        p_w = ph.ps("p_w", [P, 4, P])
        loaded, turned, placed = ph.sem("loaded"), ph.sem("turned"), ph.sem("placed")
        with nc.Block() as block:
            @block.sync
            def _(sp):
                sp.dma_start(w_in[:, :, :], w.rearrange("(b p) n -> p b n", p=P)).then_inc(loaded, 16)

            @block.tensor
            def _(pe):
                pe.wait_ge(loaded, 16)
                for ob in range(2):
                    for ib in range(2):
                        nc.tensor.transpose(p_w[:, 2 * ob + ib, :], w_in[:, ob, ib * P:(ib + 1) * P], g.ident[:, :]).then_inc(turned, 1)

            @block.vector
            def _(dv):
                dv.wait_ge(turned, 4)
                for ob in range(2):
                    for ib in range(2):
                        nc.vector.tensor_copy(g.wt[:, ib, ob * P:(ob + 1) * P], p_w[:, 2 * ob + ib, :]).then_inc(placed, 1)
                dv.wait_ge(placed, 4)


def tile_of(t, i, n):
    return t[:, bass.ds(i, 1), 0:n].rearrange("p a d -> p (a d)")


def x_plus_product(nc, g, name, rhs, bias=None):
    layernorm_stats(nc, g)
    with Phase(nc, name) as ph:
        prod = Products(nc, g, ph, 2, P, D, True)
        wide = ph.sb("wide", [P, D])
        loaded, biased = ph.sem("loaded"), ph.sem("biased")
        with nc.Block() as block:
            @block.sync
            def _(sp):
                if bias is not None:
                    sp.dma_start(wide[:, :], bias.rearrange("(o n) -> o n", o=1).to_broadcast([P, D])).then_inc(loaded, 16)

            @block.scalar
            def _(ac):
                prod.scalar(ac)

            @block.tensor
            def _(pe):
                prod.tensor(pe, rhs)

            @block.vector
            def _(dv):
                nc.vector.sem_inc(prod.taken, 2)
                if bias is not None:
                    dv.wait_ge(loaded, 16)

                def take(i, s):
                    x = tile_of(g.x, i, D)
                    dv.wait_ge(prod.multiplied, i + 3)
                    nc.vector.tensor_tensor(x, x, prod.out[s][:, :], ALU.add).then_inc(prod.taken, 1)
                    if bias is not None:
                        dv.wait_ge(prod.taken, i + 3)
                        nc.vector.tensor_tensor(x, x, wide[:, :], ALU.add).then_inc(biased, 1)
                by_two(dv, NT, take)


def ln_rows(nc, g, name, table=None):
    layernorm_stats(nc, g)
    with Phase(nc, name) as ph:
        row = ph.sb("row", [P, 2, GROUP, D])
        made, added = ph.sem("made"), ph.sem("added")
        stored = [ph.sem(f"stored{s}") for s in range(2)]
        with nc.Block() as block:
            @block.scalar
            def _(ac):
                for n in range(NT // GROUP):
                    if n >= 2:
                        if table is not None:
                            ac.wait_ge(stored[n % 2], 16 * (n // 2))
                        else:
                            ac.wait_ge(added, n - 1)
                    for u in range(GROUP):
                        normalised(nc, g, row[:, n % 2, u, :], n * GROUP + u).then_inc(made, 1)

            @block.sync
            def _(sp):
                if table is not None:
                    for n in range(NT // GROUP):
                        sp.wait_ge(made, GROUP * (n + 1))
                        sp.dma_start(table[n * GROUP * P:(n + 1) * GROUP * P, :].rearrange("(t p) d -> p t d", p=P), row[:, n % 2, :, :]).then_inc(stored[n % 2], 16)
                    for s in range(2):
                        sp.wait_ge(stored[s], 16 * len(range(s, NT // GROUP, 2)))

            @block.vector
            def _(dv):
                if table is None:
                    for n in range(NT // GROUP):
                        dv.wait_ge(made, GROUP * (n + 1))
                        sums = g.agg[:, n * GROUP:(n + 1) * GROUP, 0:D]
                        nc.vector.tensor_tensor(sums, sums, row[:, n % 2, :, :], ALU.add).then_inc(added, 1)


def agg_product(nc, g, name, rhs):
    with Phase(nc, name) as ph:
        prod = Products(nc, g, ph, 2, P, D, False)
        with nc.Block() as block:
            @block.scalar
            def _(ac):
                prod.scalar(ac)

            @block.tensor
            def _(pe):
                prod.tensor(pe, rhs)

            @block.vector
            def _(dv):
                nc.vector.sem_inc(prod.taken, 2)

                def take(i, s):
                    dv.wait_ge(prod.multiplied, i + 3)
                    nc.vector.tensor_copy(tile_of(g.agg, i, D), prod.out[s][:, :]).then_inc(prod.taken, 1)
                by_two(dv, NT, take)


def batch_norm(nc, g, name, cols, bias, gamma, beta, into_x, elu=False, gcn=False):
    EPS = 1e-5
    NG = NT // GROUP
    with Phase(nc, name) as ph:
        wide = ph.sb("wide", [P, 3, cols])
        mean, scale, eps = ph.sb("mean", [P, cols]), ph.sb("scale", [P, cols]), ph.sb("eps", [P, 1])
        sq = ph.sb("sq", [P, 2, GROUP, cols])
        y = ph.sb("y", [P, 2, GROUP, cols])
        low = ph.sb("low", [P, 2, GROUP, cols])
        p_m, p_v = ph.ps("p_m", [P, cols]), ph.ps("p_v", [P, cols])
        loaded, ops, biased, summed, less, squared, var_done, rooted, done, lows, exped = (
            ph.sem(n) for n in ("loaded", "ops", "biased", "summed", "less", "squared", "var_done", "rooted", "done", "lows", "exped"))
        tiles = lambda n: slice(n * GROUP, (n + 1) * GROUP)
        each = lambda t: t.unsqueeze(1).to_broadcast([P, GROUP, cols])
        steps_per = 4 if gcn else 1
        with nc.Block() as block:
            @block.sync
            def _(sp):
                for n, v in enumerate((bias, gamma, beta)):
                    sp.dma_start(wide[:, n, :], v.rearrange("(o n) -> o n", o=1).to_broadcast([P, cols])).then_inc(loaded, 16)

            @block.tensor
            def _(pe):
                def add_up(out, tile_of_group, n, sem):
                    for u in range(GROUP):
                        t = n * GROUP + u
                        k = LAST if t == NT - 1 else P
                        last = nc.tensor.matmul(out[:, :], g.ones[0:k, :], tile_of_group(u, k), start=(t == 0), stop=(t == NT - 1))
                    last.then_inc(sem, 1)
                for n in range(NG):
                    pe.wait_ge(biased, steps_per * (n + 1))
                    add_up(p_m, lambda u, k: g.agg[0:k, n * GROUP + u, 0:cols], n, summed)
                for n in range(NG):
                    pe.wait_ge(squared, n + 1)
                    add_up(p_v, lambda u, k: sq[0:k, n % 2, u, :], n, var_done)

            @block.scalar
            def _(ac):
                for n in range(NG):
                    ac.wait_ge(less, n + 1)
                    if n >= 2:
                        ac.wait_ge(var_done, n - 1)
                    nc.scalar.activation(sq[:, n % 2, :, :], g.agg[:, tiles(n), 0:cols], ACT.Square).then_inc(squared, 1)
                ac.wait_ge(var_done, NG)
                nc.scalar.activation(scale[:, :], p_v[:, :], ACT.Sqrt, scale=1.0 / N_NODES, bias=eps[:, 0:1]).then_inc(rooted, 1)
                if elu:
                    for n in range(NG):
                        ac.wait_ge(lows, n + 1)
                        nc.scalar.activation(low[:, n % 2, :, :], low[:, n % 2, :, :], ACT.Exp).then_inc(exped, 1)

            @block.vector
            def _(dv):
                V = nc.vector
                ch = Chain(dv, ops)
                ch.do(V.memset(eps[:, :], EPS))
                dv.wait_ge(loaded, 48)
                step = Chain(dv, biased)
                for n in range(NG):
                    h = g.agg[:, tiles(n), 0:cols]
                    if gcn:
                        step.do(V.tensor_tensor(h, h, g.agg[:, tiles(n), cols:2 * cols], ALU.add))
                        step.do(V.tensor_tensor(h, h, g.dinv[:, tiles(n)].unsqueeze(2).to_broadcast([P, GROUP, cols]), ALU.mult))
                        step.do(V.tensor_tensor(h, h, each(wide[:, 0, :]), ALU.add))
                        step.do(V.tensor_scalar(h, h, 0.0, None, ALU.max), wait=False)
                    else:
                        step.do(V.tensor_tensor(h, h, each(wide[:, 0, :]), ALU.add), wait=False)
                dv.wait_ge(summed, NG)
                ch.do(V.tensor_scalar(mean[:, :], p_m[:, :], 1.0 / N_NODES, None, ALU.mult))
                for n in range(NG):
                    h = g.agg[:, tiles(n), 0:cols]
                    V.tensor_tensor(h, h, each(mean[:, :]), ALU.subtract).then_inc(less, 1)
                dv.wait_ge(rooted, 1)
                ch.do(V.reciprocal(mean[:, :], scale[:, :]))
                ch.do(V.tensor_tensor(scale[:, :], mean[:, :], wide[:, 1, :], ALU.mult))
                step = Chain(dv, done)

                def out_of(n):
                    return y[:, n % 2, :, :] if into_x else g.agg[:, tiles(n), 0:cols]

                def normal(n):
                    step.do(V.tensor_tensor(out_of(n), g.agg[:, tiles(n), 0:cols], each(scale[:, :]), ALU.mult))
                    step.do(V.tensor_tensor(out_of(n), out_of(n), each(wide[:, 2, :]), ALU.add))
                    if elu:
                        V.tensor_scalar(low[:, n % 2, :, :], out_of(n), 0.0, None, ALU.min).then_inc(lows, 1)

                def finish(n):
                    if elu:
                        dv.wait_ge(lows, n + 1)
                        step.do(V.tensor_scalar(out_of(n), out_of(n), 0.0, -1.0, ALU.max, ALU.add))
                        dv.wait_ge(exped, n + 1)
                        step.do(V.tensor_tensor(out_of(n), out_of(n), low[:, n % 2, :, :], ALU.add))
                    if into_x:
                        x = g.x[:, tiles(n), 0:cols]
                        step.do(V.tensor_tensor(x, x, out_of(n), ALU.add))
                normal(0)
                for n in range(NG):
                    if n + 1 < NG:
                        normal(n + 1)
                    finish(n)


def gcn_table(nc, g, name, w):
    layernorm_stats(nc, g)
    F = 64
    with Phase(nc, name) as ph:
        prod = Products(nc, g, ph, 2, P, F, True)
        wsb = ph.sb("wsb", [P, 2, F])
        std = ph.sb("std", [P, NT])
        loaded, ops, rooted = ph.sem("loaded"), ph.sem("ops"), ph.sem("rooted")
        stored = [ph.sem(f"stored{s}") for s in range(2)]
        with nc.Block() as block:
            @block.sync
            def _(sp):
                sp.dma_start(wsb[:, :, :], w.rearrange("(b p) n -> p b n", p=P)).then_inc(loaded, 16)

                def store(i, s):
                    sp.wait_ge(prod.taken, i + 3)
                    sp.dma_start(g.table64[bass.ds(i * P, P), :], g.agg[:, bass.ds(i, 1), F:2 * F].rearrange("p a d -> p (a d)")).then_inc(stored[s], 16)
                by_two(sp, NT, store)
                sp.wait_ge(stored[0], 16 * (NT // 2 + 1))
                sp.wait_ge(stored[1], 16 * (NT // 2))

            @block.scalar
            def _(ac):
                nc.scalar.activation(std[:, :], g.deg[:, :], ACT.Sqrt, bias=g.ones[:, 0:1]).then_inc(rooted, 1)
                prod.scalar(ac)

            @block.tensor
            def _(pe):
                pe.wait_ge(loaded, 16)
                prod.tensor(pe, wsb)

            @block.vector
            def _(dv):
                dv.wait_ge(rooted, 1)
                nc.vector.reciprocal(g.dinv[:, :], std[:, :]).then_inc(ops, 1)
                dv.wait_ge(ops, 1)
                nc.vector.sem_inc(prod.taken, 2)

                def take(i, s):
                    dv.wait_ge(prod.multiplied, i + 3)
                    nc.vector.tensor_scalar(g.agg[:, bass.ds(i, 1), F:2 * F].rearrange("p a d -> p (a d)"), prod.out[s][:, :],
                                            g.dinv[:, bass.ds(i, 1)], None, ALU.mult).then_inc(prod.taken, 1)
                by_two(dv, NT, take)


def setup3(nc, g):
    sb = lambda n, s, d=F32: nc.keep.enter_context(nc.sbuf_tensor(n, s, d))
    dr = lambda n, s, d=F32: nc.dram_tensor(n, s, d, kind="Internal").ap()
    g.wt = sb("wt", [P, 2, D])
    g.dinv = sb("dinv", [P, NT])
    g.table64 = dr("table64", [NP, 64])
    g.rows256 = dr("rows256", [NP, D])
    g.table4 = dr("table4", [NP, D + 4])


def l3_gnn(nc, g, p):
    gcn_table(nc, g, "gcn", p["W_gcn"])
    gather_pass(nc, g, "gcnp", g.table64, 64)
    batch_norm(nc, g, "bn0", 64, p["b_gcn"], p["g0"], p["beta0"], False, gcn=True)
    gat_table(nc, g, "t2", p["W1"], p["a_src1"], p["a_dst1"], 4, 64, False, g.table4, g.inject4, False)
    gather_pass(nc, g, "g2", g.table4, D, 4, g.inject4)
    gat_finish(nc, g, "f2", g.table4, 4, 0.0)
    batch_norm(nc, g, "bn1", D, p["b1"], p["g1"], p["beta1"], False, elu=True)
    gat_table(nc, g, "t3", p["W2"], p["a_src2"], p["a_dst2"], 4, D, False, g.table4, g.inject4, False)
    gather_pass(nc, g, "g3", g.table4, D, 4, g.inject4)
    gat_finish(nc, g, "f3", g.table4, 4, 0.0)
    batch_norm(nc, g, "bn2", D, p["b2"], p["g2"], p["beta2"], True, elu=True)

E = 8
CAP = 977
ROOM = 1024
TILES = (2 * N_NODES + E * (P - 1)) // P
SLOTS = TILES * P
AHEAD = 4
OUT = 1000000.0
assert CAP == -(-5 * N_NODES // (4 * E)) and TILES % 2 == 1


def pipeline(eng, n, stages, unroll=2, peeled=0, before=None):
    leads = [k for k, _ in stages]
    a, b = peeled - min(leads), n - max(leads)
    turns = (b - a) // unroll

    def step(t):
        if before:
            before(t, 1)
        for lead, f in stages:
            if 0 <= t + lead < n:
                f(t + lead, (t + lead) % unroll, lead)
    for t in range(-max(leads), a):
        step(t)
    with eng.Fori(0, turns) as r:
        if before:
            before(unroll * r + a, unroll)
        for u in range(unroll):
            for lead, f in stages:
                f(unroll * r + (a + u + lead), (a + u + lead) % unroll, u + lead)
    for t in range(a + unroll * turns, n - min(leads)):
        step(t)


def two_slots(eng, n, wait_free, body):
    body(0, 0)
    body(1, 1)
    with eng.Fori(1, n // 2) as i:
        for s in range(2):
            wait_free(i, s)
            body(2 * i + s, s)
    if n % 2:
        wait_free(n // 2, 0)
        body(n - 1, 0)


def route(nc, g, name, w, bias, top2, softmax):
    layernorm_stats(nc, g)
    with Phase(nc, name) as ph:
        prod = Products(nc, g, ph, 2, P, E, True)
        wsb, gb = ph.sb("wsb", [P, 2, E]), ph.sb("gb", [P, E])
        big = lambda n: ph.sb(n, [P, E, NT])
        score, first, second, both, eq, tmp, pos, place, later = (
            big(n) for n in ("score", "first", "second", "both", "eq", "tmp", "pos", "place", "later"))
        small = lambda n: ph.sb(n, [P, NT])
        best, best2, left, valid, slot, kept = (small(n) for n in ("best", "best2", "left", "valid", "slot", "kept"))
        node, node_i, tri = small("node"), ph.sb("node_i", [P, NT], I32), ph.sb("tri", [P, P])
        count_i, tiles, bases, base = ph.sb("count_i", [P, E], I32), ph.sb("tiles", [P, E]), ph.sb("bases", [P, E]), ph.sb("base", [P, E])
        at, te = ph.sb("at", [1, 2, TILES]), ph.sb("te", [1, TILES])
        at_i = ph.sb("at_i", [1, TILES], I32)
        p_in, p_tot = ph.ps("p_in", [P, E * NT]), ph.ps("p_tot", [P, E * NT])
        loaded, seq, tri_ready, ops, counted, exped = (ph.sem(n) for n in ("loaded", "seq", "tri_ready", "ops", "counted", "exped"))
        marks, marks_pe = [], []
        by_node = lambda t: t[:, :, :].rearrange("p e t -> p t e")
        flat = lambda t: t[:, :, :].rearrange("p e t -> p (e t)")
        with nc.Block() as block:
            @block.sync
            def _(sp):
                sp.dma_start(wsb[:, :, :], w.rearrange("(b p) n -> p b n", p=P)).then_inc(loaded, 16)
                sp.dma_start(gb[:, :], bias.rearrange("(o n) -> o n", o=1).to_broadcast([P, E])).then_inc(loaded, 16)

            @block.gpsimd
            def _(gp):
                nc.gpsimd.iota(node_i[:, :], [[P, NT]], base=0, channel_multiplier=1).then_inc(seq, 1)
                nc.gpsimd.iota(at_i[:, :], [[1, TILES]], base=0, channel_multiplier=0).then_inc(seq, 1)
                nc.gpsimd.memset(tri[:, :], 0.0).then_inc(tri_ready, 1)
                gp.wait_ge(tri_ready, 1)
                nc.gpsimd.affine_select(out=tri[:, :], in_=tri[:, :], compare_op=ALU.is_ge, fill=1.0,
                                        base=0, pattern=[[-1, P]], channel_multiplier=1).then_inc(tri_ready, 1)

            @block.scalar
            def _(ac):
                prod.scalar(ac)

            @block.tensor
            def _(pe):
                pe.wait_ge(loaded, 32)
                prod.tensor(pe, wsb)

            @block.vector
            def _(dv):
                dv.wait_ge(loaded, 32)
                nc.vector.sem_inc(prod.taken, 2)

                def take(i, s):
                    dv.wait_ge(prod.multiplied, i + 3)
                    nc.vector.tensor_tensor(score[:, :, bass.ds(i, 1)].rearrange("p e a -> p (e a)"), prod.out[s][:, :], gb[:, :], ALU.add).then_inc(prod.taken, 1)
                by_two(dv, NT, take)
                dv.wait_ge(prod.taken, NT + 2)

        with nc.Block() as block:
            @block.vector
            def _(dv):
                ch = Chain(dv, ops)
                V = nc.vector

                def pick(out, scores, peak):
                    ch.do(V.tensor_reduce(out=peak[:, :], in_=by_node(scores), axis=AX.X, op=ALU.max))
                    ch.do(V.tensor_tensor(eq[:, :, :], scores[:, :, :], peak[:, :].unsqueeze(1).to_broadcast([P, E, NT]), ALU.is_equal))
                    ch.do(V.tensor_copy(left[:, :], valid[:, :]))
                    for e in range(E):
                        ch.do(V.tensor_tensor(out[:, e, :], eq[:, e, :], left[:, :], ALU.mult))
                        if e < E - 1:
                            ch.do(V.tensor_tensor(left[:, :], left[:, :], out[:, e, :], ALU.subtract))

                def chosen(out, mask, values):
                    ch.do(V.tensor_tensor(tmp[:, :, :], mask[:, :, :], values[:, :, :], ALU.mult))
                    ch.do(V.tensor_reduce(out=out[:, :], in_=by_node(tmp), axis=AX.X, op=ALU.add))
                dv.wait_ge(seq, 2)
                ch.do(V.tensor_copy(node[:, :], node_i[:, :]))
                ch.do(V.tensor_copy(at[0:1, 0, :], at_i[0:1, :]))
                ch.do(V.tensor_scalar(valid[:, :], node[:, :], float(N_NODES), None, ALU.is_lt))
                pick(first, score, best)
                if softmax:
                    ch.do(V.tensor_tensor(tmp[:, :, :], score[:, :, :], best[:, :].unsqueeze(1).to_broadcast([P, E, NT]), ALU.subtract))
                    marks.append(ch.n)
                    dv.wait_ge(exped, 1)
                    ch.do(V.tensor_reduce(out=slot[:, :], in_=by_node(eq), axis=AX.X, op=ALU.add))
                    ch.do(V.reciprocal(g.weight1[:, :], slot[:, :]))
                else:
                    ch.do(V.memset(g.weight1[:, :], 1.0))
                    ch.do(V.memset(g.weight2[:, :], 1.0))
                if top2:
                    ch.do(V.scalar_tensor_tensor(out=later[:, :, :], in0=first[:, :, :], scalar=-BIG, in1=score[:, :, :], op0=ALU.mult, op1=ALU.add))
                    pick(second, later, best2)
                    ch.do(V.tensor_tensor(both[:, :, :], first[:, :, :], second[:, :, :], ALU.add))
                    if softmax:
                        ch.do(V.tensor_tensor(kept[:, :], best2[:, :], best[:, :], ALU.subtract))
                        marks.append(ch.n)
                        dv.wait_ge(exped, 2)
                        ch.do(V.tensor_tensor(g.weight2[:, :], slot[:, :], g.weight1[:, :], ALU.mult))
                else:
                    ch.do(V.tensor_copy(both[:, :, :], first[:, :, :]))
                marks_pe.append(ch.n)
                dv.wait_ge(counted, 2)
                ch.do(V.memset(eq[:, :, :], 1.0))
                ch.do(V.memset(eq[:, :, 0:1], 0.0))
                ch.do(V.tensor_copy(tmp[:, :, :].rearrange("p e t -> p (e t)"), p_tot[:, :]))
                ch.do(V.tensor_tensor_scan(flat(later), flat(eq), flat(tmp), 0.0, ALU.mult, ALU.add))
                ch.do(V.tensor_tensor(flat(pos), flat(later), p_tot[:, :], ALU.subtract))
                ch.do(V.tensor_tensor(flat(pos), flat(pos), p_in[:, :], ALU.add))
                if top2:
                    ch.do(V.tensor_scalar(tiles[:, :], later[:, :, NT - 1], float(P - 1), None, ALU.add))
                    ch.do(V.tensor_copy(count_i[:, :], tiles[:, :]))
                    ch.do(V.tensor_scalar(count_i[:, :], count_i[:, :], 7, None, ALU.arith_shift_right))
                    ch.do(V.tensor_copy(tiles[:, :], count_i[:, :]))
                    ch.do(V.tensor_tensor_scan(bases[:, :], tiles[:, :], tiles[:, :], 0.0, ALU.add, ALU.bypass))
                    ch.do(V.tensor_tensor(bases[:, :], bases[:, :], tiles[:, :], ALU.subtract))
                    ch.do(V.tensor_scalar(base[:, :], bases[:, :], float(P), None, ALU.mult))
                    ch.do(V.tensor_tensor(place[:, :, :], pos[:, :, :], base[:, :].unsqueeze(2).to_broadcast([P, E, NT]), ALU.add))
                    ch.do(V.memset(te[:, :], 0.0))
                    for e in range(1, E):
                        ch.do(V.tensor_scalar(at[0:1, 1, :], at[0:1, 0, :], bases[0:1, e:e + 1], None, ALU.is_ge))
                        ch.do(V.tensor_tensor(te[:, :], te[:, :], at[0:1, 1, :], ALU.add))
                    ch.do(V.memset(g.tile_expert[:, :], 0))
                    ch.do(V.tensor_copy(g.tile_expert[:, AHEAD:AHEAD + TILES], te[:, :]))
                else:
                    for e in range(E):
                        ch.do(V.tensor_scalar(place[:, e, :], pos[:, e, :], float(CAP - 1), float(e * ROOM), ALU.min, ALU.add))
                    ch.do(V.tensor_scalar(eq[:, :, :], pos[:, :, :], float(CAP), None, ALU.is_lt))
                for mask, put, get in ((first, g.put1, g.get1), (second, g.put2, g.get2))[:1 + top2]:
                    chosen(slot, mask, place)
                    if top2:
                        ch.do(V.tensor_copy(kept[:, :], valid[:, :]))
                    else:
                        chosen(kept, mask, eq)
                        ch.do(V.tensor_tensor(g.weight1[:, :], g.weight1[:, :], kept[:, :], ALU.mult))
                    ch.do(V.tensor_copy(get[:, :], slot[:, :]))
                    ch.do(V.tensor_scalar(kept[:, :], kept[:, :], -OUT, OUT, ALU.mult, ALU.add))
                    ch.do(V.tensor_tensor(slot[:, :], slot[:, :], kept[:, :], ALU.add))
                    ch.do(V.tensor_copy(put[:, :], slot[:, :]))

            @block.scalar
            def _(ac):
                if softmax:
                    ac.wait_ge(ops, marks[0])
                    nc.scalar.activation(eq[:, :, :], tmp[:, :, :], ACT.Exp).then_inc(exped, 1)
                    if top2:
                        ac.wait_ge(ops, marks[1])
                        nc.scalar.activation(slot[:, :], kept[:, :], ACT.Exp).then_inc(exped, 1)

            @block.tensor
            def _(pe):
                pe.wait_ge(tri_ready, 2)
                pe.wait_ge(ops, marks_pe[0])
                nc.tensor.matmul(p_in[:, :], tri[:, :], flat(both), start=True, stop=True).then_inc(counted, 1)
                nc.tensor.matmul(p_tot[:, :], g.ones[:, :], flat(both), start=True, stop=True).then_inc(counted, 1)


def dispatch(nc, g, name, puts):
    K, NG = len(puts), NT // GROUP
    with Phase(nc, name) as ph:
        row = ph.sb("row", [P, 2, GROUP, D])
        idx = ph.sb("idx", [P, 2, K, GROUP], I32)
        made, placed = ph.sem("made"), ph.sem("placed")
        scattered = [ph.sem(f"scattered{s}") for s in range(2)]
        with nc.Block() as block:
            @block.scalar
            def _(ac):
                def free(uses, s):
                    ac.wait_ge(scattered[s], 16 * K * GROUP * uses)
                    ac.nop(nofuse=True)

                def make(n, s):
                    for u in range(GROUP):
                        normalised(nc, g, row[:, s, u, :], n * GROUP + u).then_inc(made, 1)
                two_slots(ac, NG, free, make)

            @block.gpsimd
            def _(gp):
                def free(uses, s):
                    gp.wait_ge(scattered[s], 16 * K * GROUP * uses)

                def scatter(n, s):
                    for k, put in enumerate(puts):
                        nc.gpsimd.tensor_copy(idx[:, s, k, :], put[:, bass.ds(n * GROUP, GROUP)]).then_inc(placed, 1)
                    gp.wait_ge(placed, K * (n + 1))
                    for u in range(GROUP):
                        gp.wait_ge(made, n * GROUP + u + 1)
                        gp.nop(nofuse=True)
                        for k in range(K):
                            gp.indirect_dma_start(g.expert_rows, bass.IndirectOffsetOnAxis(idx[:, s, k, u:u + 1], 0), row[:, s, u, :], None,
                                                  bounds_check=SLOTS - 1, oob_is_err=False).then_inc(scattered[s], 16)
                two_slots(gp, NG, free, scatter)
                gp.wait_ge(scattered[0], 16 * K * GROUP * (NG // 2 + 1))
                gp.wait_ge(scattered[1], 16 * K * GROUP * (NG // 2))


def experts_by_room(nc, g, name, w1, b1, w2, b2):
    F = w1.shape[2]
    HB, RT = F // P, ROOM // P
    NH = ROOM // 512
    with Phase(nc, name) as ph:
        w1s, w2s = ph.sb("w1s", [P, 2, 2, F]), ph.sb("w2s", [P, 2, HB, D])
        b2s = ph.sb("b2s", [P, 2, D])
        xin = ph.sb("xin", [P, RT, D])
        spare = g.agg[:, :, :].rearrange("p t w -> p (t w)")
        ht = spare[:, 0:HB * ROOM].rearrange("p (b r) -> p b r", b=HB)
        xt = spare[:, HB * ROOM:HB * ROOM + 2 * ROOM].rearrange("p (k r) -> p k r", k=2)
        b1r = ph.sb("b1r", [E * HB, P])
        b1t = ph.sb("b1t", [P, E * HB])
        y = ph.sb("y", [P, 2, D])
        p_x = [ph.ps(f"p_x{s}", [P, 2, P]) for s in range(2)]
        p_h = [ph.ps(f"p_h{s}", [P, 512]) for s in range(2)]
        p_y = [ph.ps(f"p_y{s}", [P, D]) for s in range(2)]
        p_b = ph.ps("p_b", [P, E * HB])
        b_in, b_turned, b_ready = ph.sem("b_in"), ph.sem("b_turned"), ph.sem("b_ready")
        x_in = ph.sem("x_in")
        w_in = [ph.sem(f"w_in{s}") for s in range(2)]
        turned, copied, up, hidden, down, made = (ph.sem(n) for n in ("turned", "copied", "up", "hidden", "down", "made"))
        stored = [ph.sem(f"stored{s}") for s in range(2)]
        NU = HB * NH
        with nc.Block() as block:
            @block.sync
            def _(sp):
                sp.dma_start(b1r[:, :], b1.rearrange("e (b p) -> (e b) p", p=P)).then_inc(b_in, 16)

                def weights(e, s):
                    one = bass.ds(e, 1)
                    sp.dma_start(w1s[:, s, :, :], w1[one, :, :].rearrange("e (k p) f -> p (e k) f", p=P)).then_inc(w_in[s], 16)
                    sp.dma_start(w2s[:, s, :, :], w2[one, :, :].rearrange("e (b p) d -> p (e b) d", p=P)).then_inc(w_in[s], 16)
                    sp.dma_start(b2s[:, s, :], b2[one, :].to_broadcast([P, D])).then_inc(w_in[s], 16)

                def rows(e):
                    sp.dma_start(xin[:, :, :], g.expert_rows[bass.ds(e * ROOM, ROOM), :].rearrange("(t p) d -> p t d", p=P)).then_inc(x_in, 16)
                weights(0, 0)
                rows(0)
                weights(1, 1)

                def store(e, s):
                    for t in range(RT):
                        sp.wait_ge(made, e * RT + t + 3)
                        sp.dma_start(g.expert_out[bass.ds(e * ROOM + t * P, P), :], y[:, t % 2, :]).then_inc(stored[t % 2], 16)
                with sp.Fori(0, E // 2 - 1) as i:
                    for s in range(2):
                        e = 2 * i + s
                        sp.wait_ge(turned, RT * e + RT + 2)
                        rows(e + 1)
                        store(e, s)
                        sp.wait_ge(down, RT * e + RT + 2)
                        weights(e + 2, s)
                sp.wait_ge(turned, RT * (E - 1) + 2)
                rows(E - 1)
                store(E - 2, 0)
                store(E - 1, 1)
                for s in range(2):
                    sp.wait_ge(stored[s], 16 * E * RT // 2)

            @block.tensor
            def _(pe):
                nc.tensor.sem_inc(turned, 2)
                nc.tensor.sem_inc(up, 2)
                nc.tensor.sem_inc(down, 2)
                pe.wait_ge(b_in, 16)
                nc.tensor.transpose(p_b[:, :], b1r[:, :], g.ident[0:E * HB, 0:E * HB]).then_inc(b_turned, 1)

                def expert(e, s):
                    pe.wait_ge(x_in, 16 * (e + 1))
                    for t in range(RT):
                        pe.wait_ge(copied, RT * e + t + 1)
                        for k in range(2):
                            last = nc.tensor.transpose(p_x[t % 2][:, k, :], xin[:, t, k * P:(k + 1) * P], g.ident[:, :])
                        last.then_inc(turned, 1)
                    pe.wait_ge(copied, RT * e + RT + 2)
                    pe.wait_ge(w_in[s], 48 * ((e - s) // 2 + 1))
                    for b in range(HB):
                        for h in range(NH):
                            u = b * NH + h
                            pe.wait_ge(hidden, NU * e + u + 1)
                            for k in range(2):
                                last = nc.tensor.matmul(p_h[u % 2][:, :], w1s[:, s, k, b * P:(b + 1) * P], xt[:, k, h * 512:(h + 1) * 512], start=(k == 0), stop=(k == 1))
                            last.then_inc(up, 1)
                    for t in range(RT):
                        pe.wait_ge(hidden, NU * e + NU + 2)
                        pe.wait_ge(made, RT * e + t + 1)
                        for b in range(HB):
                            last = nc.tensor.matmul(p_y[t % 2][:, :], ht[:, b, t * P:(t + 1) * P], w2s[:, s, b, :], start=(b == 0), stop=(b == HB - 1))
                        last.then_inc(down, 1)
                by_two(pe, E, expert)

            @block.scalar
            def _(ac):
                nc.scalar.sem_inc(hidden, 2)
                ac.wait_ge(b_ready, 1)

                def expert(e, s):
                    ac.wait_ge(down, RT * e + 2)
                    for b in range(HB):
                        for h in range(NH):
                            u = b * NH + h
                            ac.wait_ge(up, NU * e + u + 3)
                            ac.nop(nofuse=True)
                            nc.scalar.activation(ht[:, b, h * 512:(h + 1) * 512], p_h[u % 2][:, :], ACT.Relu, bias=b1t[:, bass.ds(e * HB + b, 1)]).then_inc(hidden, 1)
                by_two(ac, E, expert)

            @block.vector
            def _(dv):
                nc.vector.sem_inc(copied, 2)
                nc.vector.sem_inc(made, 2)
                dv.wait_ge(b_turned, 1)
                nc.vector.tensor_copy(b1t[:, :], p_b[:, :]).then_inc(b_ready, 1)

                def expert(e, s):
                    dv.wait_ge(up, NU * e + 2)
                    for t in range(RT):
                        dv.wait_ge(turned, RT * e + t + 3)
                        nc.vector.tensor_copy(xt[:, :, t * P:(t + 1) * P], p_x[t % 2][:, :, :]).then_inc(copied, 1)
                    dv.wait_ge(w_in[s], 48 * ((e - s) // 2 + 1))
                    for t in range(RT):
                        dv.wait_ge(down, RT * e + t + 3)
                        if not (isinstance(e, int) and e == 0 and t < 2):
                            dv.wait_ge(stored[t % 2], 16 * (RT // 2 * e + t // 2))
                        nc.vector.tensor_tensor(y[:, t % 2, :], p_y[t % 2][:, :], b2s[:, s, :], ALU.add).then_inc(made, 1)
                expert(0, 0)
                with dv.Fori(0, E // 2 - 1) as i:
                    expert(2 * i + 1, 1)
                    expert(2 * i + 2, 0)
                expert(E - 1, 1)


def experts_by_tile(nc, g, name, w1, b1, w2, b2):
    F = w1.shape[2]
    HB = F // P
    with Phase(nc, name) as ph:
        spare = g.agg[:, :, :].rearrange("p t w -> p (t w)")
        w1s = spare[:, 0:E * 2 * F].rearrange("p (e k f) -> p e (k f)", e=E, k=2)
        b1s = spare[:, E * 2 * F:E * 3 * F].rearrange("p (e f) -> p e f", e=E)
        w2s, b2s = ph.sb("w2s", [P, E, HB * D]), ph.sb("b2s", [P, E, D])
        xin = ph.sb("xin", [P, AHEAD, D])
        xt = ph.sb("xt", [P, 2, 2, P])
        hb, hg, ht = ph.sb("hb", [P, 2, F]), ph.sb("hg", [P, 2, F]), ph.sb("ht", [P, 2, HB, P])
        y = ph.sb("y", [P, AHEAD, D])
        p_x = [ph.ps(f"p_x{s}", [P, 2, P]) for s in range(2)]
        p_h = [ph.ps(f"p_h{s}", [P, F]) for s in range(2)]
        p_t = [ph.ps(f"p_t{s}", [P, HB, P]) for s in range(2)]
        p_y = [ph.ps(f"p_y{s}", [P, D]) for s in range(2)]
        w_in = ph.sem("w_in")
        turned, copied, up, biased, curved, h_turned, h_copied, down, made = (
            ph.sem(n) for n in ("turned", "copied", "up", "biased", "curved", "h_turned", "h_copied", "down", "made"))
        x_in = [ph.sem(f"x_in{s}") for s in range(AHEAD)]
        stored = [ph.sem(f"stored{s}") for s in range(AHEAD)]
        uses = lambda i, s: 16 * ((i - s) // AHEAD + 1)

        def experts(eng, engine):
            loaded = []

            def before(t, steps):
                eng.nop(nofuse=True)
                loaded[:] = registers(nc, engine, g.tile_expert[0:1, bass.ds(t + AHEAD - 1, steps + 2)], E - 1, waited=False)
            return before, lambda place: bass.ds(loaded[place + 1], 1)

        with nc.Block() as block:
            @block.sync
            def _(sp):
                def load(i, s, at):
                    if not (isinstance(i, int) and i < AHEAD):
                        sp.wait_ge(turned, i + 3 - AHEAD)
                    sp.dma_start(xin[:, s, :], g.expert_rows[bass.ds(i * P, P), :]).then_inc(x_in[s], 16)

                def store(i, s, at):
                    sp.wait_ge(made, i + 3)
                    sp.dma_start(g.expert_out[bass.ds(i * P, P), :], y[:, s, :]).then_inc(stored[s], 16)
                pipeline(sp, TILES, [(AHEAD, load), (-1, store)], AHEAD)
                for s in range(AHEAD):
                    sp.wait_ge(stored[s], 16 * len(range(s, TILES, AHEAD)))

            @block.gpsimd
            def _(gp):
                gp.dma_start(w1s.rearrange("p e (k f) -> p e k f", k=2), w1.rearrange("e (k p) f -> p e k f", p=P)).then_inc(w_in, 16)
                gp.dma_start(w2s[:, :, :].rearrange("p e (b d) -> p e b d", b=HB), w2.rearrange("e (b p) d -> p e b d", p=P)).then_inc(w_in, 16)
                gp.dma_start(b1s.rearrange("p e f -> p (e f)"), b1.rearrange("(o e) f -> o (e f)", o=1).to_broadcast([P, E * F])).then_inc(w_in, 16)
                gp.dma_start(b2s[:, :, :].rearrange("p e f -> p (e f)"), b2.rearrange("(o e) f -> o (e f)", o=1).to_broadcast([P, E * D])).then_inc(w_in, 16)
                gp.wait_ge(w_in, 64)

            @block.tensor
            def _(pe):
                for s in (turned, up, h_turned, down):
                    nc.tensor.sem_inc(s, 2)
                before, of = experts(pe, PE)

                def turn(i, s, at):
                    pe.wait_ge(x_in[s], uses(i, s))
                    pe.wait_ge(copied, i + 1)
                    for k in range(2):
                        last = nc.tensor.transpose(p_x[s % 2][:, k, :], xin[:, s, k * P:(k + 1) * P], g.ident[:, :])
                    last.then_inc(turned, 1)

                def first(i, s, at):
                    pe.wait_ge(copied, i + 3)
                    pe.wait_ge(biased, i + 1)
                    for k in range(2):
                        last = nc.tensor.matmul(p_h[s % 2][:, :], xt[:, s % 2, k, :], w1s[:, of(at), k * F:(k + 1) * F].rearrange("p a f -> p (a f)"), start=(k == 0), stop=(k == 1))
                    last.then_inc(up, 1)

                def turn_hidden(i, s, at):
                    pe.wait_ge(curved, i + 3)
                    pe.wait_ge(h_copied, i + 1)
                    for b in range(HB):
                        last = nc.tensor.transpose(p_t[s % 2][:, b, :], hg[:, s % 2, b * P:(b + 1) * P], g.ident[:, :])
                    last.then_inc(h_turned, 1)

                def second(i, s, at):
                    pe.wait_ge(h_copied, i + 3)
                    pe.wait_ge(made, i + 1)
                    for b in range(HB):
                        last = nc.tensor.matmul(p_y[s % 2][:, :], ht[:, s % 2, b, :], w2s[:, of(at), b * D:(b + 1) * D].rearrange("p a f -> p (a f)"), start=(b == 0), stop=(b == HB - 1))
                    last.then_inc(down, 1)
                pe.wait_ge(w_in, 64)
                pipeline(pe, TILES, [(2, turn), (1, first), (0, turn_hidden), (-1, second)], AHEAD, before=before)

            @block.scalar
            def _(ac):
                nc.scalar.sem_inc(copied, 2)
                nc.scalar.sem_inc(curved, 2)

                def copy(i, s, at):
                    ac.wait_ge(turned, i + 3)
                    ac.wait_ge(up, i + 1)
                    nc.scalar.activation(xt[:, s, :, :], p_x[s][:, :, :], ACT.Identity).then_inc(copied, 1)

                def curve(i, s, at):
                    ac.wait_ge(biased, i + 3)
                    ac.wait_ge(h_turned, i + 1)
                    nc.scalar.activation(hg[:, s, :], hb[:, s, :], ACT.Gelu).then_inc(curved, 1)
                pipeline(ac, TILES, [(2, copy), (1, curve)])

            @block.vector
            def _(dv):
                for s in (biased, h_copied, made):
                    nc.vector.sem_inc(s, 2)
                dv.wait_ge(w_in, 64)
                before, of = experts(dv, DVE)

                def bias(i, s, at):
                    dv.wait_ge(up, i + 3)
                    dv.wait_ge(curved, i + 1)
                    nc.vector.tensor_tensor(hb[:, s % 2, :], p_h[s % 2][:, :], b1s[:, of(at), :].rearrange("p a f -> p (a f)"), ALU.add).then_inc(biased, 1)

                def out(i, s, at):
                    dv.wait_ge(down, i + 3)
                    if not (isinstance(i, int) and i < AHEAD):
                        dv.wait_ge(stored[s], 16 * ((i - s) // AHEAD))
                    nc.vector.tensor_tensor(y[:, s, :], p_y[s % 2][:, :], b2s[:, of(at), :].rearrange("p a f -> p (a f)"), ALU.add).then_inc(made, 1)

                def copy_hidden(i, s, at):
                    dv.wait_ge(h_turned, i + 3)
                    dv.wait_ge(down, i + 1)
                    nc.vector.tensor_copy(ht[:, s % 2, :, :], p_t[s % 2][:, :, :]).then_inc(h_copied, 1)
                pipeline(dv, TILES, [(1, bias), (0, copy_hidden), (-1, out)], AHEAD, peeled=AHEAD, before=before)


def combine(nc, g, name, gets, weights, guard):
    K, NG = len(gets), NT // GROUP
    with Phase(nc, name) as ph:
        row = ph.sb("row", [P, 2, K, GROUP, D])
        idx = ph.sb("idx", [P, 2, K, GROUP], I32)
        bad = ph.sb("bad", [P, GROUP, D], I32)
        fill = ph.sb("fill", [P, 3, D])
        placed, used, ops, filled = ph.sem("placed"), ph.sem("used"), ph.sem("ops"), ph.sem("filled")
        got = [ph.sem(f"got{s}") for s in range(2)]
        MOST = float(np.finfo(np.float32).max)
        with nc.Block() as block:
            @block.gpsimd
            def _(gp):
                def gather(n, s):
                    gp.wait_ge(used, n + 1)
                    for k, get in enumerate(gets):
                        nc.gpsimd.tensor_copy(idx[:, s, k, :], get[:, bass.ds(n * GROUP, GROUP)]).then_inc(placed, 1)
                    gp.wait_ge(placed, K * (n + 1))
                    gp.nop(nofuse=True)
                    for k in range(K):
                        for u in range(GROUP):
                            gp.indirect_dma_start(row[:, s, k, u, :], None, g.expert_out, bass.IndirectOffsetOnAxis(idx[:, s, k, u:u + 1], 0)).then_inc(got[s], 16)
                by_two(gp, NG, gather)

            @block.vector
            def _(dv):
                V = nc.vector
                fl = Chain(dv, filled)
                if guard:
                    for n, v in enumerate((0.0, 10000.0, -10000.0)):
                        fl.do(V.memset(fill[:, n, :], v))
                V.sem_inc(used, 2)
                per = K + (K - 1) + 6 * guard

                def add(n, s):
                    tiles = bass.ds(n * GROUP, GROUP)
                    x, r = g.x[:, tiles, :], row[:, s, 0, :, :]
                    dv.wait_ge(got[s], 16 * K * GROUP * ((n - s) // 2 + 1))
                    step = Chain(dv, ops, per * n)
                    for k in range(K):
                        each = row[:, s, k, :, :]
                        step.do(V.tensor_tensor(each, each, weights[k][:, tiles].unsqueeze(2).to_broadcast([P, GROUP, D]), ALU.mult))
                    for k in range(1, K):
                        step.do(V.tensor_tensor(r, r, row[:, s, k, :, :], ALU.add))
                    if guard:
                        for k in range(3):
                            if k == 0:
                                step.do(V.tensor_tensor(bad[:, :, :], r, r, ALU.not_equal))
                            else:
                                step.do(V.tensor_scalar(bad[:, :, :], r, (MOST, -MOST)[k - 1], None, (ALU.is_gt, ALU.is_lt)[k - 1]))
                            dv.nop(nofuse=True)
                            step.do(V.copy_predicated(r, bad[:, :, :], fill[:, k, :].unsqueeze(1).to_broadcast([P, GROUP, D])))
                    V.tensor_tensor(x, x, r, ALU.add).then_inc(used, 1)
                by_two(dv, NG, add)


def setup4(nc, g):
    sb = lambda n, s, d=F32: nc.keep.enter_context(nc.sbuf_tensor(n, s, d))
    dr = lambda n, s, d=F32: nc.dram_tensor(n, s, d, kind="Internal").ap()
    g.put1, g.put2, g.get1, g.get2 = (sb(n, [P, NT], I32) for n in ("put1", "put2", "get1", "get2"))
    g.weight1, g.weight2 = sb("weight1", [P, NT]), sb("weight2", [P, NT])
    g.tile_expert = sb("tile_expert", [1, AHEAD + TILES + AHEAD], I32)
    g.expert_rows, g.expert_out = dr("expert_rows", [SLOTS, D]), dr("expert_out", [SLOTS, D])


class Filling:

    def __init__(self, nc, g, ph):
        self.nc, self.g = nc, g
        self.ready, self.filled = ph.sem("fill_ready"), ph.sem("filled")
        self.low = ph.sb("low", [P, EP * 4 // P])
        self.zero = g.agg[:, :, :].rearrange("p t w -> p (t w)")[:, 0:15 * D]

    def gpsimd(self, gp):
        self.nc.gpsimd.memset(self.low[:, :], -BIG).then_inc(self.ready, 1)
        self.nc.gpsimd.memset(self.zero, 0.0).then_inc(self.ready, 1)

    def scalar(self, ac):
        g, n = self.g, EP * 4 // P
        ac.wait_ge(self.ready, 2)
        for inject, parts in ((g.inject8, 4), (g.inject4, 2)):
            for q in range(parts):
                ac.dma_start(inject.rearrange("(p r) q -> p (r q)", p=P)[:, q * n:(q + 1) * n], self.low[:, :]).then_inc(self.filled, 16)
        for rows in (g.expert_rows, g.expert_out):
            v = rows.rearrange("(p r) d -> p (r d)", p=P)
            for q in range(TILES // 15):
                ac.dma_start(v[:, q * 15 * D:(q + 1) * 15 * D], self.zero).then_inc(self.filled, 16)
        ac.wait_ge(self.filled, 16 * (6 + 2 * TILES // 15))


def l0_ffn(nc, g, a):
    route(nc, g, "r0", a["L0_ffn_gate_w"], a["L0_ffn_gate_b"], False, True)
    dispatch(nc, g, "d0", [g.put1])
    experts_by_room(nc, g, "e0", a["L0_ffn_w1"], a["L0_ffn_b1"], a["L0_ffn_w2"], a["L0_ffn_b2"])
    combine(nc, g, "c0", [g.get1], [g.weight1], True)


def top2_ffn(nc, g, gw, gb, w1, b1, w2, b2, softmax):
    route(nc, g, "r2", gw, gb, True, softmax)
    dispatch(nc, g, "d2", [g.put1, g.put2])
    experts_by_tile(nc, g, "e2", w1, b1, w2, b2)
    combine(nc, g, "c2", [g.get1, g.get2], [g.weight1, g.weight2], False)

TP = EP // P
QC = 512
NQ = EP // QC
LISTED = 8
ALPHA, BETA, COS, SIN, READ, WRITE, ROW, LATE = range(LISTED)
NONE = float(D)
BATCH = 8
TWO_PI = 6.283185307179586
TWO_PI_HI = 6.28125
ROUND = 12582912.0


def rotation_list(nc, g):
    with Phase(nc, "list") as ph:
        src_i, dst_i, w = ph.sb("src_i", [P, TP], I32), ph.sb("dst_i", [P, TP], I32), ph.sb("w", [P, TP])
        spare = g.agg[:, :, :].rearrange("p t w -> p (t w)").rearrange("p (k t) -> p k t", t=TP)
        rec = g.agg[:, :, :].rearrange("p t w -> p (t w)")[:, 0:TP * LISTED].rearrange("p (t f) -> p t f", f=LISTED)
        turns, half, early, inside, event, late, psn, d1, pc = (spare[:, LISTED + k, :] for k in range(9))
        srcf, dstf, cos, sin, listed, tmp, tmp2, reset = (
            ph.sb(n, [P, TP]) for n in ("srcf", "dstf", "cos", "sin", "listed", "tmp", "tmp2", "reset"))
        back_i, back, first_i, firstf = ph.sb("back_i", [P, TP], I32), ph.sb("back", [P, TP]), ph.sb("first_i", [P, 1], I32), ph.sb("firstf", [P, 1])
        keys = ph.sb("keys", [P, TP + 16])
        rank_i, rank, key8 = ph.sb("rank_i", [P, TP + 16], I32), ph.sb("rank", [P, TP + 16]), ph.sb("key8", [P, 8])
        edge, place = ph.sb("edge", [P, TP + 16], I32), ph.sb("place", [P, TP + 16], I32)
        counts = ph.sb("counts", [P, 2])
        base = ph.sb("base", [P, 1])
        most = ph.sb("most", [1, 3])
        tri = ph.sb("tri", [P, P])
        fill = ph.sb("fill", [P, TP * LISTED // 4])
        got = ph.sb("got", [P, 2, 8, LISTED])
        ids, tos = ph.sb("ids", [P, 2, 8], I32), ph.sb("tos", [P, 2, 8], I32)
        p_cnt = ph.ps("p_cnt", [1, P])
        p_tot = ph.ps("p_tot", [P, 2])
        p_base = ph.ps("p_base", [P, 1])
        blank, din, seq, ops, waves, squared, tri_ready, summed, stored, chunks = (
            ph.sem(n) for n in ("blank", "din", "seq", "ops", "waves", "squared", "tri_ready", "summed", "stored", "chunks"))
        set_up, copied = ph.sem("set_up"), ph.sem("copied")
        fetched = [ph.sem(f"fetched{s}") for s in range(2)]
        placed = [ph.sem(f"placed{s}") for s in range(2)]
        fill_ready = ph.sem("fill_ready")
        mark = {}
        last = N_EDGES - (P - 1) * TP
        with nc.Block() as block:
            @block.sync
            def _(sp):
                sp.wait_ge(blank, 3)
                for dram, t in ((g.src_dram, src_i), (g.dst_dram, dst_i), (g.w_dram, w)):
                    sp.dma_start(t[0:P - 1, :], dram_view(dram, 0, [[TP, P - 1], [1, TP]])).then_inc(din, 16)
                    sp.dma_start(t[P - 1:P, 0:last], dram_view(dram, (P - 1) * TP, [[TP, 1], [1, last]])).then_inc(din, 16)
                sp.wait_ge(fill_ready, 2)
                n = TP * LISTED // 4
                for q in range(4):
                    sp.dma_start(g.steps.rearrange("(p r) q -> p (r q)", p=P)[:, q * n:(q + 1) * n], fill[:, :]).then_inc(stored, 16)

            @block.gpsimd
            def _(gp):
                nc.gpsimd.iota(back_i[:, :], [[-1, TP]], base=TP, channel_multiplier=0).then_inc(seq, 1)
                nc.gpsimd.iota(first_i[:, :], [[1, 1]], base=TP, channel_multiplier=TP).then_inc(seq, 1)
                nc.gpsimd.iota(rank_i[:, :], [[1, TP + 16]], base=0, channel_multiplier=0).then_inc(seq, 1)
                nc.gpsimd.memset(fill[:, :], NONE).then_inc(fill_ready, 1)
                gp.wait_ge(fill_ready, 1)
                nc.gpsimd.memset(fill[:, :].rearrange("p (t f) -> p t f", f=LISTED)[:, :, ROW], NONE + 1).then_inc(fill_ready, 1)
                nc.gpsimd.memset(tri[:, :], 0.0).then_inc(tri_ready, 1)
                gp.wait_ge(tri_ready, 1)
                nc.gpsimd.affine_select(out=tri[:, :], in_=tri[:, :], compare_op=ALU.is_ge, fill=1.0,
                                        base=0, pattern=[[-1, P]], channel_multiplier=1).then_inc(tri_ready, 1)

            @block.vector
            def _(dv):
                V = nc.vector
                V.memset(src_i[:, :], NP - 1).then_inc(blank, 1)
                V.memset(dst_i[:, :], NP - 1).then_inc(blank, 1)
                V.memset(w[:, :], 0.0).then_inc(blank, 1)
                ch = Chain(dv, ops)
                dv.wait_ge(seq, 3)
                dv.wait_ge(din, 6 * 16)
                ch.do(V.tensor_scalar(turns[:, :], w[:, :], 1.0 / TWO_PI, ROUND, ALU.mult, ALU.add))
                ch.do(V.tensor_scalar(turns[:, :], turns[:, :], ROUND, None, ALU.subtract))
                ch.do(V.scalar_tensor_tensor(out=w[:, :], in0=turns[:, :], scalar=-TWO_PI_HI, in1=w[:, :], op0=ALU.mult, op1=ALU.add))
                ch.do(V.scalar_tensor_tensor(out=w[:, :], in0=turns[:, :], scalar=-(TWO_PI - TWO_PI_HI), in1=w[:, :], op0=ALU.mult, op1=ALU.add))
                ch.do(V.tensor_scalar(w[:, :], w[:, :], TWO_PI / 2 - 1e-6, -TWO_PI / 2 + 1e-6, ALU.min, ALU.max))
                mark["angle"] = ch.n
                ch.do(V.tensor_copy(srcf[:, :], src_i[:, :]))
                ch.do(V.tensor_copy(dstf[:, :], dst_i[:, :]))
                ch.do(V.tensor_copy(back[:, :], back_i[:, :]))
                ch.do(V.tensor_copy(firstf[:, :], first_i[:, :]))
                ch.do(V.tensor_copy(rank[:, :], rank_i[:, :]))
                ch.do(V.memset(keys[:, :], 0.0))
                ch.do(V.tensor_scalar(early[:, :], dstf[:, :], float(D), None, ALU.is_lt))
                ch.do(V.tensor_scalar(inside[:, :], srcf[:, :], float(D), None, ALU.is_lt))
                ch.do(V.memset(event[:, :], 1.0))
                ch.do(V.tensor_tensor(event[:, 0:TP - 1], dstf[:, 1:TP], dstf[:, 0:TP - 1], ALU.not_equal))
                ch.do(V.tensor_tensor(event[:, :], event[:, :], inside[:, :], ALU.max))
                ch.do(V.tensor_tensor(event[:, :], event[:, :], early[:, :], ALU.mult))
                ch.do(V.tensor_tensor(tmp[:, :], inside[:, :], early[:, :], ALU.mult))
                ch.do(V.tensor_tensor(late[:, :], inside[:, :], tmp[:, :], ALU.subtract))
                ch.do(V.tensor_tensor(listed[:, :], event[:, :], late[:, :], ALU.add))
                ch.do(V.tensor_reduce(out=counts[:, 0:1], in_=listed[:, :], axis=AX.X, op=ALU.add))
                ch.do(V.tensor_reduce(out=counts[:, 1:2], in_=event[:, :], axis=AX.X, op=ALU.add))
                mark["counts"] = ch.n
                ch.do(V.tensor_tensor(listed[:, :], listed[:, :], back[:, :], ALU.mult))
                plain = tmp2
                ch.do(V.tensor_tensor(plain[:, :], early[:, :], tmp[:, :], ALU.subtract))
                ch.do(V.memset(reset[:, 0:1], 1.0))
                ch.do(V.tensor_copy(reset[:, 1:TP], event[:, 0:TP - 1]))
                dv.wait_ge(waves, 2)
                ch.do(V.tensor_scalar(cos[:, :], half[:, :], -2.0, 1.0, ALU.mult, ALU.add))
                ch.do(V.tensor_scalar(tmp[:, :], dstf[:, :], float(D - 1), None, ALU.is_equal))
                ch.do(V.tensor_tensor(d1[:, :], tmp[:, :], sin[:, :], ALU.mult))
                ch.do(V.tensor_tensor(pc[:, :], cos[:, :], d1[:, :], ALU.add))
                ch.do(V.tensor_tensor(psn[:, :], sin[:, :], d1[:, :], ALU.subtract))
                ch.do(V.tensor_tensor(psn[:, :], psn[:, :], plain[:, :], ALU.mult))
                ch.do(V.scalar_tensor_tensor(out=pc[:, :], in0=pc[:, :], scalar=-1.0, in1=plain[:, :], op0=ALU.add, op1=ALU.mult))
                ch.do(V.tensor_scalar(pc[:, :], pc[:, :], 1.0, None, ALU.add))
                ch.do(V.tensor_tensor(d1[:, :], pc[:, :], reset[:, :], ALU.mult))
                ch.do(V.tensor_tensor(pc[:, :], pc[:, :], d1[:, :], ALU.subtract))
                ch.do(V.tensor_tensor_scan(tmp[:, :], pc[:, :], d1[:, :], 0.0, ALU.mult, ALU.add))
                ch.do(V.tensor_tensor_scan(tmp2[:, :], pc[:, :], psn[:, :], 0.0, ALU.mult, ALU.add))
                ch.do(V.tensor_copy(rec[:, :, ALPHA], tmp[:, :]))
                ch.do(V.tensor_copy(rec[:, :, BETA], tmp2[:, :]))
                ch.do(V.scalar_tensor_tensor(out=tmp[:, :], in0=cos[:, :], scalar=-1.0, in1=inside[:, :], op0=ALU.add, op1=ALU.mult))
                ch.do(V.tensor_scalar(rec[:, :, COS], tmp[:, :], 1.0, None, ALU.add))
                ch.do(V.tensor_tensor(rec[:, :, SIN], sin[:, :], inside[:, :], ALU.mult))
                ch.do(V.tensor_scalar(rec[:, :, READ], srcf[:, :], float(D - 1), None, ALU.min))
                ch.do(V.tensor_tensor(tmp[:, :], srcf[:, :], dstf[:, :], ALU.is_equal))
                ch.do(V.tensor_tensor(tmp[:, :], tmp[:, :], late[:, :], ALU.max))
                ch.do(V.tensor_scalar(tmp[:, :], tmp[:, :], NONE, None, ALU.mult))
                ch.do(V.scalar_tensor_tensor(out=rec[:, :, WRITE], in0=srcf[:, :], scalar=float(D), in1=tmp[:, :], op0=ALU.min, op1=ALU.max))
                ch.do(V.scalar_tensor_tensor(out=rec[:, :, ROW], in0=dstf[:, :], scalar=NONE, in1=late[:, :], op0=ALU.min, op1=ALU.add))
                ch.do(V.scalar_tensor_tensor(out=tmp[:, :], in0=srcf[:, :], scalar=-NONE, in1=late[:, :], op0=ALU.add, op1=ALU.mult))
                ch.do(V.tensor_scalar(rec[:, :, LATE], tmp[:, :], NONE, None, ALU.add))
                mark["rec"] = ch.n
                dv.wait_ge(summed, 3)
                ch.do(V.tensor_reduce(out=most[0:1, 0:1], in_=p_cnt[0:1, :], axis=AX.X, op=ALU.max))
                ch.do(V.tensor_copy(most[0:1, 1:3], p_tot[0:1, :]))
                ch.do(V.tensor_copy(base[:, :], p_base[:, :]))
                ch.do(V.tensor_scalar(most[0:1, 0:1], most[0:1, 0:1], 15.0, 16.0, ALU.add, ALU.max))
                ch.do(V.tensor_copy(g.sizes[0:1, 0:3], most[0:1, :]))
                ch.do(V.tensor_scalar(g.sizes[0:1, 0:1], g.sizes[0:1, 0:1], 4, None, ALU.arith_shift_right))
                for k in (1, 2):
                    ch.do(V.tensor_scalar(most[0:1, k:k + 1], most[0:1, k:k + 1], float(QC - 1), None, ALU.add))
                ch.do(V.tensor_copy(g.sizes[0:1, 3:5], most[0:1, 1:3]))
                ch.do(V.tensor_scalar(g.sizes[0:1, 3:5], g.sizes[0:1, 3:5], 9, None, ALU.arith_shift_right))
                ch.do(V.tensor_copy(tmp[0:1, 0:NQ], g.sizes[0:1, 2:3].to_broadcast([1, NQ])))
                ch.do(V.scalar_tensor_tensor(out=tmp[0:1, 0:NQ], in0=rank[0:1, 0:NQ], scalar=-float(QC), in1=tmp[0:1, 0:NQ], op0=ALU.mult, op1=ALU.add))
                ch.do(V.tensor_scalar(tmp[0:1, 0:NQ], tmp[0:1, 0:NQ], 0.0, float(QC), ALU.max, ALU.min))
                ch.do(V.tensor_scalar(tmp[0:1, 0:NQ], tmp[0:1, 0:NQ], float(BATCH - 1), None, ALU.add))
                ch.do(V.tensor_copy(g.chunk_early[0:1, :], tmp[0:1, 0:NQ]))
                ch.do(V.tensor_scalar(g.chunk_early[0:1, :], g.chunk_early[0:1, :], BATCH.bit_length() - 1, None, ALU.arith_shift_right))
                V.sem_inc(set_up, 1)
                dv.nop(nofuse=True)
                n = dv.value_load(g.sizes[0:1, 0:1], min_val=0, max_val=TP // 16)
                with dv.Fori(0, n) as i:
                    for u in range(2):
                        c = Chain(dv, chunks, 6 * i + 3 * u)
                        dv.nop(nofuse=True)
                        c.do(V.max(key8[:, :], listed[:, :]))
                        c.do(V.tensor_copy(keys[:, bass.ds(16 * i + 8 * u, 8)], key8[:, :]))
                        dv.nop(nofuse=True)
                        c.do(V.match_replace(listed[:, :], key8[:, :], listed[:, :], 0.0))
                ch.do(V.tensor_scalar(keys[:, :], keys[:, :], -1.0, firstf[:, 0:1], ALU.mult, ALU.add))
                ch.do(V.tensor_scalar(keys[:, :], keys[:, :], float(EP - 1), None, ALU.min))
                ch.do(V.tensor_copy(edge[:, :], keys[:, :]))
                ch.do(V.tensor_scalar(keys[:, :], rank[:, :], counts[:, 0:1], OUT, ALU.is_ge, ALU.mult))
                ch.do(V.scalar_tensor_tensor(out=keys[:, :], in0=rank[:, :], scalar=base[:, 0:1], in1=keys[:, :], op0=ALU.add, op1=ALU.add))
                ch.do(V.tensor_copy(place[:, :], keys[:, :]))
                V.sem_inc(set_up, 1)

            @block.scalar
            def _(ac):
                ac.wait_ge(ops, mark["angle"])
                nc.scalar.activation(sin[:, :], w[:, :], ACT.Sin).then_inc(waves, 1)
                nc.scalar.activation(half[:, :], w[:, :], ACT.Sin, scale=0.5).then_inc(squared, 1)
                ac.wait_ge(squared, 1)
                nc.scalar.activation(half[:, :], half[:, :], ACT.Square).then_inc(waves, 1)
                ac.wait_ge(ops, mark["rec"])
                ac.dma_start(g.records.rearrange("(p t) f -> p (t f)", p=P), rec[:, :, :].rearrange("p t f -> p (t f)")).then_inc(stored, 16)
                ac.wait_ge(stored, 5 * 16)

            @block.tensor
            def _(pe):
                pe.wait_ge(tri_ready, 2)
                pe.wait_ge(ops, mark["counts"])
                nc.tensor.transpose(p_cnt[:, :], counts[:, 0:1], g.ident[:, :]).then_inc(summed, 1)
                nc.tensor.matmul(p_tot[:, :], g.ones[:, :], counts[:, :], start=True, stop=True).then_inc(summed, 1)
                nc.tensor.matmul(p_base[:, :], tri[:, :], counts[:, 0:1], start=True, stop=True).then_inc(summed, 1)

        with nc.Block() as block:
            @block.gpsimd
            def _(gp):
                def fetch(i, s):
                    G = nc.gpsimd
                    G.tensor_copy(ids[:, s, :], edge[:, bass.ds(i * 8, 8)]).then_inc(copied, 1)
                    G.tensor_copy(tos[:, s, :], place[:, bass.ds(i * 8, 8)]).then_inc(copied, 1)
                    gp.wait_ge(copied, 2 * (i + 1))
                    gp.nop(nofuse=True)
                    for k in range(8):
                        gp.indirect_dma_start(got[:, s, k, :], None, g.records, bass.IndirectOffsetOnAxis(ids[:, s, k:k + 1], 0)).then_inc(fetched[s], 16)

                def put(s):
                    for k in range(8):
                        gp.indirect_dma_start(g.steps, bass.IndirectOffsetOnAxis(tos[:, s, k:k + 1], 0), got[:, s, k, :], None,
                                              bounds_check=EP - 1, oob_is_err=False).then_inc(placed[s], 16)
                n = gp.value_load(g.sizes[0:1, 0:1], min_val=0, max_val=TP // 16)
                fetch(0, 0)
                with gp.Fori(0, n) as i:
                    fetch(2 * i + 1, 1)
                    gp.wait_ge(fetched[0], 128 * (i + 1))
                    gp.nop(nofuse=True)
                    put(0)
                    gp.wait_ge(placed[0], 128 * (i + 1))
                    fetch(2 * i + 2, 0)
                    gp.wait_ge(fetched[1], 128 * (i + 1))
                    gp.nop(nofuse=True)
                    put(1)
                    gp.wait_ge(placed[1], 128 * (i + 1))
                gp.wait_ge(fetched[0], 128 * (n + 1))


def early_steps(nc, g):
    with Phase(nc, "early") as ph:
        entry = ph.sb("entry", [1, QC, LISTED])
        at = ph.sb("at", [1, QC, 3], I32)
        fac, now = ph.sb("fac", [P, 4, QC]), ph.sb("now", [P, 4, BATCH])
        t0, t1, t2 = ph.sb("t0", [P, 2]), ph.sb("t1", [P, 2]), ph.sb("t2", [P, 2])
        p_f = [ph.ps(f"p_f{f}", [P, QC]) for f in range(4)]
        loaded, spread, used, ops, ready, init = (ph.sem(n) for n in ("loaded", "spread", "used", "ops", "ready", "init"))
        row = lambda n: g.mt[:, :, bass.ds(n, 1)].rearrange("p b a -> p (b a)")
        last_row = g.mt[:, :, D - 1]
        per = 6 * BATCH + 1
        filling = Filling(nc, g, ph)
        with nc.Block() as block:
            @block.gpsimd
            def _(gp):
                filling.gpsimd(gp)

            @block.scalar
            def _(ac):
                filling.scalar(ac)

            @block.sync
            def _(sp):
                n = sp.value_load(g.sizes[0:1, 4:5], min_val=0, max_val=NQ)
                with sp.Fori(0, n) as q:
                    sp.wait_ge(used, q + 1)
                    sp.dma_start(entry[:, :, :], g.steps[bass.ds(q * QC, QC), :].rearrange("(o e) f -> o e f", o=1)).then_inc(loaded, 16)

            @block.tensor
            def _(pe):
                n = pe.value_load(g.sizes[0:1, 4:5], min_val=0, max_val=NQ)
                with pe.Fori(0, n) as q:
                    pe.wait_ge(loaded, 16 * (q + 1))
                    for f in range(4):
                        nc.tensor.matmul(p_f[f][:, :], g.ones[0:1, :], entry[0:1, :, f], start=True, stop=True).then_inc(spread, 1)

            @block.vector
            def _(dv):
                V = nc.vector
                V.sem_inc(used, 1)
                c0 = Chain(dv, init)
                c0.do(V.memset(g.mt[:, :, :], 0.0))
                for b in range(2):
                    c0.do(V.tensor_copy(g.mt[:, b, b * P:(b + 1) * P], g.ident[:, :]))
                n = dv.value_load(g.sizes[0:1, 4:5], min_val=0, max_val=NQ)
                with dv.Fori(0, n) as q:
                    dv.wait_ge(loaded, 16 * (q + 1))
                    V.tensor_copy(at[:, :, :], entry[:, :, READ:READ + 3]).then_inc(ready, 1)
                    dv.wait_ge(spread, 4 * (q + 1))
                    for f in range(4):
                        V.tensor_copy(fac[:, f, :], p_f[f][:, :]).then_inc(ready, 1)
                    dv.wait_ge(ready, 5 * (q + 1))
                    dv.nop(nofuse=True)
                    m = dv.value_load(g.chunk_early[0:1, bass.ds(q, 1)], min_val=0, max_val=QC // BATCH)
                    with dv.Fori(0, m) as r:
                        rows_of = registers(nc, DVE, at[0:1, bass.ds(r * BATCH, BATCH), :].rearrange("o a f -> o (a f)"), D + 1, waited=False)
                        s = Chain(dv, ops, per * (QC // BATCH) * q + per * r)
                        s.do(V.tensor_copy(now[:, :, :], fac[:, :, bass.ds(r * BATCH, BATCH)]))
                        for u in range(BATCH):
                            i, wi, j = rows_of[3 * u:3 * u + 3]
                            f = lambda k: now[:, k, u:u + 1]
                            s.do(V.tensor_scalar(t0[:, :], last_row, f(BETA), None, ALU.mult))
                            s.do(V.scalar_tensor_tensor(out=row(j), in0=row(j), scalar=f(ALPHA), in1=t0[:, :], op0=ALU.mult, op1=ALU.add))
                            s.do(V.tensor_scalar(t1[:, :], row(j), f(SIN), None, ALU.mult), wait=False)
                            s.do(V.tensor_scalar(t2[:, :], row(i), f(SIN), None, ALU.mult))
                            s.do(V.scalar_tensor_tensor(out=row(wi), in0=row(i), scalar=f(COS), in1=t1[:, :], op0=ALU.mult, op1=ALU.subtract), wait=False)
                            s.do(V.scalar_tensor_tensor(out=row(j), in0=row(j), scalar=f(COS), in1=t2[:, :], op0=ALU.mult, op1=ALU.add))
                    V.sem_inc(used, 1)


def late_steps(nc, g):
    with Phase(nc, "late") as ph:
        entry = ph.sb("entry", [1, QC, LISTED])
        who_i, who = ph.sb("who_i", [P, 2], I32), ph.sb("who", [P, 2])
        cos, sin, is_last, scale, other = (ph.sb(n, [P, QC]) for n in ("cos", "sin", "is_last", "scale", "other"))
        late = ph.sb("late", [P, QC])
        grown = ph.sb("grown", [P, QC + 1])
        mine, factor, term, out_a, out_b = (ph.sb(n, [P, 2, QC]) for n in ("mine", "factor", "term", "out_a", "out_b"))
        state = ph.sb("state", [P, 4])
        wide = ph.sb("wide", [P, 4, P])
        p_f = [ph.ps(f"p_f{f}", [P, QC]) for f in range(3)]
        p_s = ph.ps("p_s", [P, 4, P])
        seq, spread, used, ops, init, ready, turned = (ph.sem(n) for n in ("seq", "spread", "used", "ops", "init", "ready", "turned"))
        final = ph.sem("final")
        loaded = ph.sem("loaded")
        per = 22
        with nc.Block() as block:
            @block.sync
            def _(sp):
                n = sp.value_load(g.sizes[0:1, 3:4], min_val=0, max_val=NQ)
                with sp.Fori(0, n) as q:
                    sp.wait_ge(spread, 3 * q + 3)
                    sp.dma_start(entry[:, :, :], g.steps[bass.ds(q * QC, QC), :].rearrange("(o e) f -> o e f", o=1)).then_inc(loaded, 16)

            @block.gpsimd
            def _(gp):
                nc.gpsimd.iota(who_i[:, :], [[P, 2]], base=0, channel_multiplier=1).then_inc(seq, 1)

            @block.tensor
            def _(pe):
                nc.tensor.sem_inc(spread, 3)
                n = pe.value_load(g.sizes[0:1, 3:4], min_val=0, max_val=NQ)
                with pe.Fori(0, n) as q:
                    pe.wait_ge(loaded, 16 * (q + 1))
                    pe.wait_ge(used, q + 1)
                    for k, f in enumerate((COS, SIN, LATE)):
                        nc.tensor.matmul(p_f[k][:, :], g.ones[0:1, :], entry[0:1, :, f], start=True, stop=True).then_inc(spread, 1)
                pe.wait_ge(ready, 1)
                for k in range(4):
                    nc.tensor.matmul(p_s[:, k, :], wide[:, k, :], g.ident[:, :], start=True, stop=True).then_inc(turned, 1)

            @block.vector
            def _(dv):
                V = nc.vector
                V.sem_inc(used, 1)
                c0 = Chain(dv, init)
                dv.wait_ge(seq, 1)
                c0.do(V.tensor_copy(who[:, :], who_i[:, :]))
                c0.do(V.memset(grown[:, QC:QC + 1], 1.0))
                c0.do(V.memset(state[:, 0:2], 1.0))
                c0.do(V.memset(state[:, 2:4], 0.0))
                n = dv.value_load(g.sizes[0:1, 3:4], min_val=0, max_val=NQ)
                with dv.Fori(0, n) as q:
                    dv.wait_ge(spread, 3 * q + 6)
                    s = Chain(dv, ops, per * q)
                    s.do(V.tensor_copy(cos[:, :], p_f[0][:, :]), wait=False)
                    s.do(V.tensor_copy(late[:, :], p_f[2][:, :]), wait=False)
                    s.do(V.tensor_copy(sin[:, :], p_f[1][:, :]))
                    V.sem_inc(used, 1)
                    s.do(V.tensor_copy(grown[:, 0:1], grown[:, QC:QC + 1]), wait=False)
                    s.do(V.tensor_scalar(is_last[:, :], late[:, :], float(D - 1), None, ALU.is_equal), wait=False)
                    s.do(V.tensor_tensor(scale[:, :], cos[:, :], sin[:, :], ALU.subtract))
                    s.do(V.scalar_tensor_tensor(out=scale[:, :], in0=scale[:, :], scalar=-1.0, in1=is_last[:, :], op0=ALU.add, op1=ALU.mult))
                    s.do(V.tensor_scalar(scale[:, :], scale[:, :], 1.0, None, ALU.add))
                    s.do(V.tensor_tensor_scan(grown[:, 1:QC + 1], scale[:, :], scale[:, :], grown[:, 0:1], ALU.mult, ALU.bypass), wait=False)
                    for h in range(2):
                        s.do(V.tensor_scalar(mine[:, h, :], late[:, :], who[:, h:h + 1], None, ALU.is_equal), wait=h == 1)
                    s.do(V.scalar_tensor_tensor(out=other[:, :], in0=sin[:, :], scalar=-1.0, in1=grown[:, 0:QC], op0=ALU.mult, op1=ALU.mult), wait=False)
                    for h in range(2):
                        s.do(V.scalar_tensor_tensor(out=factor[:, h, :], in0=cos[:, :], scalar=-1.0, in1=mine[:, h, :], op0=ALU.add, op1=ALU.mult), wait=h == 1)
                    s.do(V.tensor_tensor(term[:, :, :], mine[:, :, :], other[:, :].unsqueeze(1).to_broadcast([P, 2, QC]), ALU.mult), wait=False)
                    s.do(V.tensor_scalar(factor[:, :, :], factor[:, :, :], 1.0, None, ALU.add))
                    for h in range(2):
                        s.do(V.tensor_tensor_scan(out_a[:, h, :], factor[:, h, :], factor[:, h, :], state[:, h:h + 1], ALU.mult, ALU.bypass), wait=False)
                        s.do(V.tensor_tensor_scan(out_b[:, h, :], factor[:, h, :], term[:, h, :], state[:, 2 + h:3 + h], ALU.mult, ALU.add), wait=h == 1)
                    s.do(V.tensor_copy(state[:, 0:2], out_a[:, :, QC - 1]), wait=False)
                    s.do(V.tensor_copy(state[:, 2:4], out_b[:, :, QC - 1]))
                    assert s.n == per, s.n
                for k in range(4):
                    c0.do(V.tensor_copy(wide[:, k, :], state[:, k:k + 1].to_broadcast([P, P])))
                V.sem_inc(ready, 1)
                dv.wait_ge(turned, 4)
                by_row = lambda h: p_s[:, 2 * h:2 * h + 2, :].rearrange("p k n -> p (k n)")[:, 0:D - 1]
                f = Chain(dv, final)
                for b in range(2):
                    f.do(V.tensor_scalar(out_a[:, b, 0:D - 1], by_row(1), g.mt[:, b, D - 1:D], None, ALU.mult))
                    f.do(V.tensor_tensor(g.mt[:, b, 0:D - 1], g.mt[:, b, 0:D - 1], by_row(0), ALU.mult))
                    f.do(V.tensor_tensor(g.mt[:, b, 0:D - 1], g.mt[:, b, 0:D - 1], out_a[:, b, 0:D - 1], ALU.add))
                f.do(V.tensor_scalar(g.mt[:, :, D - 1], g.mt[:, :, D - 1], grown[:, QC:QC + 1], None, ALU.mult))


def l0_gnn(nc, g):
    with ExitStack() as own:
        sb = lambda n, s, d=F32: own.enter_context(nc.sbuf_tensor(n, s, d))
        dr = lambda n, s, d=F32: nc.dram_tensor(n, s, d, kind="Internal").ap()
        g.w_dram = g.a["edge_weight"]
        g.sizes, g.chunk_early = sb("sizes", [1, 5], I32), sb("chunk_early", [1, NQ], I32)
        g.mt = sb("mt", [P, 2, D + 2])
        g.records, g.steps = dr("records", [EP, LISTED]), dr("steps", [EP, LISTED])
        rotation_list(nc, g)
        early_steps(nc, g)
        late_steps(nc, g)
        x_plus_product(nc, g, "l0g", g.mt[:, :, 0:D])


def add_agg(nc, g):
    with Phase(nc, "add") as ph:
        added = ph.sem("added")
        with nc.Block() as block:
            @block.vector
            def _(dv):
                nc.vector.tensor_tensor(g.x[:, :, :], g.x[:, :, :], g.agg[:, :, 0:D], ALU.add).then_inc(added, 1)
                dv.wait_ge(added, 1)


def store_x(nc, g):
    with Phase(nc, "out") as ph:
        stored = ph.sem("stored")
        with nc.Block() as block:
            @block.sync
            def _(sp):
                sp.dma_start(g.out[0:(NT - 1) * P, :].rearrange("(t p) d -> p t d", p=P), g.x[:, 0:NT - 1, :]).then_inc(stored, 16)
                sp.dma_start(g.out[(NT - 1) * P:N_NODES, :], g.x[0:LAST, NT - 1, :]).then_inc(stored, 16)
                sp.wait_ge(stored, 32)


def gnn_ffn_stack(nc, a, out):
    g = setup(nc, a, out)
    setup3(nc, g)
    setup4(nc, g)
    constants(nc, g)
    l0_gnn(nc, g)
    l0_ffn(nc, g, a)
    edge_tables(nc, g)
    gat_table(nc, g, "t1", a["L1_gnn_W"], a["L1_gnn_a_left"], a["L1_gnn_a_right"], 8, D, True, g.table, g.inject8, True)
    gather_pass(nc, g, "g1", g.table, D, 8, g.inject8)
    gat_finish(nc, g, "f1", g.table, 8, 1e-16)
    add_agg(nc, g)
    turned_weights(nc, g, a["L1_ffn_weight"], "wt1")
    x_plus_product(nc, g, "l1f", g.wt, a["L1_ffn_bias"])
    ln_rows(nc, g, "lnr", table=g.rows256)
    gather_pass(nc, g, "g2p", g.rows256, D)
    ln_rows(nc, g, "lna")
    turned_weights(nc, g, a["L2_gnn_W"], "wt2")
    agg_product(nc, g, "l2w", g.wt)
    batch_norm(nc, g, "bnl2", D, a["L2_gnn_b"], a["L2_gnn_bn_w"], a["L2_gnn_bn_b"], True)
    top2_ffn(nc, g, *(a["L2_ffn_" + n] for n in ("gate_w", "gate_b", "W1", "b1", "W2", "b2")), True)
    l3_gnn(nc, g, {n: a["L3_gnn_" + n] for n in ("W_gcn", "b_gcn", "g0", "beta0", "W1", "a_src1", "a_dst1", "b1", "g1", "beta1",
                                                 "W2", "a_src2", "a_dst2", "b2", "g2", "beta2")})
    top2_ffn(nc, g, *(a["L3_ffn_" + n] for n in ("Wg", "bg", "W1", "b1", "W2", "b2")), False)
    store_x(nc, g)
    nc.keep.close()


def kernel(**inputs):
    import concourse.bacc as bacc
    from concourse.bass_utils import run_bass_kernel_spmd

    nc = bacc.Bacc("TRN2", target_bir_lowering=False, num_devices=1)
    arrays = {f"in_{name}_dram": np.ascontiguousarray(value) for name, value in inputs.items()}
    args = {name: nc.dram_tensor(f"in_{name}_dram", value.shape, mybir.dt.from_np(value.dtype), kind="ExternalInput").ap()
            for name, value in ((n, arrays[f"in_{n}_dram"]) for n in inputs)}
    out = nc.dram_tensor("out_0_dram", (N_NODES, D), F32, kind="ExternalOutput").ap()
    gnn_ffn_stack(nc, args, out)
    result = run_bass_kernel_spmd(nc, [arrays], core_ids=[0])
    return result.results[0]["out_0_dram"]
```
